# Optimizing a Trainium2 kernel written in Bass

```python
import numpy as np
import jax
import jax.numpy as jnp

def _softmax(x, axis=-1):
    return jax.nn.softmax(x, axis=axis)

def _gelu(x):
    return jax.nn.gelu(x, approximate=True)

def _silu(x):
    return jax.nn.silu(x)

def _sigmoid(x):
    return jax.nn.sigmoid(x)

def _layernorm(x, axis=-1, eps=1e-05):
    m = jnp.mean(x, axis=axis, keepdims=True)
    v = jnp.var(x, axis=axis, keepdims=True)
    return (x - m) / jnp.sqrt(v + eps)

def _scatter_add(tgt, idx, src, axis=0):
    return tgt.at[idx].add(src)

def _segment_sum(src, seg, n):
    return jax.ops.segment_sum(src, seg, n)
kernel_name = 'mk_decoder_postln_d2_seqx_r8_e81c9c'

def setup_inputs(seed: int=0):
    np.random.seed(seed)
    _w = jnp.asarray

    def _rec_inputs():
        import jax
        import jax.numpy as jnp
        _rk = jax.random.key(seed)
        x = -0.0005207 + 1.001 * jax.random.normal(jax.random.fold_in(_rk, 1), (32, 56, 128), jnp.float32)
        _lenS = 56 - jax.random.randint(jax.random.fold_in(_rk, 7), (32,), 0, max(1, 56 // 4) + 1, jnp.int32)
        _lenS2 = 1500 - jax.random.randint(jax.random.fold_in(_rk, 8), (32,), 0, max(1, 1500 // 4) + 1, jnp.int32)
        _ctx_1024P = jax.random.normal(jax.random.fold_in(_rk, 11), (32, 16, 128), jnp.float32)
        _ctx_1024c = jax.random.dirichlet(jax.random.fold_in(_rk, 511), 0.3 * jnp.ones((16,), jnp.float32), (32, 1500))
        _ctx_1024t = jnp.einsum('bsk,bkd->bsd', _ctx_1024c, _ctx_1024P)
        _ctx_1024t = _ctx_1024t * jax.lax.rsqrt(jnp.mean(jnp.square(_ctx_1024t)) + 1e-12) * 0.953939
        ctx_1024 = -1.39393e-06 + 0.999914 * (_ctx_1024t + 0.3 * jax.random.normal(jax.random.fold_in(_rk, 611), (32, 1500, 128), jnp.float32))
        _validS = jnp.arange(56)[None, :] < _lenS[:, None]
        _validS2 = jnp.arange(1500)[None, :] < _lenS2[:, None]
        _causal = jnp.tril(jnp.ones((56, 56), dtype=bool))
        mask_BxS2_bk0 = jnp.logical_not(jnp.broadcast_to(_validS2[:, :], (32, 1500)))
        return (x, ctx_1024, mask_BxS2_bk0)
    x, ctx_1024, mask_BxS2_bk0 = _rec_inputs()

    def _L0_attn_setup():
        import jax, jax.numpy as jnp
        import numpy as np
        D_MODEL = 128
        N_HEADS = 16
        D_LATENT = 32
        HEAD_DIM = D_MODEL // N_HEADS

        def apply_rope(x):
            B, T, H, D = x.shape
            inv_freq = 1.0 / 10000.0 ** (jnp.arange(0, D, 2, dtype=jnp.float32) / D)
            t = jnp.arange(T, dtype=jnp.float32)
            freqs = t[:, None] * inv_freq[None, :]
            sin_f = jnp.sin(freqs)[None, :, None, :]
            cos_f = jnp.cos(freqs)[None, :, None, :]
            x1, x2 = jnp.split(x, 2, axis=-1)
            return jnp.concatenate([x1 * cos_f - x2 * sin_f, x1 * sin_f + x2 * cos_f], axis=-1)
        key = jax.random.key(seed)
        ks = jax.random.split(key, 10)
        B, T = (4, 512)
        s = lambda fan_in: 1.0 / np.sqrt(fan_in)
        return {'x': jax.random.normal(ks[0], (B, T, D_MODEL), dtype=jnp.float32), 'Wq': jax.random.normal(ks[1], (D_MODEL, D_MODEL), dtype=jnp.float32) * s(D_MODEL), 'bq': jnp.zeros((D_MODEL,), jnp.float32), 'Wdown': jax.random.normal(ks[2], (D_MODEL, D_LATENT), dtype=jnp.float32) * s(D_MODEL), 'bdown': jnp.zeros((D_LATENT,), jnp.float32), 'Wup': jax.random.normal(ks[3], (D_LATENT, 2 * D_MODEL), dtype=jnp.float32) * s(D_LATENT), 'bup': jnp.zeros((2 * D_MODEL,), jnp.float32), 'Wout': jax.random.normal(ks[4], (D_MODEL, D_MODEL), dtype=jnp.float32) * s(D_MODEL), 'bout': jnp.zeros((D_MODEL,), jnp.float32)}
    _L0_attn_all = _L0_attn_setup()
    _L0_attn_in = {k: v for k, v in _L0_attn_all.items() if k in ('Wq', 'bq', 'Wdown', 'bdown', 'Wup', 'bup', 'Wout', 'bout')}
    del _L0_attn_all

    def _L0_xattn_setup():
        import jax, jax.numpy as jnp
        import numpy as np
        EMBED_DIM = 128
        NUM_HEADS = 16
        HEAD_DIM = EMBED_DIM // NUM_HEADS
        SCALE = HEAD_DIM ** (-0.5)
        key = jax.random.key(seed)
        ks = jax.random.split(key, 8)
        B, Nq, Nkv, C = (2, 128, 256, EMBED_DIM)
        xavier = (6.0 / (C + C)) ** 0.5

        def w(k):
            return jax.random.uniform(k, (C, C), jnp.float32, -xavier, xavier)
        return {'query': jax.random.normal(ks[0], (B, Nq, C), jnp.float32), 'key': jax.random.normal(ks[1], (B, Nkv, C), jnp.float32), 'value': jax.random.normal(ks[2], (B, Nkv, C), jnp.float32), 'Wq': w(ks[3]), 'bq': jnp.zeros((C,), jnp.float32), 'Wk': w(ks[4]), 'bk': jnp.zeros((C,), jnp.float32), 'Wv': w(ks[5]), 'bv': jnp.zeros((C,), jnp.float32), 'Wo': w(ks[6]), 'bo': jnp.zeros((C,), jnp.float32), 'temperature': jnp.ones((NUM_HEADS, 1, 1), jnp.float32)}
    _L0_xattn_all = _L0_xattn_setup()
    _L0_xattn_in = {k: v for k, v in _L0_xattn_all.items() if k in ('Wq', 'bq', 'Wk', 'bk', 'Wv', 'bv', 'Wo', 'bo', 'temperature')}
    del _L0_xattn_all

    def _L0_ffn_setup():
        import jax, jax.numpy as jnp
        import numpy as np
        H = 128
        E = 64
        K = 8
        G = 8
        TOPK_GROUP = 4
        I_MOE = 64
        I_SHARED = 256
        SCALE = 2.5

        def relu2(x):
            return jnp.square(jax.nn.relu(x))

        def _route(xf, router_w, correction_bias):
            T = xf.shape[0]
            logits = xf @ router_w.T
            scores = jax.nn.sigmoid(logits)
            sfc = scores + correction_bias[None, :]
            grp = sfc.reshape(T, G, E // G)
            top2, _ = jax.lax.top_k(grp, 2)
            group_scores = top2.sum(-1)
            _, gidx = jax.lax.top_k(group_scores, TOPK_GROUP)
            gmask = jnp.zeros((T, G), sfc.dtype).at[jnp.arange(T)[:, None], gidx].set(1.0)
            emask = jnp.repeat(gmask, E // G, axis=1)
            masked = jnp.where(emask > 0, sfc, 0.0)
            _, tidx = jax.lax.top_k(masked, K)
            tw = jnp.take_along_axis(scores, tidx, axis=1)
            tw = tw / (tw.sum(-1, keepdims=True) + 1e-20)
            return (tidx, tw * SCALE)
        key = jax.random.key(seed)
        ks = jax.random.split(key, 7)
        x = jax.random.normal(ks[0], (2, 128, H), dtype=jnp.float32)
        router_w = jax.random.normal(ks[1], (E, H), dtype=jnp.float32) * 0.02
        correction_bias = jax.random.normal(ks[2], (E,), dtype=jnp.float32) * 0.01
        up_w = jax.random.normal(ks[3], (E, H, I_MOE), dtype=jnp.float32) * 0.02
        down_w = jax.random.normal(ks[4], (E, I_MOE, H), dtype=jnp.float32) * 0.02
        shared_up_w = jax.random.normal(ks[5], (H, I_SHARED), dtype=jnp.float32) * 0.02
        shared_down_w = jax.random.normal(ks[6], (I_SHARED, H), dtype=jnp.float32) * 0.02
        return {'x': x, 'router_w': router_w, 'correction_bias': correction_bias, 'up_w': up_w, 'down_w': down_w, 'shared_up_w': shared_up_w, 'shared_down_w': shared_down_w}
    _L0_ffn_all = _L0_ffn_setup()
    _L0_ffn_in = {k: v for k, v in _L0_ffn_all.items() if k in ('router_w', 'correction_bias', 'up_w', 'down_w', 'shared_up_w', 'shared_down_w')}
    del _L0_ffn_all

    def _L1_attn_setup():
        import jax, jax.numpy as jnp
        import numpy as np
        N_HEADS = 16
        EPS = 1e-06
        key = jax.random.key(seed)
        ks = jax.random.split(key, 5)
        B, N, D, H = (4, 256, 128, N_HEADS)
        x = jax.random.normal(ks[0], (B, N, D), dtype=jnp.float32)
        Wq = jax.random.normal(ks[1], (D, D), dtype=jnp.float32) * D ** (-0.5)
        Wk = jax.random.normal(ks[2], (D, D), dtype=jnp.float32) * D ** (-0.5)
        Wv = jax.random.normal(ks[3], (D, D), dtype=jnp.float32) * D ** (-0.5)
        Wo = jax.random.normal(ks[4], (D, D), dtype=jnp.float32) * D ** (-0.5)
        q_scale = jnp.ones((H,), dtype=jnp.float32)
        k_scale = jnp.ones((H,), dtype=jnp.float32)
        return {'x': x, 'Wq': Wq, 'Wk': Wk, 'Wv': Wv, 'Wo': Wo, 'q_scale': q_scale, 'k_scale': k_scale}
    _L1_attn_all = _L1_attn_setup()
    _L1_attn_in = {k: v for k, v in _L1_attn_all.items() if k in ('Wq', 'Wk', 'Wv', 'Wo', 'q_scale', 'k_scale')}
    del _L1_attn_all

    def _L1_xattn_setup():
        import jax, jax.numpy as jnp
        import numpy as np
        B, LQ, LKV, D, H = (2, 256, 512, 128, 16)
        HD = D // H
        key = jax.random.key(seed)
        ks = jax.random.split(key, 12)
        s = 1.0 / np.sqrt(D)
        return {'x_q': jax.random.normal(ks[0], (B, LQ, D), jnp.float32), 'x_kv': jax.random.normal(ks[1], (B, LKV, D), jnp.float32), 'mask_kv': jax.random.randint(ks[2], (B, LKV), 0, 2).astype(bool), 'Wq': jax.random.normal(ks[3], (D, D), jnp.float32) * s, 'bq': jnp.zeros((D,), jnp.float32), 'Wk': jax.random.normal(ks[4], (D, D), jnp.float32) * s, 'bk': jnp.zeros((D,), jnp.float32), 'Wv': jax.random.normal(ks[5], (D, D), jnp.float32) * s, 'bv': jnp.zeros((D,), jnp.float32), 'Wo': jax.random.normal(ks[6], (D, D), jnp.float32) * s, 'bo': jnp.zeros((D,), jnp.float32)}
    _L1_xattn_all = _L1_xattn_setup()
    _L1_xattn_in = {k: v for k, v in _L1_xattn_all.items() if k in ('Wq', 'bq', 'Wk', 'bk', 'Wv', 'bv', 'Wo', 'bo')}
    del _L1_xattn_all

    def _L1_ffn_setup():
        import jax, jax.numpy as jnp
        import numpy as np
        B, S, D, E, K = (2, 256, 128, 8, 2)
        H = 4 * D
        key = jax.random.key(seed)
        ks = jax.random.split(key, 6)
        x = jax.random.normal(ks[0], (B, S, D), dtype=jnp.float32)
        lim_g = np.sqrt(6.0 / (D + E)).astype(np.float32)
        W_gate = jax.random.uniform(ks[1], (D, E), minval=-lim_g, maxval=lim_g, dtype=jnp.float32)
        lim1 = np.sqrt(1.0 / D).astype(np.float32)
        lim2 = np.sqrt(1.0 / H).astype(np.float32)
        W1 = jax.random.uniform(ks[2], (E, D, H), minval=-lim1, maxval=lim1, dtype=jnp.float32)
        b1 = jax.random.uniform(ks[3], (E, H), minval=-lim1, maxval=lim1, dtype=jnp.float32)
        W2 = jax.random.uniform(ks[4], (E, H, D), minval=-lim2, maxval=lim2, dtype=jnp.float32)
        b2 = jax.random.uniform(ks[5], (E, D), minval=-lim2, maxval=lim2, dtype=jnp.float32)
        return {'x': x, 'W_gate': W_gate, 'W1': W1, 'b1': b1, 'W2': W2, 'b2': b2}
    _L1_ffn_all = _L1_ffn_setup()
    _L1_ffn_in = {k: v for k, v in _L1_ffn_all.items() if k in ('W_gate', 'W1', 'b1', 'W2', 'b2')}
    del _L1_ffn_all
    return {'x': x, 'ctx_1024': ctx_1024, 'mask_BxS2_bk0': mask_BxS2_bk0, 'L0_attn_Wq': _L0_attn_in['Wq'], 'L0_attn_bq': _L0_attn_in['bq'], 'L0_attn_Wdown': _L0_attn_in['Wdown'], 'L0_attn_bdown': _L0_attn_in['bdown'], 'L0_attn_Wup': _L0_attn_in['Wup'], 'L0_attn_bup': _L0_attn_in['bup'], 'L0_attn_Wout': _L0_attn_in['Wout'], 'L0_attn_bout': _L0_attn_in['bout'], 'L0_xattn_Wq': _L0_xattn_in['Wq'], 'L0_xattn_bq': _L0_xattn_in['bq'], 'L0_xattn_Wk': _L0_xattn_in['Wk'], 'L0_xattn_bk': _L0_xattn_in['bk'], 'L0_xattn_Wv': _L0_xattn_in['Wv'], 'L0_xattn_bv': _L0_xattn_in['bv'], 'L0_xattn_Wo': _L0_xattn_in['Wo'], 'L0_xattn_bo': _L0_xattn_in['bo'], 'L0_xattn_temperature': _L0_xattn_in['temperature'], 'L0_ffn_router_w': _L0_ffn_in['router_w'], 'L0_ffn_correction_bias': _L0_ffn_in['correction_bias'], 'L0_ffn_up_w': _L0_ffn_in['up_w'], 'L0_ffn_down_w': _L0_ffn_in['down_w'], 'L0_ffn_shared_up_w': _L0_ffn_in['shared_up_w'], 'L0_ffn_shared_down_w': _L0_ffn_in['shared_down_w'], 'L1_attn_Wq': _L1_attn_in['Wq'], 'L1_attn_Wk': _L1_attn_in['Wk'], 'L1_attn_Wv': _L1_attn_in['Wv'], 'L1_attn_Wo': _L1_attn_in['Wo'], 'L1_attn_q_scale': _L1_attn_in['q_scale'], 'L1_attn_k_scale': _L1_attn_in['k_scale'], 'L1_xattn_Wq': _L1_xattn_in['Wq'], 'L1_xattn_bq': _L1_xattn_in['bq'], 'L1_xattn_Wk': _L1_xattn_in['Wk'], 'L1_xattn_bk': _L1_xattn_in['bk'], 'L1_xattn_Wv': _L1_xattn_in['Wv'], 'L1_xattn_bv': _L1_xattn_in['bv'], 'L1_xattn_Wo': _L1_xattn_in['Wo'], 'L1_xattn_bo': _L1_xattn_in['bo'], 'L1_ffn_W_gate': _L1_ffn_in['W_gate'], 'L1_ffn_W1': _L1_ffn_in['W1'], 'L1_ffn_b1': _L1_ffn_in['b1'], 'L1_ffn_W2': _L1_ffn_in['W2'], 'L1_ffn_b2': _L1_ffn_in['b2']}

def reference(x, ctx_1024, mask_BxS2_bk0, L0_attn_Wq, L0_attn_bq, L0_attn_Wdown, L0_attn_bdown, L0_attn_Wup, L0_attn_bup, L0_attn_Wout, L0_attn_bout, L0_xattn_Wq, L0_xattn_bq, L0_xattn_Wk, L0_xattn_bk, L0_xattn_Wv, L0_xattn_bv, L0_xattn_Wo, L0_xattn_bo, L0_xattn_temperature, L0_ffn_router_w, L0_ffn_correction_bias, L0_ffn_up_w, L0_ffn_down_w, L0_ffn_shared_up_w, L0_ffn_shared_down_w, L1_attn_Wq, L1_attn_Wk, L1_attn_Wv, L1_attn_Wo, L1_attn_q_scale, L1_attn_k_scale, L1_xattn_Wq, L1_xattn_bq, L1_xattn_Wk, L1_xattn_bk, L1_xattn_Wv, L1_xattn_bv, L1_xattn_Wo, L1_xattn_bo, L1_ffn_W_gate, L1_ffn_W1, L1_ffn_b1, L1_ffn_W2, L1_ffn_b2):
    import jax
    import jax.numpy as jnp

    def _L0_attn_ref(x, Wq, bq, Wdown, bdown, Wup, bup, Wout, bout):
        import jax, jax.numpy as jnp
        import numpy as np
        D_MODEL = 128
        N_HEADS = 16
        D_LATENT = 32
        HEAD_DIM = D_MODEL // N_HEADS

        def apply_rope(x):
            B, T, H, D = x.shape
            inv_freq = 1.0 / 10000.0 ** (jnp.arange(0, D, 2, dtype=jnp.float32) / D)
            t = jnp.arange(T, dtype=jnp.float32)
            freqs = t[:, None] * inv_freq[None, :]
            sin_f = jnp.sin(freqs)[None, :, None, :]
            cos_f = jnp.cos(freqs)[None, :, None, :]
            x1, x2 = jnp.split(x, 2, axis=-1)
            return jnp.concatenate([x1 * cos_f - x2 * sin_f, x1 * sin_f + x2 * cos_f], axis=-1)
        B, T, D = x.shape
        H, Dh = (N_HEADS, HEAD_DIM)
        q = x @ Wq + bq
        kv_latent = x @ Wdown + bdown
        kv = kv_latent @ Wup + bup
        q = q.reshape(B, T, H, Dh)
        kv = kv.reshape(B, T, H, 2 * Dh)
        k, v = jnp.split(kv, 2, axis=-1)
        q = apply_rope(q)
        k = apply_rope(k)
        att = jnp.einsum('bthd,btgd->bthg', q, k) / jnp.sqrt(jnp.float32(Dh))
        att = jax.nn.softmax(att, axis=-1)
        out = jnp.einsum('bthg,btgd->bthd', att, v)
        out = out.reshape(B, T, D)
        return out @ Wout + bout

    def _L0_xattn_ref(query, key, value, Wq, bq, Wk, bk, Wv, bv, Wo, bo, temperature):
        import jax, jax.numpy as jnp
        import numpy as np
        EMBED_DIM = 128
        NUM_HEADS = 16
        HEAD_DIM = EMBED_DIM // NUM_HEADS
        SCALE = HEAD_DIM ** (-0.5)
        B, Nq, C = query.shape
        Nkv = key.shape[1]
        H, D = (NUM_HEADS, HEAD_DIM)
        Q = (query @ Wq.T + bq).reshape(B, Nq, H, D).transpose(0, 2, 1, 3)
        K = (key @ Wk.T + bk).reshape(B, Nkv, H, D).transpose(0, 2, 1, 3)
        V = (value @ Wv.T + bv).reshape(B, Nkv, H, D).transpose(0, 2, 1, 3)
        scores = jnp.einsum('bhqd,bhkd->bhqk', Q, K) * SCALE
        scores = scores / temperature
        attn = jax.nn.softmax(scores, axis=-1)
        out = jnp.einsum('bhqk,bhkd->bhqd', attn, V)
        out = out.transpose(0, 2, 1, 3).reshape(B, Nq, C)
        return out @ Wo.T + bo

    def _L0_ffn_ref(x, router_w, correction_bias, up_w, down_w, shared_up_w, shared_down_w):
        import jax, jax.numpy as jnp
        import numpy as np
        H = 128
        E = 64
        K = 8
        G = 8
        TOPK_GROUP = 4
        I_MOE = 64
        I_SHARED = 256
        SCALE = 2.5

        def relu2(x):
            return jnp.square(jax.nn.relu(x))

        def _route(xf, router_w, correction_bias):
            T = xf.shape[0]
            logits = xf @ router_w.T
            scores = jax.nn.sigmoid(logits)
            sfc = scores + correction_bias[None, :]
            grp = sfc.reshape(T, G, E // G)
            top2, _ = jax.lax.top_k(grp, 2)
            group_scores = top2.sum(-1)
            _, gidx = jax.lax.top_k(group_scores, TOPK_GROUP)
            gmask = jnp.zeros((T, G), sfc.dtype).at[jnp.arange(T)[:, None], gidx].set(1.0)
            emask = jnp.repeat(gmask, E // G, axis=1)
            masked = jnp.where(emask > 0, sfc, 0.0)
            _, tidx = jax.lax.top_k(masked, K)
            tw = jnp.take_along_axis(scores, tidx, axis=1)
            tw = tw / (tw.sum(-1, keepdims=True) + 1e-20)
            return (tidx, tw * SCALE)
        B, S, Hd = x.shape
        xf = x.reshape(-1, Hd)
        T = xf.shape[0]
        tidx, tw = _route(xf.astype(jnp.float32), router_w, correction_bias)
        combine = jnp.zeros((T, E), xf.dtype).at[jnp.arange(T)[:, None], tidx].add(tw.astype(xf.dtype))

        def body(acc, ew):
            wu, wd, c = ew
            return (acc + c[:, None] * (relu2(xf @ wu) @ wd), None)
        routed, _ = jax.lax.scan(body, jnp.zeros_like(xf), (up_w, down_w, combine.T))
        shared = relu2(xf @ shared_up_w) @ shared_down_w
        return (routed + shared).reshape(B, S, Hd)

    def _L1_attn_ref(x, Wq, Wk, Wv, Wo, q_scale, k_scale):
        import jax, jax.numpy as jnp
        import numpy as np
        N_HEADS = 16
        EPS = 1e-06
        B, N, D = x.shape
        H = N_HEADS
        hd = D // H
        q = jax.nn.silu(x @ Wq.T)
        k = jax.nn.silu(x @ Wk.T)
        v = jax.nn.silu(x @ Wv.T)
        q = q.reshape(B, N, H, hd).transpose(0, 2, 1, 3)
        k = k.reshape(B, N, H, hd).transpose(0, 2, 1, 3)
        v = v.reshape(B, N, H, hd).transpose(0, 2, 1, 3)
        r_q = jnp.linalg.norm(q, axis=-1, keepdims=True)
        r_k = jnp.linalg.norm(k, axis=-1, keepdims=True)
        q_dir = q / (r_q + EPS)
        k_dir = k / (r_k + EPS)
        scores = jnp.einsum('bhnd,bhmd->bhnm', q_dir, k_dir)
        sq = q_scale[None, :, None, None]
        sk = k_scale[None, :, None, None]
        scores = scores * (r_q * sq) * (jnp.swapaxes(r_k, -2, -1) * sk)
        mask = jnp.tril(jnp.ones((N, N), dtype=bool))
        scores = jnp.where(mask, scores, -jnp.inf)
        probs = jax.nn.softmax(scores, axis=-1)
        out = jnp.einsum('bhnm,bhmd->bhnd', probs, v)
        out = out.transpose(0, 2, 1, 3).reshape(B, N, D)
        return out @ Wo.T

    def _L1_xattn_ref(x_q, x_kv, mask_kv, Wq, bq, Wk, bk, Wv, bv, Wo, bo):
        import jax, jax.numpy as jnp
        import numpy as np
        B, LQ, LKV, D, H = (2, 256, 512, 128, 16)
        HD = D // H
        Bq, Lq, _ = x_q.shape
        Lkv = x_kv.shape[1]
        q = (x_q @ Wq + bq).reshape(Bq, Lq, H, HD).transpose(0, 2, 1, 3)
        k = (x_kv @ Wk + bk).reshape(Bq, Lkv, H, HD).transpose(0, 2, 1, 3)
        v = (x_kv @ Wv + bv).reshape(Bq, Lkv, H, HD).transpose(0, 2, 1, 3)
        logits = jnp.einsum('bhqd,bhkd->bhqk', q, k) / np.sqrt(HD)
        logits = jnp.where(mask_kv[:, None, None, :], logits, -jnp.inf)
        weights = jax.nn.softmax(logits, axis=-1)
        attn = jnp.einsum('bhqk,bhkd->bhqd', weights, v)
        attn = attn.transpose(0, 2, 1, 3).reshape(Bq, Lq, D)
        return attn @ Wo + bo

    def _L1_ffn_ref(x, W_gate, W1, b1, W2, b2):
        import jax, jax.numpy as jnp
        import numpy as np
        B, S, D, E, K = (2, 256, 128, 8, 2)
        H = 4 * D
        gate = jnp.einsum('bsd,de->bse', x, W_gate)
        kth = jax.lax.top_k(gate, K)[0][..., -1:]
        mask = jax.nn.softmax(jnp.where(gate >= kth, gate, -jnp.inf), axis=-1)
        h = jax.nn.relu(jnp.einsum('bsd,edh->bseh', x, W1) + b1)
        y = jnp.einsum('bseh,ehd->bsed', h, W2) + b2
        return (y * mask[..., None]).mean(axis=-2)
    x = _layernorm(x + _L0_attn_ref(x, L0_attn_Wq, L0_attn_bq, L0_attn_Wdown, L0_attn_bdown, L0_attn_Wup, L0_attn_bup, L0_attn_Wout, L0_attn_bout), axis=-1)
    x = _layernorm(x + _L0_xattn_ref(x, ctx_1024, ctx_1024, L0_xattn_Wq, L0_xattn_bq, L0_xattn_Wk, L0_xattn_bk, L0_xattn_Wv, L0_xattn_bv, L0_xattn_Wo, L0_xattn_bo, L0_xattn_temperature), axis=-1)
    x = _layernorm(x + _L0_ffn_ref(x, L0_ffn_router_w, L0_ffn_correction_bias, L0_ffn_up_w, L0_ffn_down_w, L0_ffn_shared_up_w, L0_ffn_shared_down_w), axis=-1)
    x = _layernorm(x + _L1_attn_ref(x, L1_attn_Wq, L1_attn_Wk, L1_attn_Wv, L1_attn_Wo, L1_attn_q_scale, L1_attn_k_scale), axis=-1)
    x = _layernorm(x + _L1_xattn_ref(x, ctx_1024, mask_BxS2_bk0, L1_xattn_Wq, L1_xattn_bq, L1_xattn_Wk, L1_xattn_bk, L1_xattn_Wv, L1_xattn_bv, L1_xattn_Wo, L1_xattn_bo), axis=-1)
    x = _layernorm(x + _L1_ffn_ref(x, L1_ffn_W_gate, L1_ffn_W1, L1_ffn_b1, L1_ffn_W2, L1_ffn_b2), axis=-1)
    return x

_drawn_inputs = setup_inputs


def setup_inputs(seed=0):
    import zlib

    import numpy as np

    out = dict(_drawn_inputs(seed))
    spreads = {'L0_attn_bq': (0.0, 0.362),
     'L0_attn_bdown': (0.0, 0.1),
     'L0_attn_bup': (0.0, 0.1),
     'L0_attn_bout': (0.0, 0.1),
     'L0_xattn_bq': (0.0, 0.376),
     'L0_xattn_bk': (0.0, 2.0),
     'L0_xattn_bv': (0.0, 0.1),
     'L0_xattn_bo': (0.0, 0.1),
     'L0_xattn_temperature': (1.0, 0.2),
     'L1_attn_q_scale': (1.0, 0.2),
     'L1_attn_k_scale': (1.0, 0.6),
     'L1_xattn_bq': (0.0, 0.385),
     'L1_xattn_bk': (0.0, 2.0),
     'L1_xattn_bv': (0.0, 0.1),
     'L1_xattn_bo': (0.0, 0.1)}
    factors = {'L0_ffn_router_w': 7.713,
     'L0_ffn_correction_bias': 8.0,
     'L0_ffn_up_w': 7.8,
     'L0_ffn_down_w': 7.136,
     'L0_ffn_shared_up_w': 3.476,
     'L0_ffn_shared_down_w': 3.133,
     'L1_ffn_W_gate': 2.747,
     'L1_ffn_W1': 3.046,
     'L1_ffn_b1': 25.872,
     'L1_ffn_b2': 8.0}
    for name, (base, spread) in spreads.items():
        noise = np.random.default_rng([zlib.crc32(name.encode()), seed]).standard_normal(out[name].shape)
        drawn = base * np.exp(spread * noise) if base else spread * noise
        out[name] = jnp.asarray(drawn.astype(out[name].dtype))
    for name, factor in factors.items():
        out[name] = (out[name] * factor).astype(out[name].dtype)
    return out
```

```python
from contextlib import ExitStack

import numpy as np

import concourse.bass as bass
from concourse import mybir

F32 = mybir.dt.float32
BF16 = mybir.dt.bfloat16
U8 = mybir.dt.uint8
ACT = mybir.ActivationFunctionType
ALU = mybir.AluOpType
AX = mybir.AxisListType.X

SEQS, SEQ, D = 32, 56, 128
HEADS, HD = 16, 8
KEYS = 1500
TOKENS = SEQS * SEQ
TILE = 2 * SEQ
TILES = 4
GROUP = TILE * TILES
GROUPS = TOKENS // GROUP
GSEQS = GROUP // SEQ
PAIRS = HEADS // 2
PR = 2 * HD
CH = 125
CHUNKS = KEYS // CH
KB = 500
KBANKS = KEYS // KB
CB = CHUNKS // KBANKS
PROD = 6
SROWS = PR * PROD
SHIFT_ROW, MASK_ROW = SROWS, SROWS + 1
STACK = SROWS + 2
E0, I0, K0, G0 = 64, 64, 8, 8
SHARED = 256
NCH0 = (E0 * I0 + SHARED) // 128
E1, I1 = 8, 512
NCH1 = E1 * I1 // 128
EPS = 1e-5
PICKED = 1e30
ABSENT = -3e38


class Steps:

    def __init__(self, sem, names):
        self.sem, self.names, self.k = sem, names.split(), 0
        assert len(set(self.names)) == len(self.names)
        self.per = len(self.names)

    def at(self, t, name):
        return t * self.per + (self.names.index(name) + 1)

    def one(self, name):
        assert self.names[self.k % self.per] == name, (self.names[self.k % self.per], name)
        self.k += 1
        return 1

    def turns(self, t):
        return t * self.per


def bc(ap, n, axis):
    shape = list(ap.shape)
    shape.insert(axis, n)
    return ap.unsqueeze(axis).broadcast_to(shape)


class Stage:

    def __init__(self, nc, name):
        self.nc, self.name, self.ctx = nc, name, ExitStack()

    def sb(self, name, shape, dt=F32):
        return self.ctx.enter_context(self.nc.sbuf_tensor(f"{self.name}_{name}", shape, dt))

    def sem(self, name):
        return self.ctx.enter_context(self.nc.semaphore(f"{self.name}_{name}"))

    def __enter__(self):
        return self

    def __exit__(self, *a):
        self.ctx.close()


def hold(e, sem, value):
    e.wait_ge(sem, value)
    e.nop(nofuse=True)


def tok_major(dram, t):
    return dram[bass.ds(t * GROUP, GROUP), :].rearrange("(s p) d -> p s d", p=TILE)


NORM_VEC = "stats0 stats1 stats2 stats3 aggr0 aggr1 aggr2 aggr3 vareps normed0 normed1 normed2 normed3"


def norm_vector(v, V, P, t, r, stats, mv, ve, rstd, out, before):
    v.wait_ge(V.sem, V.at(t, before))
    for s in range(TILES):
        v.bn_stats(stats[:, s, :], r[:, s, :]).then_inc(V.sem, V.one(f"stats{s}"))
    hold(v, V.sem, V.at(t, "stats3"))
    for s in range(TILES):
        v.bn_aggr(mv[:, s, :], stats[:, s, :]).then_inc(V.sem, V.one(f"aggr{s}"))
    v.wait_ge(V.sem, V.at(t, "aggr3"))
    v.tensor_scalar(ve[:, :], mv[:, :, 1], EPS, None, ALU.add).then_inc(V.sem, V.one("vareps"))
    v.wait_ge(P.sem, P.at(t, "rstd"))
    for s in range(TILES):
        v.tensor_scalar(out[:, s, :], r[:, s, :], mv[:, s, 0:1], rstd[:, s:s + 1], ALU.subtract,
                        ALU.mult).then_inc(V.sem, V.one(f"normed{s}"))


QPREP_POOL = "q_h q_rest q_m q_l x_h x_m x_l x_h2"


def qprep_pool(p, P, S, t, qT, qh, qr, qm, ql, qx, parity):
    hold(p, S.sem, S.at(t, "qT"))
    p.tensor_copy(qh[:, :], qT[:, :]).then_inc(P.sem, P.one("q_h"))
    hold(p, P.sem, P.at(t, "q_h"))
    p.tensor_tensor(qr[:, :], qT[:, :], qh[:, :], ALU.subtract).then_inc(P.sem, P.one("q_rest"))
    hold(p, P.sem, P.at(t, "q_rest"))
    p.tensor_copy(qm[:, :], qr[:, :]).then_inc(P.sem, P.one("q_m"))
    hold(p, P.sem, P.at(t, "q_m"))
    p.tensor_tensor(ql[:, :], qr[:, :], qm[:, :], ALU.subtract).then_inc(P.sem, P.one("q_l"))
    hold(p, P.sem, P.at(t, "q_l"))
    for part, c, n, name in ((qh, 0, 2, "x_h"), (qm, 2, 2, "x_m"), (ql, 4, 1, "x_l"), (qh, 5, 1, "x_h2")):
        for k in range(n):
            last = p.tensor_tensor(qx[:, :, c + k, :, :].rearrange("p b h q -> p h b q"),
                                   bc(part[:, :].rearrange("p (b q) -> p b q", q=SEQ), 2, 1),
                                   bc(bc(parity[:, :], GSEQS, 2), SEQ, 3), ALU.mult)
        last.then_inc(P.sem, P.one(name))


def store_queries(e, stored, t, qx_dram, qx):
    for b in range(GSEQS):
        for a in range(2):
            e.dma_start(qx_dram[t * GSEQS + b].rearrange("j (a r c) n -> a j r (c n)", a=2, r=PR)[a],
                        qx[:, b, 3 * a:3 * a + 3, :, :].rearrange("p c h q -> p (c h q)")).then_inc(stored, 16)


def load_all(e, sem, pairs):
    for dst, src in pairs:
        e.dma_start(dst, src).then_inc(sem, 16)
    return 16 * len(pairs)


def rows_of(vec, n=TILE):
    return vec.rearrange("(a d) -> a d", a=1).broadcast_to([n, vec.shape[0]])


def column(vec):
    return vec.rearrange("(d a) -> d a", a=1)


def self_attention_0(nc, bank, I, x1, qx_dram, consts):
    with Stage(nc, "sa0") as g:
        X, XT = g.sb("X", [TILE, TILES, D]), g.sb("XT", [D, GROUP])
        wq, wdn, wup, wout = g.sb("wq", [D, D]), g.sb("wdn", [D, 32]), g.sb("wup", [32, 2 * D]), g.sb("wout", [D, D])
        bq, bup, bout = g.sb("bq", [TILE, D]), g.sb("bup", [TILE, 2 * D]), g.sb("bout", [TILE, D])
        bdn, wq1 = g.sb("bdn", [32, 1]), g.sb("wq1", [D, D])
        cos, sin = g.sb("cos", [TILE, 4]), g.sb("sin", [TILE, 4])
        qb1, temp, qs, qbs = g.sb("qb1", [D, 1]), g.sb("temp", [D, 1]), g.sb("qs", [D, 1]), g.sb("qbs", [D, 1])
        parity, ident = consts["parity"], consts["ident"]
        lat, q, kv = g.sb("lat", [32, GROUP]), g.sb("q", [TILE, TILES, D]), g.sb("kv", [TILE, TILES, 2 * D])
        qr, kr = g.sb("qr", [TILE, TILES, D]), g.sb("kr", [TILE, TILES, D])
        ta, tb = g.sb("ta", [TILE, 64, 4]), g.sb("tb", [TILE, 64, 4])
        prod = g.sb("prod", [TILE, TILES, 2048])
        S = g.sb("S", [TILE, TILES, 256])
        mx, den = g.sb("mx", [TILE, 64]), g.sb("den", [TILE, 64])
        o, oT, r, xn = g.sb("o", [TILE, TILES, D]), g.sb("oT", [D, GROUP]), g.sb("r", [TILE, TILES, D]), g.sb("xn", [TILE, TILES, D])
        stats, mv, ve, rstd = g.sb("stats", [TILE, 4, 6]), g.sb("mv", [TILE, 4, 2]), g.sb("ve", [TILE, 4]), g.sb("rstd", [TILE, 4])
        xT1, qT = g.sb("xT1", [D, GROUP]), g.sb("qT", [D, GROUP])
        qh, qm, ql, qrest = g.sb("qh", [D, GROUP], BF16), g.sb("qm", [D, GROUP], BF16), g.sb("ql", [D, GROUP], BF16), g.sb("qrest", [D, GROUP])
        qx = g.sb("qx", [D, GSEQS, PROD, 2, SEQ], BF16)
        half = consts["minus_half"]
        weights, loaded, stored = g.sem("weights_loaded"), g.sem("group_loaded"), g.sem("group_stored")
        consts_ready = g.sem("query_scale_ready")
        T = Steps(g.sem("tensor_steps"), "q_ps lat_ps kv_ps oT_ps y_ps xT_ps qT_ps")
        A = Steps(g.sem("scalar_steps"), "lat exp oT xT qT")
        V = Steps(g.sem("vector_steps"), "q kv_a kv_b q1c q2s q1 q2c q1s q2 k1c k2s k1 k2c k1s k2 prod0 prod1 "
                  "S0 S1 S2 S3 max shifted sum inv P vprod0 vprod1 o0 o1 o2 o3 y_bias y_res " + NORM_VEC)
        P = Steps(g.sem("gpsimd_steps"), "prod2 prod3 vprod2 vprod3 rstd " + QPREP_POOL)
        nw = [0]
        with nc.Block() as block:
            @block.sync
            def _(e):
                nw[0] = load_all(e, weights, [
                    (wq[:, :], I["L0_attn_Wq"]), (wdn[:, :], I["L0_attn_Wdown"]), (wup[:, :], I["L0_attn_Wup"]),
                    (wout[:, :], I["L0_attn_Wout"]), (bq[:, :], rows_of(I["L0_attn_bq"])),
                    (bup[:, :], rows_of(I["L0_attn_bup"])), (bout[:, :], rows_of(I["L0_attn_bout"])),
                    (bdn[:, :], column(I["L0_attn_bdown"])), (wq1[:, :], I["L0_xattn_WqT"]),
                    (cos[:, :], I["rope_cos"]), (sin[:, :], I["rope_sin"]), (qb1[:, :], column(I["L0_xattn_bq"])),
                    (temp[:, :], column(I["temperature_rows"]))])
                with e.Fori(0, GROUPS) as t:
                    e.dma_start(X[:, :, :], tok_major(I["x"], t)).then_inc(loaded, 16)
                    e.dma_start(XT[:, :], I["xT"][:, bass.ds(t * GROUP, GROUP)]).then_inc(loaded, 16)
                    hold(e, V.sem, V.at(t, "normed3"))
                    e.dma_start(tok_major(x1, t), xn[:, :, :]).then_inc(stored, 16)
                    hold(e, P.sem, P.at(t, "x_h2"))
                    store_queries(e, stored, t, qx_dram, qx)
                    hold(e, stored, (t + 1) * 16 * (1 + 2 * GSEQS))
                    for X_ in (T, A, V, P):
                        hold(e, X_.sem, X_.turns(t + 1))

            @block.tensor
            def _(e):
                e.wait_ge(weights, nw[0])
                with e.Fori(0, GROUPS) as t:
                    e.wait_ge(loaded, (t + 1) * 32)
                    for s in range(TILES):
                        m = e.matmul(bank[0][0:TILE, s * D:(s + 1) * D], XT[:, s * TILE:(s + 1) * TILE], wq[:, :], start=True, stop=True)
                    m.then_inc(T.sem, T.one("q_ps"))
                    e.matmul(bank[1][0:32, 0:GROUP], wdn[:, :], XT[:, :], start=True, stop=True).then_inc(T.sem, T.one("lat_ps"))
                    e.wait_ge(A.sem, A.at(t, "lat"))
                    for s in range(TILES):
                        m = e.matmul(bank[2 + s // 2][0:TILE, s % 2 * 256:s % 2 * 256 + 256], lat[:, s * TILE:(s + 1) * TILE], wup[:, :], start=True, stop=True)
                    m.then_inc(T.sem, T.one("kv_ps"))
                    e.wait_ge(V.sem, V.at(t, "o3"))
                    for s in range(TILES):
                        m = e.transpose(bank[4][:, s * TILE:(s + 1) * TILE], o[:, s, :], ident[0:TILE, 0:TILE])
                    m.then_inc(T.sem, T.one("oT_ps"))
                    e.wait_ge(A.sem, A.at(t, "oT"))
                    for s in range(TILES):
                        m = e.matmul(bank[5][0:TILE, s * D:(s + 1) * D], oT[:, s * TILE:(s + 1) * TILE], wout[:, :], start=True, stop=True)
                    m.then_inc(T.sem, T.one("y_ps"))
                    e.wait_ge(V.sem, V.at(t, "normed3"))
                    for s in range(TILES):
                        m = e.transpose(bank[6][:, s * TILE:(s + 1) * TILE], xn[:, s, :], ident[0:TILE, 0:TILE])
                    m.then_inc(T.sem, T.one("xT_ps"))
                    e.wait_ge(A.sem, A.at(t, "xT"))
                    e.matmul(bank[7][:, 0:GROUP], wq1[:, :], xT1[:, :], start=True, stop=True).then_inc(T.sem, T.one("qT_ps"))

            @block.scalar
            def _(e):
                e.wait_ge(weights, nw[0])
                e.wait_ge(consts_ready, 3)
                with e.Fori(0, GROUPS) as t:
                    e.wait_ge(loaded, (t + 1) * 32)
                    e.wait_ge(T.sem, T.at(t, "lat_ps"))
                    e.activation(lat[:, :], bank[1][0:32, 0:GROUP], ACT.Identity, bias=bdn[:, :]).then_inc(A.sem, A.one("lat"))
                    e.wait_ge(V.sem, V.at(t, "shifted"))
                    e.activation(S[:, :, :], S[:, :, :], ACT.Exp, scale=HD ** -0.5).then_inc(A.sem, A.one("exp"))
                    e.wait_ge(T.sem, T.at(t, "oT_ps"))
                    e.copy(oT[:, :], bank[4][:, 0:GROUP]).then_inc(A.sem, A.one("oT"))
                    e.wait_ge(T.sem, T.at(t, "xT_ps"))
                    e.copy(xT1[:, :], bank[6][:, 0:GROUP]).then_inc(A.sem, A.one("xT"))
                    e.wait_ge(T.sem, T.at(t, "qT_ps"))
                    e.activation(qT[:, :], bank[7][:, 0:GROUP], ACT.Identity, bias=qbs[:, :], scale=qs[:, :]).then_inc(A.sem, A.one("qT"))

            def head_view(x, s):
                return x[:, s, :].rearrange("p (h d) -> p h d", d=HD)

            def score_product(e, s):
                return e.tensor_tensor(prod[:, s, :].rearrange("p (h g d) -> p h g d", h=HEADS, g=HEADS),
                                       bc(head_view(qr, s), HEADS, 2), bc(head_view(kr, s), HEADS, 1), ALU.mult)

            def value_product(e, s):
                v = kv[:, s, :].rearrange("p (g d) -> p d g", d=2 * HD)[:, HD:2 * HD, :]
                return e.tensor_tensor(prod[:, s, :].rearrange("p (h d g) -> p h d g", h=HEADS, d=HD),
                                       bc(S[:, s, :].rearrange("p (h g) -> p h g", g=HEADS), HD, 2), bc(v, HEADS, 1), ALU.mult)

            @block.vector
            def _(e):
                e.wait_ge(weights, nw[0])
                e.reciprocal(temp[:, :], temp[:, :]).then_inc(consts_ready, 1)
                e.wait_ge(consts_ready, 1)
                e.tensor_scalar(qs[:, :], temp[:, :], HD ** -0.5, None, ALU.mult).then_inc(consts_ready, 1)
                e.wait_ge(consts_ready, 2)
                e.tensor_tensor(qbs[:, :], qb1[:, :], qs[:, :], ALU.mult).then_inc(consts_ready, 1)
                with e.Fori(0, GROUPS) as t:
                    e.wait_ge(loaded, (t + 1) * 32)
                    e.wait_ge(T.sem, T.at(t, "q_ps"))
                    ps4 = lambda b: bank[b][0:TILE, :].rearrange("p (s d) -> p s d", s=TILES)
                    e.tensor_tensor(q[:, :, :], ps4(0), bc(bq[:, :], TILES, 1), ALU.add).then_inc(V.sem, V.one("q"))
                    e.wait_ge(T.sem, T.at(t, "kv_ps"))
                    for i, n in enumerate(("kv_a", "kv_b")):
                        e.tensor_tensor(kv[:, 2 * i:2 * i + 2, :], bank[2 + i][0:TILE, :].rearrange("p (s d) -> p s d", s=2),
                                        bc(bup[:, :], 2, 1), ALU.add).then_inc(V.sem, V.one(n))
                    qv = q[:, :, :].rearrange("p s (h d) -> p (s h) d", d=HD)
                    kk = kv[:, :, :].rearrange("p s (h d) -> p (s h) d", d=2 * HD)
                    for x, y, n, before in ((qv, qr, "q", "q"), (kk, kr, "k", "kv_b")):
                        yv = y[:, :, :].rearrange("p s (h d) -> p (s h) d", d=HD)
                        c, s_ = bc(cos[:, :], 64, 1), bc(sin[:, :], 64, 1)
                        e.wait_ge(V.sem, V.at(t, before))
                        for a, b, half_, op in ((c, s_, 0, ALU.subtract), (s_, c, 1, ALU.add)):
                            na, nb = (f"{n}1c", f"{n}2s") if half_ == 0 else (f"{n}2c", f"{n}1s")
                            first, second = (x[:, :, 0:4], x[:, :, 4:8]) if half_ == 0 else (x[:, :, 4:8], x[:, :, 0:4])
                            if half_ or n == "k":
                                e.wait_ge(V.sem, V.at(t, f"{n}1" if half_ else "q2"))
                            e.tensor_tensor(ta[:, :, :], first, c, ALU.mult).then_inc(V.sem, V.one(na))
                            e.tensor_tensor(tb[:, :, :], second, s_, ALU.mult).then_inc(V.sem, V.one(nb))
                            e.wait_ge(V.sem, V.at(t, nb))
                            e.tensor_tensor(yv[:, :, 4 * half_:4 * half_ + 4], ta[:, :, :], tb[:, :, :], op).then_inc(V.sem, V.one(f"{n}{half_ + 1}"))
                    e.wait_ge(V.sem, V.at(t, "k2"))
                    for s in range(2):
                        score_product(e, s).then_inc(V.sem, V.one(f"prod{s}"))
                    for s in range(TILES):
                        if s < 2:
                            e.wait_ge(V.sem, V.at(t, f"prod{s}"))
                        else:
                            e.wait_ge(P.sem, P.at(t, f"prod{s}"))
                        e.tensor_reduce(S[:, s, :], prod[:, s, :].rearrange("p (a d) -> p a d", d=HD), AX, ALU.add).then_inc(V.sem, V.one(f"S{s}"))
                    e.wait_ge(V.sem, V.at(t, "S3"))
                    Sv = S[:, :, :].rearrange("p s (h g) -> p (s h) g", g=HEADS)
                    e.tensor_reduce(mx[:, :], Sv, AX, ALU.max).then_inc(V.sem, V.one("max"))
                    e.wait_ge(V.sem, V.at(t, "max"))
                    e.tensor_tensor(Sv, Sv, bc(mx[:, :], HEADS, 2), ALU.subtract).then_inc(V.sem, V.one("shifted"))
                    e.wait_ge(A.sem, A.at(t, "exp"))
                    e.tensor_reduce(den[:, :], Sv, AX, ALU.add).then_inc(V.sem, V.one("sum"))
                    e.wait_ge(V.sem, V.at(t, "sum"))
                    e.reciprocal(den[:, :], den[:, :]).then_inc(V.sem, V.one("inv"))
                    e.wait_ge(V.sem, V.at(t, "inv"))
                    e.tensor_tensor(Sv, Sv, bc(den[:, :], HEADS, 2), ALU.mult).then_inc(V.sem, V.one("P"))
                    e.wait_ge(V.sem, V.at(t, "P"))
                    for s in range(2):
                        value_product(e, s).then_inc(V.sem, V.one(f"vprod{s}"))
                    for s in range(TILES):
                        if s < 2:
                            e.wait_ge(V.sem, V.at(t, f"vprod{s}"))
                        else:
                            e.wait_ge(P.sem, P.at(t, f"vprod{s}"))
                        e.tensor_reduce(o[:, s, :], prod[:, s, :].rearrange("p (a g) -> p a g", g=HEADS), AX, ALU.add).then_inc(V.sem, V.one(f"o{s}"))
                    e.wait_ge(T.sem, T.at(t, "y_ps"))
                    e.tensor_tensor(r[:, :, :], ps4(5), bc(bout[:, :], TILES, 1), ALU.add).then_inc(V.sem, V.one("y_bias"))
                    e.wait_ge(V.sem, V.at(t, "y_bias"))
                    e.tensor_tensor(r[:, :, :], r[:, :, :], X[:, :, :], ALU.add).then_inc(V.sem, V.one("y_res"))
                    norm_vector(e, V, P, t, r, stats, mv, ve, rstd, xn, "y_res")

            @block.gpsimd
            def _(e):
                with e.Fori(0, GROUPS) as t:
                    e.wait_ge(V.sem, V.at(t, "k2"))
                    for s in (2, 3):
                        score_product(e, s).then_inc(P.sem, P.one(f"prod{s}"))
                    e.wait_ge(V.sem, V.at(t, "P"))
                    for s in (2, 3):
                        value_product(e, s).then_inc(P.sem, P.one(f"vprod{s}"))
                    e.wait_ge(V.sem, V.at(t, "vareps"))
                    e.tensor_tensor(rstd[:, :], ve[:, :], half[0:TILE, :], ALU.pow).then_inc(P.sem, P.one("rstd"))
                    qprep_pool(e, P, A, t, qT, qh, qrest, qm, ql, qx, parity)


def cross_attention(nc, bank, name, W, qx_dram, mask_rows, at_dram, consts, I):
    UT = 2 * PAIRS
    TURNS = SEQS // 2
    LAG = 2
    K_AT, SUM_AT, V_AT = (0, 1, 2), 3, (4, 5, 6)
    SCORES, PV, MISC = 3, 6, 7
    Q = 2 * SEQ
    with Stage(nc, name) as g:
        wk, wv, bk = g.sb("wk", [D, D]), g.sb("wv", [D, D]), g.sb("bk", [D, 1])
        ctx = [g.sb(f"ctx{i}", [D, KEYS]) for i in range(2)]
        kf, krest = g.sb("kf", [D, KEYS]), g.sb("krest", [D, KB])
        kp = g.sb("kparts", [D, 4, KEYS], BF16)
        ks = [g.sb(f"kstack{i}", [STACK, PAIRS, KEYS], BF16) for i in range(2)]
        qs = [g.sb(f"qstack{i}", [STACK, PAIRS, Q], BF16) for i in range(2)]
        vs = [g.sb(f"v{i}", [CH, CHUNKS, PAIRS, 2 * PR]) for i in range(2)]
        pt = [g.sb(f"probs{i}", [CH, CB, Q]) for i in range(KBANKS)]
        mx3 = [g.sb(f"mx3_{i}", [Q, KBANKS]) for i in range(2)]
        nmx = [g.sb(f"nmx{i}", [Q, 1], BF16) for i in range(2)]
        pv = [g.sb(f"pv{i}", [D, PAIRS, 2, SEQ]) for i in range(2)]
        rden, att = g.sb("rden", [PR, PAIRS * SEQ]), g.sb("att", [PR, PAIRS * SEQ])
        identb, sumq = consts["identb"], consts["sumq"]
        S = {n: g.sem(n) for n in (
            "weights_loaded", "rows_set", "ctx_loaded0", "ctx_loaded1", "k_ps", "k_f32", "v_ps",
            "v_copied", "q_loaded0", "q_loaded1", "max_ps", "bank_max", "unit_max", "shift_ps", "shift_row",
            "score_ps", "probs", "pv_ps", "pv_copied", "sum_ps", "inv_den", "attended", "stored")}
        k_stacked = [[g.sem(f"k_stacked{i}_half{j}") for j in range(2)] for i in range(2)]
        P = Steps(g.sem("split_steps"), " ".join(f"h{n} rest{n} m{n} l{n} hh{n}" for n in range(KBANKS)))
        KDMA = 16 * PAIRS
        QDMA = 48 if mask_rows is not None else 32

        def turns(e, slot):
            for w in range(UT):
                slot(e, 0, w, True, False)
            with e.Fori(1, TURNS - 1) as i:
                for w in range(UT):
                    slot(e, i, w, False, False)
            for w in range(UT):
                slot(e, TURNS - 1, w, False, True)

        def keys_matmul(e, b, n):
            e.matmul(bank[MISC][:, 0:KB], wk[:, :], ctx[b][:, n * KB:(n + 1) * KB],
                     start=True, stop=True).then_inc(S["k_ps"], 1)

        def values_matmul(e, b, n):
            for c in range(CB):
                lo = (n * CB + c) * CH
                m = e.matmul(bank[MISC][0:CH, c * D:(c + 1) * D], ctx[b][:, lo:lo + CH], wv[:, :], start=True, stop=True)
            m.then_inc(S["v_ps"], 1)

        def scores_matmul(e, u, b, j, k, first_unit):
            if k == 0:
                e.wait_ge(S["shift_row"], u + 1)
            if not first_unit:
                e.wait_ge(S["probs"], (u - 1) * KBANKS + k + 1)
            for c in range(CB):
                lo = (k * CB + c) * CH
                m = e.matmul(bank[SCORES + k][0:CH, c * Q:(c + 1) * Q], ks[b][:, j, lo:lo + CH], qs[b][:, j, :],
                             start=True, stop=True)
            m.then_inc(S["score_ps"], 1)

        def pv_matmul(e, u, b, j, k, first_unit):
            e.wait_ge(S["probs"], u * KBANKS + k + 1)
            if k == 0 and not first_unit:
                e.wait_ge(S["pv_copied"], u)
            for c in range(CB):
                m = e.matmul(bank[PV][32 * c:32 * c + 2 * PR, 0:Q], vs[b][:, k * CB + c, j, :], pt[k][:, c, :],
                             start=(k == 0), stop=(k == KBANKS - 1))
            m.then_inc(S["pv_ps"], 1)

        def shift_matmul(e, u, j):
            e.wait_ge(S["unit_max"], u + 1)
            e.matmul(bank[MISC][SHIFT_ROW:SHIFT_ROW + 1, 0:Q], nmx[j % 2][:, :], identb[0:Q, 0:Q],
                     start=True, stop=True).then_inc(S["shift_ps"], 1)

        def sum_matmul(e, b):
            for hh in range(2):
                m = e.matmul(bank[MISC][0:48, 0:PAIRS * SEQ], sumq[:, hh, :], pv[b][:, :, hh, :],
                             start=(hh == 0), stop=(hh == 1))
            m.then_inc(S["sum_ps"], 1)

        def tensor_slot(e, i, w, first, last):
            b, j = w // PAIRS, w % PAIRS
            seq, u = i * 2 + b, i * UT + w
            start_up = first and w < LAG
            lb, lj, lu = (w - LAG) % UT // PAIRS, (w - LAG) % PAIRS, u - LAG
            more = not (last and b == 1)
            for k in range(KBANKS):
                if k == 0:
                    if j % (PAIRS // 2) == 0:
                        e.wait_ge(k_stacked[b][j // (PAIRS // 2)], (i + 1) * KDMA)
                    if j == 0:
                        e.wait_ge(S[f"q_loaded{b}"], (i + 1) * QDMA)
                if not (first and w == 0):
                    e.wait_ge(S["bank_max"], (u - 1) * KBANKS + k + 1)
                e.matmul(bank[k][0:Q, 0:KB], qs[b][:, j, :], ks[b][:, j, k * KB:(k + 1) * KB],
                         start=True, stop=True).then_inc(S["max_ps"], 1)
                if not start_up:
                    scores_matmul(e, lu, lb, lj, k, first and w == LAG)
                    if k > 0:
                        if k == 1 and lj == 0:
                            e.wait_ge(S["v_copied"], (seq + 1) * KBANKS)
                        pv_matmul(e, lu, lb, lj, k - 1, first and w == LAG)
                if k == 1 and not (first and w == 0):
                    if j in (1, 2, 3) and more:
                        e.wait_ge(S["k_f32"], (seq + 1) * KBANKS + j)
                    if j == 4 and not (first and b == 0):
                        e.wait_ge(S["attended"], seq)
                    if j in (5, 6, 7) and more:
                        e.wait_ge(S["v_copied"], (seq + 1) * KBANKS + j - 4)
                    shift_matmul(e, u - 1, (j - 1) % 2)
            if not start_up:
                pv_matmul(e, lu, lb, lj, KBANKS - 1, first and w == LAG)
            if first and w == 0:
                e.wait_ge(S["v_copied"], KBANKS)
            elif (j in K_AT + V_AT and more) or j == SUM_AT:
                e.wait_ge(S["shift_row"], u)
            if j in K_AT and more:
                if j == 0:
                    e.wait_ge(S[f"ctx_loaded{1 - b}"], (i + b + 1) * 16)
                keys_matmul(e, 1 - b, K_AT.index(j))
            if j in V_AT and more:
                values_matmul(e, 1 - b, V_AT.index(j))
            if j == SUM_AT and not (first and b == 0):
                e.wait_ge(S["pv_copied"], seq * PAIRS)
                sum_matmul(e, 1 - b)

        def key_copy(e, seq, n, first_seq):
            e.wait_ge(S["k_ps"], seq * KBANKS + n + 1)
            if not first_seq:
                e.wait_ge(P.sem, P.at(seq - 1, f"hh{n}"))
            e.activation(kf[:, n * KB:(n + 1) * KB], bank[MISC][:, 0:KB], ACT.Identity, bias=bk[:, :]).then_inc(S["k_f32"], 1)

        def value_copy(e, seq, b, n):
            e.wait_ge(S["v_ps"], seq * KBANKS + n + 1)
            e.copy(vs[b][:, n * CB:(n + 1) * CB, :, 0:PR],
                   bank[MISC][0:CH, :].rearrange("p (c j r) -> p c j r", c=CB, r=PR)).then_inc(S["v_copied"], 1)

        def exp_bank(e, u, k, first_unit):
            e.wait_ge(S["score_ps"], u * KBANKS + k + 1)
            if not first_unit:
                e.wait_ge(S["pv_ps"], (u - 1) * KBANKS + k + 1)
            e.activation(pt[k][:, :, :], bank[SCORES + k][0:CH, 0:CB * Q].rearrange("p (c q) -> p c q", c=CB),
                         ACT.Exp).then_inc(S["probs"], 1)

        def pv_copy(e, u, b, j):
            e.wait_ge(S["pv_ps"], (u + 1) * KBANKS)
            e.copy(pv[b][:, j, :, :], bank[PV][:, 0:Q].rearrange("p (h q) -> p h q", h=2)).then_inc(S["pv_copied"], 1)

        def scalar_slot(e, i, w, first, last):
            b, j = w // PAIRS, w % PAIRS
            seq, u = i * 2 + b, i * UT + w
            lb, lj, lu = (w - LAG) % UT // PAIRS, (w - LAG) % PAIRS, u - LAG
            more = not (last and b == 1)
            if not (first and w < LAG):
                for k in range(KBANKS):
                    exp_bank(e, lu, k, first and w == LAG)
                if lj == 0 and not (first and w < LAG + UT):
                    e.wait_ge(S["sum_ps"], seq - 1)
                pv_copy(e, lu, lb, lj)
            if j in K_AT and more:
                key_copy(e, seq + 1, K_AT.index(j), False)
            if j in V_AT and more:
                value_copy(e, seq + 1, 1 - b, V_AT.index(j))

        def shift_copy(e, u, b, j):
            e.wait_ge(S["shift_ps"], u + 1)
            e.tensor_copy(qs[b][SHIFT_ROW:SHIFT_ROW + 1, j, :], bank[MISC][SHIFT_ROW:SHIFT_ROW + 1, 0:Q]).then_inc(S["shift_row"], 1)

        def divide(e, seq, first_seq):
            e.wait_ge(S["sum_ps"], seq + 1)
            e.reciprocal(rden[:, :], bank[MISC][32:48, 0:PAIRS * SEQ]).then_inc(S["inv_den"], 1)
            e.wait_ge(S["inv_den"], seq + 1)
            if not first_seq:
                e.wait_ge(S["stored"], seq * 16)
            e.tensor_tensor(att[:, :], bank[MISC][0:PR, 0:PAIRS * SEQ], rden[:, :], ALU.mult).then_inc(S["attended"], 1)

        def vector_slot(e, i, w, first, last):
            b, j = w // PAIRS, w % PAIRS
            seq, u = i * 2 + b, i * UT + w
            for k in range(KBANKS):
                e.wait_ge(S["max_ps"], u * KBANKS + k + 1)
                e.tensor_reduce(mx3[w % 2][:, k:k + 1], bank[k][0:Q, 0:KB], AX, ALU.max).then_inc(S["bank_max"], 1)
                if k == 1:
                    if j == 4 and not (first and b == 0):
                        divide(e, seq - 1, first and b == 1)
                    if not (first and w == 0):
                        shift_copy(e, u - 1, (w - 1) % UT // PAIRS, (w - 1) % PAIRS)
            e.wait_ge(S["bank_max"], (u + 1) * KBANKS)
            e.tensor_reduce(nmx[w % 2][:, :], mx3[w % 2][:, :], AX, ALU.max, negate=True).then_inc(S["unit_max"], 1)

        def split_keys(e, seq, first_seq, pieces, waits):
            if waits is not None:
                for sem in k_stacked[waits[0]]:
                    hold(e, sem, waits[1])
            for n in pieces:
                cols = slice(n * KB, (n + 1) * KB)
                hold(e, S["k_f32"], seq * KBANKS + n + 1)
                e.tensor_copy(kp[:, 0, cols], kf[:, cols]).then_inc(P.sem, P.one(f"h{n}"))
                hold(e, P.sem, P.at(seq, f"h{n}"))
                e.tensor_tensor(krest[:, :], kf[:, cols], kp[:, 0, cols], ALU.subtract).then_inc(P.sem, P.one(f"rest{n}"))
                hold(e, P.sem, P.at(seq, f"rest{n}"))
                e.tensor_copy(kp[:, 1, cols], krest[:, :]).then_inc(P.sem, P.one(f"m{n}"))
                hold(e, P.sem, P.at(seq, f"m{n}"))
                e.tensor_tensor(kp[:, 3, cols], krest[:, :], kp[:, 1, cols], ALU.subtract).then_inc(P.sem, P.one(f"l{n}"))
                e.tensor_copy(kp[:, 2, cols], kf[:, cols]).then_inc(P.sem, P.one(f"hh{n}"))
                hold(e, P.sem, P.at(seq, f"hh{n}"))

        def gpsimd_slot(e, i, w, first, last):
            b, j = w // PAIRS, w % PAIRS
            if j == 0 and not (last and b == 1):
                split_keys(e, i * 2 + b + 1, False, range(KBANKS), (b, (i + 1) * KDMA))

        def load_queries(e, seq, b):
            e.dma_start(qs[b][0:SROWS, :, :], qx_dram[seq].rearrange("j r n -> r j n")).then_inc(S[f"q_loaded{b}"], 16)
            e.dma_start(qs[b][SHIFT_ROW:STACK, :, :], I["query_rows"]).then_inc(S[f"q_loaded{b}"], 16)
            if mask_rows is not None:
                e.dma_start(ks[b][MASK_ROW:STACK, :, :],
                            mask_rows[seq].rearrange("(a n) -> a n", a=1).unsqueeze(1).broadcast_to([1, PAIRS, KEYS])
                            ).then_inc(S[f"q_loaded{b}"], 16)

        def stack_keys(e, seq, b):
            hold(e, P.sem, P.turns(seq + 1))
            for j in range(PAIRS):
                for a in range(2):
                    e.dma_start(ks[b][a * SROWS // 2:(a + 1) * SROWS // 2, j, :],
                                kp[PR * j:PR * (j + 1), a:a + 3, :]).then_inc(k_stacked[b][j // (PAIRS // 2)], 16)

        def store(e, seq):
            hold(e, S["attended"], seq + 1)
            e.dma_start(at_dram.rearrange("(j r) t -> r j t", r=PR)[:, :, bass.ds(seq * SEQ, SEQ)],
                        att[:, :].rearrange("r (j q) -> r j q", j=PAIRS)).then_inc(S["stored"], 16)

        def sync_seq(e, i, w, first, last):
            b, j = w // PAIRS, w % PAIRS
            if j:
                return
            seq = i * 2 + b
            if not last:
                hold(e, S["v_ps"], (seq + 1) * KBANKS)
                e.dma_start(ctx[b][:, :], I["ctxT"][seq + 2]).then_inc(S[f"ctx_loaded{b}"], 16)
            if not (last and b == 1):
                if not (first and b == 0):
                    hold(e, S["score_ps"], seq * PAIRS * KBANKS)
                load_queries(e, seq + 1, 1 - b)
                stack_keys(e, seq + 1, 1 - b)
            if not (first and b == 0):
                store(e, seq - 1)

        with nc.Block() as block:
            @block.sync
            def _(e):
                load_all(e, S["weights_loaded"], [(wk[:, :], I[W + "WkT"]), (wv[:, :], I[W + "WvT"]), (bk[:, :], column(I[W + "bk"]))])
                for b in range(2):
                    e.dma_start(ctx[b][:, :], I["ctxT"][b]).then_inc(S[f"ctx_loaded{b}"], 16)
                hold(e, S["rows_set"], 6)
                load_queries(e, 0, 0)
                stack_keys(e, 0, 0)
                turns(e, sync_seq)
                store(e, SEQS - 1)
                hold(e, S["stored"], SEQS * 16)

            @block.tensor
            def _(e):
                e.wait_ge(S["weights_loaded"], 48)
                e.wait_ge(S["ctx_loaded0"], 16)
                for n in range(KBANKS):
                    if n:
                        e.wait_ge(S["k_f32"], n)
                    keys_matmul(e, 0, n)
                e.wait_ge(S["k_f32"], KBANKS)
                for n in range(KBANKS):
                    if n:
                        e.wait_ge(S["v_copied"], n)
                    values_matmul(e, 0, n)
                turns(e, tensor_slot)
                last = SEQS * PAIRS
                e.wait_ge(S["bank_max"], last * KBANKS)
                shift_matmul(e, last - 1, 1)
                for u in range(last - LAG, last):
                    for k in range(KBANKS):
                        scores_matmul(e, u, 1, u % PAIRS, k, False)
                        pv_matmul(e, u, 1, u % PAIRS, k, False)
                e.wait_ge(S["pv_copied"], last)
                sum_matmul(e, 1)

            @block.scalar
            def _(e):
                e.wait_ge(S["weights_loaded"], 48)
                for n in range(KBANKS):
                    key_copy(e, 0, n, True)
                e.wait_ge(S["rows_set"], 6)
                for n in range(KBANKS):
                    value_copy(e, 0, 0, n)
                turns(e, scalar_slot)
                last = SEQS * PAIRS
                for u in range(last - LAG, last):
                    for k in range(KBANKS):
                        exp_bank(e, u, k, False)
                    pv_copy(e, u, 1, u % PAIRS)

            @block.vector
            def _(e):
                turns(e, vector_slot)
                shift_copy(e, SEQS * PAIRS - 1, 1, PAIRS - 1)
                divide(e, SEQS - 1, False)

            @block.gpsimd
            def _(e):
                for b in range(2):
                    for n, (place, value) in enumerate(((ks[b][SHIFT_ROW:STACK, :, :], 0.0), (vs[b][:, :, :, PR:2 * PR], 1.0),
                                                        (ks[b][SHIFT_ROW:SHIFT_ROW + 1, :, :], 1.0))):
                        if 3 * b + n:
                            e.wait_ge(S["rows_set"], 3 * b + n)
                        e.memset(place, value).then_inc(S["rows_set"], 1)
                e.wait_ge(S["rows_set"], 6)
                split_keys(e, 0, True, range(KBANKS), None)
                turns(e, gpsimd_slot)


def project_and_route(nc, bank, name, layer, at_dram, x_in, x_out, xT_dram, cT_dram, consts, I):
    W = f"L{layer}_xattn_"
    E = E0 if layer == 0 else E1
    with Stage(nc, name) as g:
        AT, X = g.sb("AT", [D, GROUP]), g.sb("X", [TILE, TILES, D])
        wo, wr = g.sb("wo", [D, D]), g.sb("wr", [D, E])
        bo, bv = g.sb("bo", [TILE, D]), g.sb("bv", [D, 1])
        r, xn, xT = g.sb("r", [TILE, TILES, D]), g.sb("xn", [TILE, TILES, D]), g.sb("xT", [D, GROUP])
        stats, mv, ve, rstd = g.sb("stats", [TILE, 4, 6]), g.sb("mv", [TILE, 4, 2]), g.sb("ve", [TILE, 4]), g.sb("rstd", [TILE, 4])
        sc, c, cT = g.sb("sc", [TILE, TILES, E]), g.sb("c", [TILE, TILES, E]), g.sb("cT", [E, GROUP])
        den = g.sb("den", [TILE, TILES])
        ident, half = consts["ident"], consts["minus_half"]
        if layer == 0:
            cb = g.sb("cb", [TILE, E])
            sfc, t8 = g.sb("sfc", [TILE, TILES, E]), g.sb("t8", [TILE, TILES, G0, 8])
            gs, gtop, gm = g.sb("gs", [TILE, TILES, 12]), g.sb("gtop", [TILE, TILES, 8]), g.sb("gm", [TILE, TILES, 12])
            masked, etop, em = g.sb("masked", [TILE, TILES, E]), g.sb("etop", [TILE, TILES, 8]), g.sb("em", [TILE, TILES, E])
            route = ("plus1 scores biased top2 gsum " + " ".join(f"gtop{s}" for s in range(4)) + " rep "
                     + " ".join(f"gpick{s}" for s in range(4)) + " gmask masked " + " ".join(f"etop{s}" for s in range(4)) + " "
                     + " ".join(f"epick{s}" for s in range(4)) + " emask chosen csum csum_eps cinv weights")
        else:
            b2 = g.sb("b2", [E1, D])
            top = g.sb("top", [TILE, TILES, 8])
            yb = g.sb("yb", [D, GROUP])
            route = " ".join(f"gtop{s}" for s in range(4)) + " keep less kept csum cinv weights"
        weights, loaded, stored, set_ = g.sem("weights_loaded"), g.sem("group_loaded"), g.sem("group_stored"), g.sem("sentinels_set")
        T = Steps(g.sem("tensor_steps"), "y_ps xT_ps logits_ps cT_ps")
        A = Steps(g.sem("scalar_steps"), "AT xT exp cT")
        V = Steps(g.sem("vector_steps"), "y_bias y_res " + NORM_VEC + " " + route)
        P = Steps(g.sem("gpsimd_steps"), "rstd")
        nw = [0]
        with nc.Block() as block:
            @block.sync
            def _(e):
                ws = [(wo[:, :], I[W + "WoT"]), (bo[:, :], rows_of(I[W + "bo"])), (bv[:, :], column(I[W + "bv"])),
                      (wr[:, :], I["router" + str(layer)])]
                ws += [(cb[:, :], rows_of(I["L0_ffn_correction_bias"]))] if layer == 0 else []
                nw[0] = load_all(e, weights, ws)
                with e.Fori(0, GROUPS) as t:
                    e.dma_start(AT[:, :], at_dram[:, bass.ds(t * GROUP, GROUP)]).then_inc(loaded, 16)
                    e.dma_start(X[:, :, :], tok_major(x_in, t)).then_inc(loaded, 16)
                    hold(e, V.sem, V.at(t, "normed3"))
                    e.dma_start(tok_major(x_out, t), xn[:, :, :]).then_inc(stored, 16)
                    hold(e, A.sem, A.at(t, "xT"))
                    e.dma_start(xT_dram[:, bass.ds(t * GROUP, GROUP)], xT[:, :]).then_inc(stored, 16)
                    hold(e, A.sem, A.at(t, "cT"))
                    e.dma_start(cT_dram[0:E, bass.ds(t * GROUP, GROUP)], cT[:, :]).then_inc(stored, 16)
                    hold(e, stored, (t + 1) * 48)
                    for X_ in (T, A, V, P):
                        hold(e, X_.sem, X_.turns(t + 1))

            @block.tensor
            def _(e):
                e.wait_ge(weights, nw[0])
                with e.Fori(0, GROUPS) as t:
                    e.wait_ge(loaded, (t + 1) * 32)
                    e.wait_ge(A.sem, A.at(t, "AT"))
                    for s in range(TILES):
                        m = e.matmul(bank[0][0:TILE, s * D:(s + 1) * D], AT[:, s * TILE:(s + 1) * TILE], wo[:, :], start=True, stop=True)
                    m.then_inc(T.sem, T.one("y_ps"))
                    e.wait_ge(V.sem, V.at(t, "normed3"))
                    for s in range(TILES):
                        m = e.transpose(bank[1][:, s * TILE:(s + 1) * TILE], xn[:, s, :], ident[0:TILE, 0:TILE])
                    m.then_inc(T.sem, T.one("xT_ps"))
                    e.wait_ge(A.sem, A.at(t, "xT"))
                    for s in range(TILES):
                        m = e.matmul(bank[2][0:TILE, s * E:(s + 1) * E], xT[:, s * TILE:(s + 1) * TILE], wr[:, :], start=True, stop=True)
                    m.then_inc(T.sem, T.one("logits_ps"))
                    hold(e, V.sem, V.at(t, "weights"))
                    for s in range(TILES):
                        m = e.transpose(bank[3][0:E, s * TILE:(s + 1) * TILE], c[:, s, :], ident[0:TILE, 0:TILE])
                    m.then_inc(T.sem, T.one("cT_ps"))

            @block.scalar
            def _(e):
                e.wait_ge(weights, nw[0])
                with e.Fori(0, GROUPS) as t:
                    e.wait_ge(loaded, (t + 1) * 32)
                    e.activation(AT[:, :], AT[:, :], ACT.Identity, bias=bv[:, :]).then_inc(A.sem, A.one("AT"))
                    e.wait_ge(T.sem, T.at(t, "xT_ps"))
                    e.copy(xT[:, :], bank[1][:, 0:GROUP]).then_inc(A.sem, A.one("xT"))
                    if layer == 0:
                        e.wait_ge(T.sem, T.at(t, "logits_ps"))
                        e.activation(sc[:, :, :], bank[2][0:TILE, 0:TILES * E].rearrange("p (s n) -> p s n", s=TILES), ACT.Exp, scale=-1.0).then_inc(A.sem, A.one("exp"))
                    else:
                        e.wait_ge(V.sem, V.at(t, "less"))
                        e.activation(sc[:, :, :], c[:, :, :], ACT.Exp).then_inc(A.sem, A.one("exp"))
                    e.wait_ge(T.sem, T.at(t, "cT_ps"))
                    e.copy(cT[:, :], bank[3][0:E, 0:GROUP]).then_inc(A.sem, A.one("cT"))

            @block.vector
            def _(e):
                e.wait_ge(weights, nw[0])
                if layer == 0:
                    e.memset(gs[:, :, 8:12], ABSENT).then_inc(set_, 1)
                    e.memset(gtop[:, :, :], ABSENT).then_inc(set_, 1)
                    e.wait_ge(set_, 2)

                def step(before, name, f):
                    e.wait_ge(V.sem, V.at(t, before))
                    return f().then_inc(V.sem, V.one(name))

                with e.Fori(0, GROUPS) as t:
                    e.wait_ge(loaded, (t + 1) * 32)
                    e.wait_ge(T.sem, T.at(t, "y_ps"))
                    e.tensor_tensor(r[:, :, :], bank[0][0:TILE, :].rearrange("p (s d) -> p s d", s=TILES), bc(bo[:, :], TILES, 1), ALU.add).then_inc(V.sem, V.one("y_bias"))
                    e.wait_ge(V.sem, V.at(t, "y_bias"))
                    e.tensor_tensor(r[:, :, :], r[:, :, :], X[:, :, :], ALU.add).then_inc(V.sem, V.one("y_res"))
                    norm_vector(e, V, P, t, r, stats, mv, ve, rstd, xn, "y_res")
                    if layer == 0:
                        e.wait_ge(A.sem, A.at(t, "exp"))
                        e.tensor_scalar(sc[:, :, :], sc[:, :, :], 1.0, None, ALU.add).then_inc(V.sem, V.one("plus1"))
                        step("plus1", "scores", lambda: e.reciprocal(sc[:, :, :], sc[:, :, :]))
                        step("scores", "biased", lambda: e.tensor_tensor(sfc[:, :, :], sc[:, :, :], bc(cb[:, :], TILES, 1), ALU.add))
                        hold(e, V.sem, V.at(t, "biased"))
                        for s in range(TILES):
                            for k in range(G0):
                                m = e.max(t8[:, s, k, :], sfc[:, s, k * 8:(k + 1) * 8])
                        m.then_inc(V.sem, V.one("top2"))
                        step("top2", "gsum", lambda: e.tensor_tensor(gs[:, :, 0:8], t8[:, :, :, 0], t8[:, :, :, 1], ALU.add))
                        hold(e, V.sem, V.at(t, "gsum"))
                        for s in range(TILES):
                            e.max(em[:, s, 0:8], gs[:, s, 0:8]).then_inc(V.sem, V.one(f"gtop{s}"))
                        step("gtop3", "rep", lambda: e.tensor_copy(gtop[:, :, 0:4], em[:, :, 0:4]))
                        hold(e, V.sem, V.at(t, "rep"))
                        for s in range(TILES):
                            e.match_replace(out=gm[:, s, :], in_to_replace=gtop[:, s, :], in_values=gs[:, s, :], imm_value=PICKED).then_inc(V.sem, V.one(f"gpick{s}"))
                        step("gpick3", "gmask", lambda: e.tensor_scalar(gm[:, :, 0:8], gm[:, :, 0:8], PICKED, None, ALU.is_ge))
                        step("gmask", "masked", lambda: e.tensor_tensor(masked[:, :, :].rearrange("p s (g n) -> p s g n", g=G0),
                             sfc[:, :, :].rearrange("p s (g n) -> p s g n", g=G0), bc(gm[:, :, 0:8], 8, 3), ALU.mult))
                        hold(e, V.sem, V.at(t, "masked"))
                        for s in range(TILES):
                            e.max(etop[:, s, :], masked[:, s, :]).then_inc(V.sem, V.one(f"etop{s}"))
                        hold(e, V.sem, V.at(t, "etop3"))
                        for s in range(TILES):
                            e.match_replace(out=em[:, s, :], in_to_replace=etop[:, s, :], in_values=masked[:, s, :], imm_value=PICKED).then_inc(V.sem, V.one(f"epick{s}"))
                        step("epick3", "emask", lambda: e.tensor_scalar(em[:, :, :], em[:, :, :], PICKED, None, ALU.is_ge))
                        step("emask", "chosen", lambda: e.tensor_tensor(c[:, :, :], em[:, :, :], sc[:, :, :], ALU.mult))
                        step("chosen", "csum", lambda: e.tensor_reduce(den[:, :], c[:, :, :], AX, ALU.add))
                        step("csum", "csum_eps", lambda: e.tensor_scalar(den[:, :], den[:, :], 1e-20, None, ALU.add))
                        step("csum_eps", "cinv", lambda: e.reciprocal(den[:, :], den[:, :]))
                        e.wait_ge(V.sem, V.at(t, "cinv"))
                        for s in range(TILES):
                            m = e.tensor_scalar(c[:, s, :], c[:, s, :], den[:, s:s + 1], 2.5, ALU.mult, ALU.mult)
                        m.then_inc(V.sem, V.one("weights"))
                    else:
                        gate = bank[2][0:TILE, 0:TILES * E].rearrange("p (s n) -> p s n", s=TILES)
                        hold(e, T.sem, T.at(t, "logits_ps"))
                        for s in range(TILES):
                            e.max(top[:, s, :], gate[:, s, :]).then_inc(V.sem, V.one(f"gtop{s}"))
                        step("gtop3", "keep", lambda: e.tensor_tensor(r[:, :, 0:E], gate, bc(top[:, :, 1], E, 2), ALU.is_ge))
                        e.tensor_tensor(c[:, :, :], gate, bc(top[:, :, 0], E, 2), ALU.subtract).then_inc(V.sem, V.one("less"))
                        e.wait_ge(A.sem, A.at(t, "exp"))
                        e.tensor_tensor(c[:, :, :], sc[:, :, :], r[:, :, 0:E], ALU.mult).then_inc(V.sem, V.one("kept"))
                        step("kept", "csum", lambda: e.tensor_reduce(den[:, :], c[:, :, :], AX, ALU.add))
                        step("csum", "cinv", lambda: e.reciprocal(den[:, :], den[:, :]))
                        e.wait_ge(V.sem, V.at(t, "cinv"))
                        for s in range(TILES):
                            m = e.tensor_scalar(c[:, s, :], c[:, s, :], den[:, s:s + 1], 1.0 / E1, ALU.mult, ALU.mult)
                        m.then_inc(V.sem, V.one("weights"))

            @block.gpsimd
            def _(e):
                with e.Fori(0, GROUPS) as t:
                    e.wait_ge(V.sem, V.at(t, "vareps"))
                    e.tensor_tensor(rstd[:, :], ve[:, :], half[0:TILE, :], ALU.pow).then_inc(P.sem, P.one("rstd"))


def experts(nc, bank, name, layer, xT_dram, cT_dram, yT_dram, consts, I):
    NCH, CPT = (NCH0, 2) if layer == 0 else (NCH1, I1 // 128)
    TURNS, UT, LAG, RING = NCH // CPT, CPT * GROUPS, 3, 4
    ACC, UP = 0, 4
    with Stage(nc, name) as g:
        xT = g.sb("xT", [D, GROUPS, GROUP])
        wu = [g.sb(f"wu{i}", [D, D]) for i in range(2)]
        wd = [g.sb(f"wd{i}", [D, D]) for i in range(2)]
        cB = [g.sb(f"cB{i}", [D, GROUPS, GROUP]) for i in range(2)]
        b1 = [g.sb(f"b1_{i}", [D, 1]) for i in range(2)]
        hr = [g.sb(f"relu{i}", [D, GROUP]) for i in range(RING)]
        hc = [g.sb(f"weighted{i}", [D, GROUP]) for i in range(RING)]
        h2 = [g.sb(f"squared{i}", [D, GROUP]) for i in range(RING)] if layer == 0 else hc
        b2, cT = g.sb("b2", [E1, D]), g.sb("cT", [E1, GROUPS, GROUP])
        out = g.sb("out", [D, GROUPS, GROUP])
        S = {n: g.sem(n) for n in ("x_loaded", "up_loaded0", "up_loaded1", "up_ps", "relu", "weighted", "squared", "down_ps", "copied", "stored", "bias_set", "ones_stored")}
        done = S["squared"] if layer == 0 else S["weighted"]
        NL = 16 * 4

        def load_chunk(e, i, cc):
            f, b = i * CPT + cc, cc % 2
            for dst, src in ((wu[b][:, :], I[f"up{layer}"][f]), (wd[b][:, :], I[f"down{layer}"][f])):
                e.dma_start(dst, src).then_inc(S[f"up_loaded{b}"], 16)
            if layer == 0:
                for h in range(2):
                    e.dma_start(cB[b][64 * h:64 * h + 64, :, :], cT_dram[2 * f + h].rearrange("(a g n) -> a g n", a=1, g=GROUPS).broadcast_to([64, GROUPS, GROUP])).then_inc(S[f"up_loaded{b}"], 16)
            else:
                e.dma_start(cB[b][:, :, :], cT_dram[i].rearrange("(a g n) -> a g n", a=1, g=GROUPS).broadcast_to([D, GROUPS, GROUP])).then_inc(S[f"up_loaded{b}"], 16)
                e.dma_start(b1[b][:, :], I["b1"][f]).then_inc(S[f"up_loaded{b}"], 16)

        def sync_turn(e, i):
            for cc in range(CPT):
                hold(e, S["down_ps"], (i * CPT + cc - 1) * GROUPS)
                load_chunk(e, i, cc)

        def chunk_loaded(e, i, cc):
            e.wait_ge(S[f"up_loaded{cc % 2}"], (i * (CPT // 2) + cc // 2 + 1) * NL)

        def tensor_unit(e, i, w, first):
            b, k = w // GROUPS % 2, w % GROUPS
            u = i * UT + w
            if k == 0:
                chunk_loaded(e, i, w // GROUPS)
            if not (first and w < 2):
                e.wait_ge(S["relu"], u - 1)
            e.matmul(bank[UP + w % 2][:, 0:GROUP], wu[b][:, :], xT[:, k, :], start=True, stop=True).then_inc(S["up_ps"], 1)
            if not (first and w < LAG):
                down(e, u - LAG, (w - LAG) % UT)

        def down(e, u, w):
            e.wait_ge(done, u + 1)
            e.matmul(bank[ACC + w % GROUPS][:, 0:GROUP], wd[w // GROUPS % 2][:, :], h2[w % RING][:, :],
                     start=False, stop=False, skip_group_check=True).then_inc(S["down_ps"], 1)

        def scalar_unit(e, i, w, first):
            b, u = w // GROUPS % 2, i * UT + w
            e.wait_ge(S["up_ps"], u + 1)
            if not (first and w < RING):
                e.wait_ge(done, u - RING + 1)
            e.activation(hr[w % RING][:, :], bank[UP + w % 2][:, 0:GROUP], ACT.Relu, bias=b1[b][:, :]).then_inc(S["relu"], 1)

        def vector_unit(e, i, w, first):
            b, u = w // GROUPS % 2, i * UT + w
            e.wait_ge(S["relu"], u + 1)
            if not (first and w < RING):
                e.wait_ge(S["squared"] if layer == 0 else S["down_ps"], u - RING + 1)
            e.tensor_tensor(hc[w % RING][:, :], hr[w % RING][:, :], cB[b][:, w % GROUPS, :], ALU.mult).then_inc(S["weighted"], 1)

        def gpsimd_unit(e, i, w, first):
            u = i * UT + w
            e.wait_ge(S["weighted"], u + 1)
            if not (first and w < RING):
                e.wait_ge(S["down_ps"], u - RING + 1)
            e.tensor_tensor(h2[w % RING][:, :], hc[w % RING][:, :], hr[w % RING][:, :], ALU.mult).then_inc(S["squared"], 1)

        def turns(e, unit):
            for w in range(UT):
                unit(e, 0, w, True)
            with e.Fori(1, TURNS) as i:
                for w in range(UT):
                    unit(e, i, w, False)

        with nc.Block() as block:
            @block.sync
            def _(e):
                if layer == 0:
                    e.dma_start(cT_dram[E0:E0 + SHARED // I0], I["ones_rows"]).then_inc(S["ones_stored"], 16)
                    hold(e, S["ones_stored"], 16)
                e.dma_start(xT[:, :, :], xT_dram.rearrange("d (g n) -> d g n", g=GROUPS)).then_inc(S["x_loaded"], 16)
                e.dma_start(b2[:, :], I["b2_or_zero" + str(layer)]).then_inc(S["x_loaded"], 16)
                e.dma_start(cT[:, :, :], cT_dram[0:E1].rearrange("c (g n) -> c g n", g=GROUPS)).then_inc(S["x_loaded"], 16)
                for cc in range(CPT):
                    if cc >= 2:
                        hold(e, S["down_ps"], (cc - 1) * GROUPS)
                    load_chunk(e, 0, cc)
                with e.Fori(1, TURNS) as i:
                    sync_turn(e, i)
                hold(e, S["copied"], GROUPS)
                e.dma_start(yT_dram.rearrange("d (g n) -> d g n", g=GROUPS), out[:, :, :]).then_inc(S["stored"], 16)
                hold(e, S["stored"], 16)

            @block.tensor
            def _(e):
                e.wait_ge(S["x_loaded"], 48)
                for k in range(GROUPS):
                    e.matmul(bank[ACC + k][:, 0:GROUP], b2[:, :], cT[:, k, :], start=True, stop=False, skip_group_check=True)
                turns(e, tensor_unit)
                for w in range(UT - LAG, UT):
                    down(e, (TURNS - 1) * UT + w, w)

            @block.scalar
            def _(e):
                if layer == 0:
                    e.wait_ge(S["bias_set"], 2)

                def unit(e, i, w, first):
                    if layer and w % GROUPS == 0:
                        chunk_loaded(e, i, w // GROUPS)
                    scalar_unit(e, i, w, first)
                turns(e, unit)

            @block.vector
            def _(e):
                if layer == 0:
                    for b in range(2):
                        e.memset(b1[b][:, :], 0.0).then_inc(S["bias_set"], 1)

                def unit(e, i, w, first):
                    if w % GROUPS == 0:
                        chunk_loaded(e, i, w // GROUPS)
                    vector_unit(e, i, w, first)
                turns(e, unit)
                e.wait_ge(S["down_ps"], TURNS * UT)
                for k in range(GROUPS):
                    e.tensor_copy(out[:, k, :], bank[ACC + k][:, 0:GROUP]).then_inc(S["copied"], 1)

            if layer == 0:
                @block.gpsimd
                def _(e):
                    turns(e, gpsimd_unit)


def norm_and_project_1(nc, bank, yT_dram, x_in, x3, qkT_dram, v_dram, consts, I):
    with Stage(nc, "np1") as g:
        YT, X = g.sb("YT", [D, GROUP]), g.sb("X", [TILE, TILES, D])
        w = g.sb("w", [D, 3, D])
        qks = g.sb("qks", [D, 2])
        ident, half, ones8, plus = consts["ident"], consts["minus_half"], g.sb("ones8", [D, D]), g.sb("plus_half", [D, 1])
        r, xn, xT = g.sb("r", [TILE, TILES, D]), g.sb("xn", [TILE, TILES, D]), g.sb("xT", [D, GROUP])
        stats, mv, ve, rstd = g.sb("stats", [TILE, 4, 6]), g.sb("mv", [TILE, 4, 2]), g.sb("ve", [TILE, 4]), g.sb("rstd", [TILE, 4])
        qk, sig, sq, nrm = [g.sb(n, [D, 2, GROUP]) for n in ("qk", "sig", "sq", "nrm")]
        v, sv = g.sb("v", [TILE, TILES, D]), g.sb("sv", [TILE, TILES, D])
        weights, loaded, stored, set_ = g.sem("weights_loaded"), g.sem("group_loaded"), g.sem("group_stored"), g.sem("half_set")
        T = Steps(g.sem("tensor_steps"), "y_ps xT_ps q_ps k_ps v_ps norms_ps")
        A = Steps(g.sem("scalar_steps"), "xT expq expk expv norms")
        V = Steps(g.sem("vector_steps"), "y_res " + NORM_VEC + " plus1 inv silu_q silu_k squares vplus1 vinv silu_v r_eps r_inv ratio scaled_q scaled_k")
        P = Steps(g.sem("gpsimd_steps"), "rstd roots")
        with nc.Block() as block:
            @block.sync
            def _(e):
                load_all(e, weights, [(w[:, n, :], I[f"L1_attn_W{c}T"]) for n, c in enumerate("qkv")]
                         + [(qks[:, 0:1], column(I["q_scale_rows"])), (qks[:, 1:2], column(I["k_scale_rows"])), (ones8[:, :], I["ones8"])])
                with e.Fori(0, GROUPS) as t:
                    e.dma_start(YT[:, :], yT_dram[:, bass.ds(t * GROUP, GROUP)]).then_inc(loaded, 16)
                    e.dma_start(X[:, :, :], tok_major(x_in, t)).then_inc(loaded, 16)
                    hold(e, V.sem, V.at(t, "silu_v"))
                    e.dma_start(tok_major(x3, t), xn[:, :, :]).then_inc(stored, 16)
                    e.dma_start(tok_major(v_dram, t), v[:, :, :]).then_inc(stored, 16)
                    hold(e, V.sem, V.at(t, "scaled_k"))
                    e.dma_start(qkT_dram[:, :, bass.ds(t * GROUP, GROUP)], qk[:, :, :]).then_inc(stored, 16)
                    hold(e, stored, (t + 1) * 48)
                    for X_ in (T, A, V, P):
                        hold(e, X_.sem, X_.turns(t + 1))

            @block.tensor
            def _(e):
                e.wait_ge(weights, 96)
                with e.Fori(0, GROUPS) as t:
                    e.wait_ge(loaded, (t + 1) * 32)
                    for s in range(TILES):
                        m = e.transpose(bank[0][0:TILE, s * D:(s + 1) * D], YT[:, s * TILE:(s + 1) * TILE], ident[:, :])
                    m.then_inc(T.sem, T.one("y_ps"))
                    e.wait_ge(V.sem, V.at(t, "normed3"))
                    for s in range(TILES):
                        m = e.transpose(bank[1][:, s * TILE:(s + 1) * TILE], xn[:, s, :], ident[0:TILE, 0:TILE])
                    m.then_inc(T.sem, T.one("xT_ps"))
                    e.wait_ge(A.sem, A.at(t, "xT"))
                    for n, c in enumerate("qk"):
                        e.matmul(bank[2 + n][:, 0:GROUP], w[:, n, :], xT[:, :], start=True, stop=True).then_inc(T.sem, T.one(f"{c}_ps"))
                    for s in range(TILES):
                        m = e.matmul(bank[4][0:TILE, s * D:(s + 1) * D], xT[:, s * TILE:(s + 1) * TILE], w[:, 2, :], start=True, stop=True)
                    m.then_inc(T.sem, T.one("v_ps"))
                    e.wait_ge(V.sem, V.at(t, "squares"))
                    for n in range(2):
                        m = e.matmul(bank[5 + n][:, 0:GROUP], ones8[:, :], sq[:, n, :], start=True, stop=True)
                    m.then_inc(T.sem, T.one("norms_ps"))

            @block.scalar
            def _(e):
                with e.Fori(0, GROUPS) as t:
                    e.wait_ge(loaded, (t + 1) * 32)
                    e.wait_ge(T.sem, T.at(t, "xT_ps"))
                    e.copy(xT[:, :], bank[1][:, 0:GROUP]).then_inc(A.sem, A.one("xT"))
                    for n, c in enumerate("qk"):
                        e.wait_ge(T.sem, T.at(t, f"{c}_ps"))
                        e.activation(sig[:, n, :], bank[2 + n][:, 0:GROUP], ACT.Exp, scale=-1.0).then_inc(A.sem, A.one(f"exp{c}"))
                    e.wait_ge(T.sem, T.at(t, "v_ps"))
                    e.activation(sv[:, :, :], bank[4][0:TILE, :].rearrange("p (s d) -> p s d", s=TILES), ACT.Exp, scale=-1.0).then_inc(A.sem, A.one("expv"))
                    e.wait_ge(T.sem, T.at(t, "norms_ps"))
                    for n in range(2):
                        m = e.copy(nrm[:, n, :], bank[5 + n][:, 0:GROUP])
                    m.then_inc(A.sem, A.one("norms"))

            @block.vector
            def _(e):
                e.wait_ge(weights, 96)

                def step(before, name, f):
                    e.wait_ge(V.sem, V.at(t, before))
                    return f().then_inc(V.sem, V.one(name))

                with e.Fori(0, GROUPS) as t:
                    e.wait_ge(loaded, (t + 1) * 32)
                    e.wait_ge(T.sem, T.at(t, "y_ps"))
                    e.tensor_tensor(r[:, :, :], bank[0][0:TILE, :].rearrange("p (s d) -> p s d", s=TILES), X[:, :, :], ALU.add).then_inc(V.sem, V.one("y_res"))
                    norm_vector(e, V, P, t, r, stats, mv, ve, rstd, xn, "y_res")
                    e.wait_ge(A.sem, A.at(t, "expk"))
                    e.tensor_scalar(sig[:, :, :], sig[:, :, :], 1.0, None, ALU.add).then_inc(V.sem, V.one("plus1"))
                    step("plus1", "inv", lambda: e.reciprocal(sig[:, :, :], sig[:, :, :]))
                    e.wait_ge(V.sem, V.at(t, "inv"))
                    for n, c in enumerate("qk"):
                        e.tensor_tensor(qk[:, n, :], sig[:, n, :], bank[2 + n][:, 0:GROUP], ALU.mult).then_inc(V.sem, V.one(f"silu_{c}"))
                    step("silu_k", "squares", lambda: e.tensor_tensor(sq[:, :, :], qk[:, :, :], qk[:, :, :], ALU.mult))
                    e.wait_ge(A.sem, A.at(t, "expv"))
                    e.tensor_scalar(sv[:, :, :], sv[:, :, :], 1.0, None, ALU.add).then_inc(V.sem, V.one("vplus1"))
                    step("vplus1", "vinv", lambda: e.reciprocal(sv[:, :, :], sv[:, :, :]))
                    step("vinv", "silu_v", lambda: e.tensor_tensor(v[:, :, :], sv[:, :, :], bank[4][0:TILE, :].rearrange("p (s d) -> p s d", s=TILES), ALU.mult))
                    e.wait_ge(P.sem, P.at(t, "roots"))
                    e.tensor_scalar(sig[:, :, :], nrm[:, :, :], 1e-6, None, ALU.add).then_inc(V.sem, V.one("r_eps"))
                    step("r_eps", "r_inv", lambda: e.reciprocal(sig[:, :, :], sig[:, :, :]))
                    step("r_inv", "ratio", lambda: e.tensor_tensor(sig[:, :, :], sig[:, :, :], nrm[:, :, :], ALU.mult))
                    e.wait_ge(V.sem, V.at(t, "ratio"))
                    for n, c in enumerate("qk"):
                        e.scalar_tensor_tensor(out=qk[:, n, :], in0=qk[:, n, :], scalar=qks[:, n:n + 1], in1=sig[:, n, :], op0=ALU.mult, op1=ALU.mult).then_inc(V.sem, V.one(f"scaled_{c}"))

            @block.gpsimd
            def _(e):
                e.memset(plus[:, :], 0.5).then_inc(set_, 1)
                e.wait_ge(set_, 1)
                with e.Fori(0, GROUPS) as t:
                    e.wait_ge(V.sem, V.at(t, "vareps"))
                    e.tensor_tensor(rstd[:, :], ve[:, :], half[0:TILE, :], ALU.pow).then_inc(P.sem, P.one("rstd"))
                    e.wait_ge(A.sem, A.at(t, "norms"))
                    flat = nrm[:, :, :].rearrange("p a n -> p (a n)")
                    e.tensor_tensor(flat, flat, plus[:, :].broadcast_to([D, 2 * GROUP]), ALU.pow).then_inc(P.sem, P.one("roots"))


def causal_attention(nc, bank, qkT_dram, v_dram, oT_dram, consts, I):
    N = HEADS * SEQ
    HH = HEADS // 2
    with Stage(nc, "ca") as g:
        qk = [g.sb(f"qk{i}", [D, 2, SEQ]) for i in range(2)]
        v = [g.sb(f"v{i}", [SEQ, D]) for i in range(2)]
        kx = [g.sb(f"kx{i}", [D, HEADS, SEQ]) for i in range(2)]
        p = [g.sb(f"p{i}", [SEQ, HEADS, SEQ]) for i in range(2)]
        pT = [g.sb(f"pT{i}", [SEQ, HEADS, SEQ]) for i in range(2)]
        mx, den = [g.sb(f"mx{i}", [SEQ, HEADS]) for i in range(2)], [g.sb(f"den{i}", [SEQ, HEADS]) for i in range(2)]
        o, oT = [g.sb(f"o{i}", [SEQ, D]) for i in range(2)], [g.sb(f"oT{i}", [D, SEQ]) for i in range(2)]
        causal, headmask, ident = g.sb("causal", [SEQ, SEQ]), g.sb("headmask", [D, HEADS]), consts["ident"]
        weights = g.sem("weights_loaded")
        loaded = [g.sem(f"seq_loaded{i}") for i in range(2)]
        stored = [g.sem(f"seq_stored{i}") for i in range(2)]
        T = [Steps(g.sem(f"tensor_steps{i}"), "s_ps pT_ps o_ps oT_ps") for i in range(2)]
        A = [Steps(g.sem(f"scalar_steps{i}"), "exp pT_a pT_b o oT") for i in range(2)]
        V = [Steps(g.sem(f"vector_steps{i}"), "masked_a masked_b max sum inv") for i in range(2)]
        P = [Steps(g.sem(f"gpsimd_steps{i}"), "kx shifted probs") for i in range(2)]
        with nc.Block() as block:
            @block.sync
            def _(e):
                load_all(e, weights, [(causal[:, :], I["causal"]), (headmask[:, :], I["headmask"])])
                with e.Fori(0, SEQS // 2) as t:
                    for b in range(2):
                        e.dma_start(qk[b][:, :, :], qkT_dram[:, :, bass.ds((t * 2 + b) * SEQ, SEQ)]).then_inc(loaded[b], 16)
                        e.dma_start(v[b][:, :], v_dram[bass.ds((t * 2 + b) * SEQ, SEQ), :]).then_inc(loaded[b], 16)
                    for b in range(2):
                        hold(e, A[b].sem, A[b].at(t, "oT"))
                        e.dma_start(oT_dram[:, bass.ds((t * 2 + b) * SEQ, SEQ)], oT[b][:, :]).then_inc(stored[b], 16)
                    for b in range(2):
                        hold(e, stored[b], (t + 1) * 16)
                        for X_ in (T[b], A[b], V[b], P[b]):
                            hold(e, X_.sem, X_.turns(t + 1))

            @block.tensor
            def _(e):
                with e.Fori(0, SEQS // 2) as t:
                    for b in range(2):
                        hold(e, loaded[b], (t + 1) * 32)
                        hold(e, P[b].sem, P[b].at(t, "kx"))
                        for h in range(2):
                            m = e.matmul(bank[4 * b + h][0:SEQ, 0:N // 2], qk[b][:, 0, :],
                                         kx[b][:, h * HH:(h + 1) * HH, :], start=True, stop=True)
                        m.then_inc(T[b].sem, T[b].one("s_ps"))
                    for b in range(2):
                        hold(e, P[b].sem, P[b].at(t, "probs"))
                        for h in range(HEADS):
                            m = e.transpose(bank[4 * b + h // HH][0:SEQ, h % HH * SEQ:(h % HH + 1) * SEQ],
                                            p[b][:, h, :], ident[0:SEQ, 0:SEQ])
                        m.then_inc(T[b].sem, T[b].one("pT_ps"))
                    for b in range(2):
                        hold(e, A[b].sem, A[b].at(t, "pT_b"))
                        for h in range(HEADS):
                            m = e.matmul(bank[4 * b + 2][0:SEQ, h * HD:(h + 1) * HD], pT[b][:, h, :], v[b][:, h * HD:(h + 1) * HD],
                                         start=True, stop=True)
                        m.then_inc(T[b].sem, T[b].one("o_ps"))
                    for b in range(2):
                        hold(e, A[b].sem, A[b].at(t, "o"))
                        e.transpose(bank[4 * b + 3][:, 0:SEQ], o[b][:, :], ident[0:SEQ, 0:SEQ]).then_inc(T[b].sem, T[b].one("oT_ps"))

            @block.scalar
            def _(e):
                with e.Fori(0, SEQS // 2) as t:
                    for b in range(2):
                        e.wait_ge(P[b].sem, P[b].at(t, "shifted"))
                        e.activation(p[b][:, :, :], p[b][:, :, :], ACT.Exp).then_inc(A[b].sem, A[b].one("exp"))
                    for b in range(2):
                        e.wait_ge(T[b].sem, T[b].at(t, "pT_ps"))
                        for h in range(2):
                            e.copy(pT[b][:, h * HH:(h + 1) * HH, :], bank[4 * b + h][0:SEQ, 0:N // 2].rearrange("p (h q) -> p h q", h=HH)
                                   ).then_inc(A[b].sem, A[b].one(f"pT_{'ab'[h]}"))
                    for b in range(2):
                        e.wait_ge(T[b].sem, T[b].at(t, "o_ps"))
                        e.copy(o[b][:, :], bank[4 * b + 2][0:SEQ, 0:D]).then_inc(A[b].sem, A[b].one("o"))
                    for b in range(2):
                        e.wait_ge(T[b].sem, T[b].at(t, "oT_ps"))
                        e.copy(oT[b][:, :], bank[4 * b + 3][:, 0:SEQ]).then_inc(A[b].sem, A[b].one("oT"))

            @block.vector
            def _(e):
                e.wait_ge(weights, 32)
                with e.Fori(0, SEQS // 2) as t:
                    for b in range(2):
                        e.wait_ge(T[b].sem, T[b].at(t, "s_ps"))
                        for h in range(2):
                            e.tensor_tensor(p[b][:, h * HH:(h + 1) * HH, :], bank[4 * b + h][0:SEQ, 0:N // 2].rearrange("p (h k) -> p h k", h=HH),
                                            bc(causal[:, :], HH, 1), ALU.add).then_inc(V[b].sem, V[b].one(f"masked_{'ab'[h]}"))
                        e.wait_ge(V[b].sem, V[b].at(t, "masked_b"))
                        e.tensor_reduce(mx[b][:, :], p[b][:, :, :], AX, ALU.max).then_inc(V[b].sem, V[b].one("max"))
                    for b in range(2):
                        e.wait_ge(A[b].sem, A[b].at(t, "exp"))
                        e.tensor_reduce(den[b][:, :], p[b][:, :, :], AX, ALU.add).then_inc(V[b].sem, V[b].one("sum"))
                        e.wait_ge(V[b].sem, V[b].at(t, "sum"))
                        e.reciprocal(den[b][:, :], den[b][:, :]).then_inc(V[b].sem, V[b].one("inv"))

            @block.gpsimd
            def _(e):
                e.wait_ge(weights, 32)
                with e.Fori(0, SEQS // 2) as t:
                    for b in range(2):
                        e.wait_ge(loaded[b], (t + 1) * 32)
                        e.tensor_tensor(kx[b][:, :, :], bc(qk[b][:, 1, :], HEADS, 1), bc(headmask[:, :], SEQ, 2), ALU.mult).then_inc(P[b].sem, P[b].one("kx"))
                    for b in range(2):
                        e.wait_ge(V[b].sem, V[b].at(t, "max"))
                        e.tensor_tensor(p[b][:, :, :], p[b][:, :, :], bc(mx[b][:, :], SEQ, 2), ALU.subtract).then_inc(P[b].sem, P[b].one("shifted"))
                    for b in range(2):
                        e.wait_ge(V[b].sem, V[b].at(t, "inv"))
                        e.tensor_tensor(p[b][:, :, :], p[b][:, :, :], bc(den[b][:, :], SEQ, 2), ALU.mult).then_inc(P[b].sem, P[b].one("probs"))


def project_1(nc, bank, oT_dram, x_in, x_out, qx_dram, consts, I):
    with Stage(nc, "pr1") as g:
        OT, X = g.sb("OT", [D, GROUP]), g.sb("X", [TILE, TILES, D])
        wo, wq, bq, bqs = g.sb("wo", [D, D]), g.sb("wq", [D, D]), g.sb("bq", [D, 1]), g.sb("bqs", [D, 1])
        ident, half, parity = consts["ident"], consts["minus_half"], consts["parity"]
        r, xn, xT, qT = g.sb("r", [TILE, TILES, D]), g.sb("xn", [TILE, TILES, D]), g.sb("xT", [D, GROUP]), g.sb("qT", [D, GROUP])
        stats, mv, ve, rstd = g.sb("stats", [TILE, 4, 6]), g.sb("mv", [TILE, 4, 2]), g.sb("ve", [TILE, 4]), g.sb("rstd", [TILE, 4])
        qh, qm, ql, qrest = g.sb("qh", [D, GROUP], BF16), g.sb("qm", [D, GROUP], BF16), g.sb("ql", [D, GROUP], BF16), g.sb("qrest", [D, GROUP])
        qx = g.sb("qx", [D, GSEQS, PROD, 2, SEQ], BF16)
        weights, loaded, stored, scaled = g.sem("weights_loaded"), g.sem("group_loaded"), g.sem("group_stored"), g.sem("bias_scaled")
        T = Steps(g.sem("tensor_steps"), "y_ps xT_ps qT_ps")
        A = Steps(g.sem("scalar_steps"), "xT qT")
        V = Steps(g.sem("vector_steps"), "y_res " + NORM_VEC)
        P = Steps(g.sem("gpsimd_steps"), "rstd " + QPREP_POOL)
        with nc.Block() as block:
            @block.sync
            def _(e):
                load_all(e, weights, [(wo[:, :], I["L1_attn_WoT"]), (wq[:, :], I["L1_xattn_Wq"]), (bq[:, :], column(I["L1_xattn_bq"]))])
                with e.Fori(0, GROUPS) as t:
                    e.dma_start(OT[:, :], oT_dram[:, bass.ds(t * GROUP, GROUP)]).then_inc(loaded, 16)
                    e.dma_start(X[:, :, :], tok_major(x_in, t)).then_inc(loaded, 16)
                    hold(e, V.sem, V.at(t, "normed3"))
                    e.dma_start(tok_major(x_out, t), xn[:, :, :]).then_inc(stored, 16)
                    hold(e, P.sem, P.at(t, "x_h2"))
                    store_queries(e, stored, t, qx_dram, qx)
                    hold(e, stored, (t + 1) * 16 * (1 + 2 * GSEQS))
                    for X_ in (T, A, V, P):
                        hold(e, X_.sem, X_.turns(t + 1))

            @block.tensor
            def _(e):
                e.wait_ge(weights, 48)
                with e.Fori(0, GROUPS) as t:
                    e.wait_ge(loaded, (t + 1) * 32)
                    for s in range(TILES):
                        m = e.matmul(bank[0][0:TILE, s * D:(s + 1) * D], OT[:, s * TILE:(s + 1) * TILE], wo[:, :], start=True, stop=True)
                    m.then_inc(T.sem, T.one("y_ps"))
                    e.wait_ge(V.sem, V.at(t, "normed3"))
                    for s in range(TILES):
                        m = e.transpose(bank[1][:, s * TILE:(s + 1) * TILE], xn[:, s, :], ident[0:TILE, 0:TILE])
                    m.then_inc(T.sem, T.one("xT_ps"))
                    e.wait_ge(A.sem, A.at(t, "xT"))
                    e.matmul(bank[2][:, 0:GROUP], wq[:, :], xT[:, :], start=True, stop=True).then_inc(T.sem, T.one("qT_ps"))

            @block.scalar
            def _(e):
                e.wait_ge(scaled, 1)
                with e.Fori(0, GROUPS) as t:
                    e.wait_ge(loaded, (t + 1) * 32)
                    e.wait_ge(T.sem, T.at(t, "xT_ps"))
                    e.copy(xT[:, :], bank[1][:, 0:GROUP]).then_inc(A.sem, A.one("xT"))
                    e.wait_ge(T.sem, T.at(t, "qT_ps"))
                    e.activation(qT[:, :], bank[2][:, 0:GROUP], ACT.Identity, bias=bqs[:, :], scale=HD ** -0.5).then_inc(A.sem, A.one("qT"))

            @block.vector
            def _(e):
                e.wait_ge(weights, 48)
                e.tensor_scalar(bqs[:, :], bq[:, :], HD ** -0.5, None, ALU.mult).then_inc(scaled, 1)
                with e.Fori(0, GROUPS) as t:
                    e.wait_ge(loaded, (t + 1) * 32)
                    e.wait_ge(T.sem, T.at(t, "y_ps"))
                    e.tensor_tensor(r[:, :, :], bank[0][0:TILE, :].rearrange("p (s d) -> p s d", s=TILES), X[:, :, :], ALU.add).then_inc(V.sem, V.one("y_res"))
                    norm_vector(e, V, P, t, r, stats, mv, ve, rstd, xn, "y_res")

            @block.gpsimd
            def _(e):
                with e.Fori(0, GROUPS) as t:
                    e.wait_ge(V.sem, V.at(t, "vareps"))
                    e.tensor_tensor(rstd[:, :], ve[:, :], half[0:TILE, :], ALU.pow).then_inc(P.sem, P.one("rstd"))
                    qprep_pool(e, P, A, t, qT, qh, qrest, qm, ql, qx, parity)


def final_norm(nc, bank, yT_dram, x_in, out, consts):
    with Stage(nc, "fin") as g:
        YT, X = g.sb("YT", [D, GROUP]), g.sb("X", [TILE, TILES, D])
        r, xn = g.sb("r", [TILE, TILES, D]), g.sb("xn", [TILE, TILES, D])
        stats, mv, ve, rstd = g.sb("stats", [TILE, 4, 6]), g.sb("mv", [TILE, 4, 2]), g.sb("ve", [TILE, 4]), g.sb("rstd", [TILE, 4])
        ident, half = consts["ident"], consts["minus_half"]
        loaded, stored = g.sem("group_loaded"), g.sem("group_stored")
        T = Steps(g.sem("tensor_steps"), "y_ps")
        V = Steps(g.sem("vector_steps"), "y_res " + NORM_VEC)
        P = Steps(g.sem("gpsimd_steps"), "rstd")
        with nc.Block() as block:
            @block.sync
            def _(e):
                with e.Fori(0, GROUPS) as t:
                    e.dma_start(YT[:, :], yT_dram[:, bass.ds(t * GROUP, GROUP)]).then_inc(loaded, 16)
                    e.dma_start(X[:, :, :], tok_major(x_in, t)).then_inc(loaded, 16)
                    hold(e, V.sem, V.at(t, "normed3"))
                    e.dma_start(tok_major(out, t), xn[:, :, :]).then_inc(stored, 16)
                    hold(e, stored, (t + 1) * 16)
                    for X_ in (T, V, P):
                        hold(e, X_.sem, X_.turns(t + 1))

            @block.tensor
            def _(e):
                with e.Fori(0, GROUPS) as t:
                    e.wait_ge(loaded, (t + 1) * 32)
                    for s in range(TILES):
                        m = e.transpose(bank[0][0:TILE, s * D:(s + 1) * D], YT[:, s * TILE:(s + 1) * TILE], ident[:, :])
                    m.then_inc(T.sem, T.one("y_ps"))

            @block.vector
            def _(e):
                with e.Fori(0, GROUPS) as t:
                    e.wait_ge(loaded, (t + 1) * 32)
                    e.wait_ge(T.sem, T.at(t, "y_ps"))
                    e.tensor_tensor(r[:, :, :], bank[0][0:TILE, :].rearrange("p (s d) -> p s d", s=TILES), X[:, :, :], ALU.add).then_inc(V.sem, V.one("y_res"))
                    norm_vector(e, V, P, t, r, stats, mv, ve, rstd, xn, "y_res")

            @block.gpsimd
            def _(e):
                with e.Fori(0, GROUPS) as t:
                    e.wait_ge(V.sem, V.at(t, "vareps"))
                    e.tensor_tensor(rstd[:, :], ve[:, :], half[0:TILE, :], ALU.pow).then_inc(P.sem, P.one("rstd"))


def set_up(nc, consts, mask_dram, I):
    with Stage(nc, "set") as g:
        m8, mf, mb = g.sb("m8", [SEQS, KEYS // 4], mybir.dt.int32), g.sb("mf", [SEQS, KEYS]), g.sb("mb", [SEQS, KEYS], BF16)
        loaded, turned, stored = g.sem("loaded"), g.sem("mask_turned"), g.sem("mask_stored")
        with nc.Block() as block:
            @block.sync
            def _(e):
                load_all(e, loaded, [(m8[:, :], I["mask"]), (consts["ident"][:, :], I["ident"]),
                                     (consts["parity"][:, :], I["parity"]), (consts["sumq"][:, :, :], I["sumq"])])
                hold(e, turned, 3)
                e.dma_start(mask_dram, mb[:, :]).then_inc(stored, 16)
                hold(e, stored, 16)

            @block.vector
            def _(e):
                e.memset(consts["minus_half"][:, :], -0.5)
                e.wait_ge(loaded, 64)
                e.tensor_copy(consts["identb"][:, :], consts["ident"][:, :]).then_inc(turned, 1)
                e.tensor_copy(mf[:, :], m8[:, :].bitcast(U8)).then_inc(turned, 1)
                e.wait_ge(turned, 2)
                e.tensor_scalar(mb[:, :], mf[:, :], -1.0, PICKED, ALU.add, ALU.mult).then_inc(turned, 1)


def decoder(nc, I, out):
    with ExitStack() as ctx:
        bank = [ctx.enter_context(nc.psum_tensor(f"bank{i}", [128, 512], F32)) for i in range(8)]
        sb = lambda n, shape, dt=F32: ctx.enter_context(nc.sbuf_tensor(n, shape, dt))
        consts = {"ident": sb("ident_sb", [128, 128]), "identb": sb("identb_sb", [128, 128], BF16),
                  "parity": sb("parity_sb", [128, 2]), "sumq": sb("sumq_sb", [128, 2, 48]), "minus_half": sb("minus_half_sb", [128, 4])}
        dram = lambda n, shape, dt=F32: nc.dram_tensor(n, shape, dt, kind="Internal").ap()
        x = [dram(f"x_after{i}", (TOKENS, D)) for i in range(5)]
        qx = [dram(f"query_operands{i}", (SEQS, PAIRS, SROWS, 2 * SEQ), BF16) for i in range(2)]
        at = [dram(f"attended{i}", (D, TOKENS)) for i in range(2)]
        xT = [dram(f"xT{i}", (D, TOKENS)) for i in range(2)]
        yT = [dram(f"yT{i}", (D, TOKENS)) for i in range(2)]
        cT = [dram("expert_weights0", (E0 + SHARED // I0, TOKENS)), dram("expert_weights1", (E1, TOKENS))]
        mask, qkT, v, oT = dram("mask_rows", (SEQS, KEYS), BF16), dram("qkT", (D, 2, TOKENS)), dram("v1", (TOKENS, D)), dram("oT1", (D, TOKENS))
        set_up(nc, consts, mask, I)
        self_attention_0(nc, bank, I, x[0], qx[0], consts)
        cross_attention(nc, bank, "xa0", "L0_xattn_", qx[0], None, at[0], consts, I)
        project_and_route(nc, bank, "rt0", 0, at[0], x[0], x[1], xT[0], cT[0], consts, I)
        experts(nc, bank, "ex0", 0, xT[0], cT[0], yT[0], consts, I)
        norm_and_project_1(nc, bank, yT[0], x[1], x[2], qkT, v, consts, I)
        causal_attention(nc, bank, qkT, v, oT, consts, I)
        project_1(nc, bank, oT, x[2], x[3], qx[1], consts, I)
        cross_attention(nc, bank, "xa1", "L1_xattn_", qx[1], mask, at[1], consts, I)
        project_and_route(nc, bank, "rt1", 1, at[1], x[3], x[4], xT[1], cT[1], consts, I)
        experts(nc, bank, "ex1", 1, xT[1], cT[1], yT[1], consts, I)
        final_norm(nc, bank, yT[1], x[4], out, consts)


def shape_constants():
    f = np.float32
    pos = (np.arange(TILE) % SEQ).astype(f)
    inv = (f(1.0) / np.power(f(10000.0), np.arange(0, HD, 2, dtype=f) / f(HD))).astype(f)
    ang = pos[:, None] * inv[None, :]
    rows = np.arange(D)
    sumq = np.zeros((D, 2, 48), f)
    for p in range(D):
        r = p % 32
        if r < PR:
            sumq[p, r // HD, r] = 1
        else:
            sumq[p, (r - PR) // HD, 32 + r - PR] = 1
    bf = mybir.dt.np(BF16)
    return {
        "rope_cos": np.cos(ang).astype(f), "rope_sin": np.sin(ang).astype(f), "ident": np.eye(D, dtype=f),
        "parity": (rows[:, None] // HD % 2 == np.arange(2)[None]).astype(f), "sumq": sumq,
        "headmask": (rows[:, None] // HD == np.arange(HEADS)[None]).astype(f),
        "ones8": (rows[:, None] // HD == rows[None] // HD).astype(f),
        "causal": np.where(np.tril(np.ones((SEQ, SEQ), bool)), 0, -PICKED).astype(f),
        "query_rows": np.stack([np.zeros((PAIRS, 2 * SEQ)), np.ones((PAIRS, 2 * SEQ))]).astype(bf),
        "ones_rows": np.ones((SHARED // I0, TOKENS), f), "b2_or_zero0": np.zeros((E1, D), f),
    }


def kernel(**inputs):
    import concourse.bacc as bacc
    from concourse.bass_utils import run_bass_kernel_spmd

    a = {k: np.asarray(v) for k, v in inputs.items()}
    c = np.ascontiguousarray
    I = shape_constants()
    x = a["x"].reshape(TOKENS, D)
    I.update(x=c(x), xT=c(x.T), ctxT=c(a["ctx_1024"].transpose(0, 2, 1)), mask=c(a["mask_BxS2_bk0"]).view(np.int32))
    for n in ("L0_attn_Wq", "L0_attn_bq", "L0_attn_Wdown", "L0_attn_bdown", "L0_attn_Wup", "L0_attn_bup", "L0_attn_Wout",
              "L0_attn_bout", "L0_xattn_bq", "L0_xattn_bk", "L0_xattn_bv", "L0_xattn_bo", "L0_ffn_correction_bias",
              "L1_xattn_Wq", "L1_xattn_bq", "L1_xattn_bk", "L1_xattn_bv", "L1_xattn_bo"):
        I[n] = c(a[n])
    for n in ("L0_xattn_Wq", "L0_xattn_Wk", "L0_xattn_Wv", "L0_xattn_Wo", "L1_attn_Wq", "L1_attn_Wk", "L1_attn_Wv", "L1_attn_Wo"):
        I[n + "T"] = c(a[n].T)
    for n in ("Wk", "Wv", "Wo"):
        I[f"L1_xattn_{n}T"] = c(a[f"L1_xattn_{n}"])
    I["temperature_rows"] = np.repeat(a["L0_xattn_temperature"].reshape(HEADS), HD)
    I["q_scale_rows"], I["k_scale_rows"] = np.repeat(a["L1_attn_q_scale"], HD), np.repeat(a["L1_attn_k_scale"], HD)
    I["router0"], I["router1"] = c(a["L0_ffn_router_w"].T), c(a["L1_ffn_W_gate"])
    up = np.concatenate([a["L0_ffn_up_w"].transpose(1, 0, 2).reshape(D, E0 * I0), a["L0_ffn_shared_up_w"]], axis=1)
    I["up0"] = c(up.reshape(D, NCH0, 128).transpose(1, 0, 2))
    I["down0"] = np.concatenate([a["L0_ffn_down_w"].reshape(E0 * I0, D), a["L0_ffn_shared_down_w"]]).reshape(NCH0, 128, D)
    n = I1 // 128
    I["up1"] = c(a["L1_ffn_W1"].reshape(E1, D, n, 128).transpose(0, 2, 1, 3).reshape(NCH1, D, 128))
    I["down1"] = c(a["L1_ffn_W2"].reshape(NCH1, 128, D))
    I["b1"] = c(a["L1_ffn_b1"].reshape(NCH1, 128, 1))
    I["b2_or_zero1"] = c(a["L1_ffn_b2"])

    nc = bacc.Bacc("TRN2", target_bir_lowering=False, num_devices=1)
    arrays = {f"in_{k}": v for k, v in I.items()}
    aps = {k: nc.dram_tensor(f"in_{k}", v.shape, mybir.dt.from_np(v.dtype), kind="ExternalInput").ap() for k, v in I.items()}
    out = nc.dram_tensor("out_0", (TOKENS, D), F32, kind="ExternalOutput").ap()
    decoder(nc, aps, out)
    r = run_bass_kernel_spmd(nc, [arrays], core_ids=[0])
    return r.results[0]["out_0"].reshape(SEQS, SEQ, D)
```

```python
from contextlib import ExitStack

import numpy as np

import concourse.bass as bass
from concourse import mybir

F32 = mybir.dt.float32
BF16 = mybir.dt.bfloat16
U8 = mybir.dt.uint8
ACT = mybir.ActivationFunctionType
ALU = mybir.AluOpType
AX = mybir.AxisListType.X

SEQS, SEQ, D = 32, 56, 128
HEADS, HD = 16, 8
KEYS = 1500
TOKENS = SEQS * SEQ
TILE = 2 * SEQ
TILES = 4
GROUP = TILE * TILES
GROUPS = TOKENS // GROUP
GSEQS = GROUP // SEQ
PAIRS = HEADS // 2
PR = 2 * HD
CH = 125
CHUNKS = KEYS // CH
KB = 500
KBANKS = KEYS // KB
CB = CHUNKS // KBANKS
PROD = 6
SROWS = PR * PROD
SHIFT_ROW, MASK_ROW = SROWS, SROWS + 1
STACK = SROWS + 2
E0, I0, K0, G0 = 64, 64, 8, 8
SHARED = 256
NCH0 = (E0 * I0 + SHARED) // 128
E1, I1 = 8, 512
NCH1 = E1 * I1 // 128
EPS = 1e-5
PICKED = 1e30
ABSENT = -3e38


class Steps:

    def __init__(self, sem, names):
        self.sem, self.names, self.k = sem, names.split(), 0
        assert len(set(self.names)) == len(self.names)
        self.per = len(self.names)

    def at(self, t, name):
        return t * self.per + (self.names.index(name) + 1)

    def one(self, name):
        assert self.names[self.k % self.per] == name, (self.names[self.k % self.per], name)
        self.k += 1
        return 1

    def turns(self, t):
        return t * self.per


def bc(ap, n, axis):
    shape = list(ap.shape)
    shape.insert(axis, n)
    return ap.unsqueeze(axis).broadcast_to(shape)


class Stage:

    def __init__(self, nc, name):
        self.nc, self.name, self.ctx = nc, name, ExitStack()

    def sb(self, name, shape, dt=F32):
        return self.ctx.enter_context(self.nc.sbuf_tensor(f"{self.name}_{name}", shape, dt))

    def sem(self, name):
        return self.ctx.enter_context(self.nc.semaphore(f"{self.name}_{name}"))

    def __enter__(self):
        return self

    def __exit__(self, *a):
        self.ctx.close()


def hold(e, sem, value):
    e.wait_ge(sem, value)
    e.nop(nofuse=True)


def tok_major(dram, t):
    return dram[bass.ds(t * GROUP, GROUP), :].rearrange("(s p) d -> p s d", p=TILE)


NORM_VEC = "stats0 stats1 stats2 stats3 aggr0 aggr1 aggr2 aggr3 vareps normed0 normed1 normed2 normed3"


def norm_vector(v, V, P, t, r, stats, mv, ve, rstd, out, before, x_stored):
    v.wait_ge(V.sem, V.at(t, before))
    for s in range(TILES):
        v.bn_stats(stats[:, s, :], r[:, s, :]).then_inc(V.sem, V.one(f"stats{s}"))
    hold(v, V.sem, V.at(t, "stats3"))
    for s in range(TILES):
        v.bn_aggr(mv[:, s, :], stats[:, s, :]).then_inc(V.sem, V.one(f"aggr{s}"))
    v.wait_ge(V.sem, V.at(t, "aggr3"))
    v.tensor_scalar(ve[:, :], mv[:, :, 1], EPS, None, ALU.add).then_inc(V.sem, V.one("vareps"))
    v.wait_ge(P.sem, P.at(t, "rstd"))
    v.wait_ge(x_stored, 16 + t * 16)
    for s in range(TILES):
        v.tensor_scalar(out[:, s, :], r[:, s, :], mv[:, s, 0:1], rstd[:, s:s + 1], ALU.subtract,
                        ALU.mult).then_inc(V.sem, V.one(f"normed{s}"))


QUERY_STORES = 16 * 2 * GSEQS
QPREP_POOL = "q_h q_rest q_m q_l x_h x_m x_l x_h2"


def qprep_pool(p, P, S, t, qT, qh, qr, qm, ql, qx, parity, q_stored):
    hold(p, S.sem, S.at(t, "qT"))
    p.tensor_copy(qh[:, :], qT[:, :]).then_inc(P.sem, P.one("q_h"))
    hold(p, P.sem, P.at(t, "q_h"))
    p.tensor_tensor(qr[:, :], qT[:, :], qh[:, :], ALU.subtract).then_inc(P.sem, P.one("q_rest"))
    hold(p, P.sem, P.at(t, "q_rest"))
    p.tensor_copy(qm[:, :], qr[:, :]).then_inc(P.sem, P.one("q_m"))
    hold(p, P.sem, P.at(t, "q_m"))
    p.tensor_tensor(ql[:, :], qr[:, :], qm[:, :], ALU.subtract).then_inc(P.sem, P.one("q_l"))
    hold(p, P.sem, P.at(t, "q_l"))
    hold(p, q_stored, 16 + t * QUERY_STORES)
    for part, c, n, name in ((qh, 0, 2, "x_h"), (qm, 2, 2, "x_m"), (ql, 4, 1, "x_l"), (qh, 5, 1, "x_h2")):
        for k in range(n):
            last = p.tensor_tensor(qx[:, :, c + k, :, :].rearrange("p b h q -> p h b q"),
                                   bc(part[:, :].rearrange("p (b q) -> p b q", q=SEQ), 2, 1),
                                   bc(bc(parity[:, :], GSEQS, 2), SEQ, 3), ALU.mult)
        last.then_inc(P.sem, P.one(name))


def store_queries(e, stored, t, qx_dram, qx):
    for b in range(GSEQS):
        for a in range(2):
            e.dma_start(qx_dram[t * GSEQS + b].rearrange("j (a r c) n -> a j r (c n)", a=2, r=PR)[a],
                        qx[:, b, 3 * a:3 * a + 3, :, :].rearrange("p c h q -> p (c h q)")).then_inc(stored, 16)


def load_all(e, sem, pairs):
    for dst, src in pairs:
        e.dma_start(dst, src).then_inc(sem, 16)
    return 16 * len(pairs)


def rows_of(vec, n=TILE):
    return vec.rearrange("(a d) -> a d", a=1).broadcast_to([n, vec.shape[0]])


def column(vec):
    return vec.rearrange("(d a) -> d a", a=1)


def self_attention_0(nc, bank, I, x1, qx_dram, consts):
    with Stage(nc, "sa0") as g:
        X, XT = g.sb("X", [TILE, TILES, D]), g.sb("XT", [D, GROUP])
        wq, wdn, wup, wout = g.sb("wq", [D, D]), g.sb("wdn", [D, 32]), g.sb("wup", [32, 2 * D]), g.sb("wout", [D, D])
        bq, bup, bout = g.sb("bq", [TILE, D]), g.sb("bup", [TILE, 2 * D]), g.sb("bout", [TILE, D])
        bdn, wq1 = g.sb("bdn", [32, 1]), g.sb("wq1", [D, D])
        cos, sin = g.sb("cos", [TILE, 4]), g.sb("sin", [TILE, 4])
        qb1, temp, qs, qbs = g.sb("qb1", [D, 1]), g.sb("temp", [D, 1]), g.sb("qs", [D, 1]), g.sb("qbs", [D, 1])
        parity, ident = consts["parity"], consts["ident"]
        lat, q, kv = g.sb("lat", [32, GROUP]), g.sb("q", [TILE, TILES, D]), g.sb("kv", [TILE, TILES, 2 * D])
        qr, kr = g.sb("qr", [TILE, TILES, D]), g.sb("kr", [TILE, TILES, D])
        ta, tb = g.sb("ta", [TILE, 64, 4]), g.sb("tb", [TILE, 64, 4])
        prod = g.sb("prod", [TILE, TILES, 2048])
        S = g.sb("S", [TILE, TILES, 256])
        mx, den = g.sb("mx", [TILE, 64]), g.sb("den", [TILE, 64])
        o, oT, r, xn = g.sb("o", [TILE, TILES, D]), g.sb("oT", [D, GROUP]), g.sb("r", [TILE, TILES, D]), g.sb("xn", [TILE, TILES, D])
        stats, mv, ve, rstd = g.sb("stats", [TILE, 4, 6]), g.sb("mv", [TILE, 4, 2]), g.sb("ve", [TILE, 4]), g.sb("rstd", [TILE, 4])
        xT1, qT = g.sb("xT1", [D, GROUP]), g.sb("qT", [D, GROUP])
        qh, qm, ql, qrest = g.sb("qh", [D, GROUP], BF16), g.sb("qm", [D, GROUP], BF16), g.sb("ql", [D, GROUP], BF16), g.sb("qrest", [D, GROUP])
        qx = g.sb("qx", [D, GSEQS, PROD, 2, SEQ], BF16)
        half = consts["minus_half"]
        weights, loaded = g.sem("weights_loaded"), g.sem("group_loaded")
        x_stored, q_stored = g.sem("weight_loaded_x_stored"), g.sem("weight_loaded_queries_stored")
        consts_ready = g.sem("query_scale_ready")
        T = Steps(g.sem("tensor_steps"), "q_ps lat_ps kv_ps oT_ps y_ps xT_ps qT_ps")
        A = Steps(g.sem("scalar_steps"), "lat exp oT xT qT")
        V = Steps(g.sem("vector_steps"), "q kv_a kv_b q1c q2s q1 q2c q1s q2 k1c k2s k1 k2c k1s k2 prod0 prod1 "
                  "S0 S1 S2 S3 max shifted sum inv P vprod0 vprod1 o0 o1 o2 o3 y_bias y_res " + NORM_VEC)
        P = Steps(g.sem("gpsimd_steps"), "prod2 prod3 vprod2 vprod3 rstd " + QPREP_POOL)
        nw = [0]
        with nc.Block() as block:
            @block.sync
            def _(e):
                nw[0] = load_all(e, weights, [
                    (wq[:, :], I["L0_attn_Wq"]), (wdn[:, :], I["L0_attn_Wdown"]), (wup[:, :], I["L0_attn_Wup"]),
                    (bq[:, :], rows_of(I["L0_attn_bq"])),
                    (bup[:, :], rows_of(I["L0_attn_bup"])), (bout[:, :], rows_of(I["L0_attn_bout"])),
                    (bdn[:, :], column(I["L0_attn_bdown"])),
                    (cos[:, :], I["rope_cos"]), (sin[:, :], I["rope_sin"]), (qb1[:, :], column(I["L0_xattn_bq"])),
                    (temp[:, :], column(I["temperature_rows"]))])
                load_all(e, x_stored, [(wout[:, :], I["L0_attn_Wout"])])
                load_all(e, q_stored, [(wq1[:, :], I["L0_xattn_WqT"])])

                def load(t):
                    e.dma_start(X[:, :, :], tok_major(I["x"], t)).then_inc(loaded, 16)
                    e.dma_start(XT[:, :], I["xT"][:, bass.ds(t * GROUP, GROUP)]).then_inc(loaded, 16)

                def store(t):
                    e.dma_start(tok_major(x1, t), xn[:, :, :]).then_inc(x_stored, 16)
                    hold(e, P.sem, P.at(t, "x_h2"))
                    store_queries(e, q_stored, t, qx_dram, qx)

                load(0)
                with e.Fori(0, GROUPS - 1) as t:
                    hold(e, V.sem, V.at(t, "normed3"))
                    load(t + 1)
                    store(t)
                hold(e, V.sem, V.at(GROUPS - 1, "normed3"))
                store(GROUPS - 1)
                hold(e, x_stored, 16 * (1 + GROUPS))
                hold(e, q_stored, 16 + GROUPS * QUERY_STORES)

            @block.tensor
            def _(e):
                e.wait_ge(weights, nw[0])
                for sem in (x_stored, q_stored):
                    e.wait_ge(sem, 16)
                with e.Fori(0, GROUPS) as t:
                    e.wait_ge(loaded, (t + 1) * 32)
                    for s in range(TILES):
                        m = e.matmul(bank[0][0:TILE, s * D:(s + 1) * D], XT[:, s * TILE:(s + 1) * TILE], wq[:, :], start=True, stop=True)
                    m.then_inc(T.sem, T.one("q_ps"))
                    e.matmul(bank[1][0:32, 0:GROUP], wdn[:, :], XT[:, :], start=True, stop=True).then_inc(T.sem, T.one("lat_ps"))
                    e.wait_ge(A.sem, A.at(t, "lat"))
                    for s in range(TILES):
                        m = e.matmul(bank[2 + s // 2][0:TILE, s % 2 * 256:s % 2 * 256 + 256], lat[:, s * TILE:(s + 1) * TILE], wup[:, :], start=True, stop=True)
                    m.then_inc(T.sem, T.one("kv_ps"))
                    e.wait_ge(V.sem, V.at(t, "o3"))
                    for s in range(TILES):
                        m = e.transpose(bank[4][:, s * TILE:(s + 1) * TILE], o[:, s, :], ident[0:TILE, 0:TILE])
                    m.then_inc(T.sem, T.one("oT_ps"))
                    e.wait_ge(A.sem, A.at(t, "oT"))
                    for s in range(TILES):
                        m = e.matmul(bank[5][0:TILE, s * D:(s + 1) * D], oT[:, s * TILE:(s + 1) * TILE], wout[:, :], start=True, stop=True)
                    m.then_inc(T.sem, T.one("y_ps"))
                    e.wait_ge(V.sem, V.at(t, "normed3"))
                    for s in range(TILES):
                        m = e.transpose(bank[6][:, s * TILE:(s + 1) * TILE], xn[:, s, :], ident[0:TILE, 0:TILE])
                    m.then_inc(T.sem, T.one("xT_ps"))
                    e.wait_ge(A.sem, A.at(t, "xT"))
                    e.matmul(bank[7][:, 0:GROUP], wq1[:, :], xT1[:, :], start=True, stop=True).then_inc(T.sem, T.one("qT_ps"))

            @block.scalar
            def _(e):
                e.wait_ge(weights, nw[0])
                e.wait_ge(consts_ready, 3)
                with e.Fori(0, GROUPS) as t:
                    e.wait_ge(loaded, (t + 1) * 32)
                    e.wait_ge(T.sem, T.at(t, "lat_ps"))
                    e.activation(lat[:, :], bank[1][0:32, 0:GROUP], ACT.Identity, bias=bdn[:, :]).then_inc(A.sem, A.one("lat"))
                    e.wait_ge(V.sem, V.at(t, "shifted"))
                    e.activation(S[:, :, :], S[:, :, :], ACT.Exp, scale=HD ** -0.5).then_inc(A.sem, A.one("exp"))
                    e.wait_ge(T.sem, T.at(t, "oT_ps"))
                    e.copy(oT[:, :], bank[4][:, 0:GROUP]).then_inc(A.sem, A.one("oT"))
                    e.wait_ge(T.sem, T.at(t, "xT_ps"))
                    e.copy(xT1[:, :], bank[6][:, 0:GROUP]).then_inc(A.sem, A.one("xT"))
                    e.wait_ge(T.sem, T.at(t, "qT_ps"))
                    e.activation(qT[:, :], bank[7][:, 0:GROUP], ACT.Identity, bias=qbs[:, :], scale=qs[:, :]).then_inc(A.sem, A.one("qT"))

            def head_view(x, s):
                return x[:, s, :].rearrange("p (h d) -> p h d", d=HD)

            def score_product(e, s):
                return e.tensor_tensor(prod[:, s, :].rearrange("p (h g d) -> p h g d", h=HEADS, g=HEADS),
                                       bc(head_view(qr, s), HEADS, 2), bc(head_view(kr, s), HEADS, 1), ALU.mult)

            def value_product(e, s):
                v = kv[:, s, :].rearrange("p (g d) -> p d g", d=2 * HD)[:, HD:2 * HD, :]
                return e.tensor_tensor(prod[:, s, :].rearrange("p (h d g) -> p h d g", h=HEADS, d=HD),
                                       bc(S[:, s, :].rearrange("p (h g) -> p h g", g=HEADS), HD, 2), bc(v, HEADS, 1), ALU.mult)

            @block.vector
            def _(e):
                e.wait_ge(weights, nw[0])
                e.reciprocal(temp[:, :], temp[:, :]).then_inc(consts_ready, 1)
                e.wait_ge(consts_ready, 1)
                e.tensor_scalar(qs[:, :], temp[:, :], HD ** -0.5, None, ALU.mult).then_inc(consts_ready, 1)
                e.wait_ge(consts_ready, 2)
                e.tensor_tensor(qbs[:, :], qb1[:, :], qs[:, :], ALU.mult).then_inc(consts_ready, 1)
                with e.Fori(0, GROUPS) as t:
                    e.wait_ge(loaded, (t + 1) * 32)
                    e.wait_ge(T.sem, T.at(t, "q_ps"))
                    ps4 = lambda b: bank[b][0:TILE, :].rearrange("p (s d) -> p s d", s=TILES)
                    e.tensor_tensor(q[:, :, :], ps4(0), bc(bq[:, :], TILES, 1), ALU.add).then_inc(V.sem, V.one("q"))
                    e.wait_ge(T.sem, T.at(t, "kv_ps"))
                    for i, n in enumerate(("kv_a", "kv_b")):
                        e.tensor_tensor(kv[:, 2 * i:2 * i + 2, :], bank[2 + i][0:TILE, :].rearrange("p (s d) -> p s d", s=2),
                                        bc(bup[:, :], 2, 1), ALU.add).then_inc(V.sem, V.one(n))
                    qv = q[:, :, :].rearrange("p s (h d) -> p (s h) d", d=HD)
                    kk = kv[:, :, :].rearrange("p s (h d) -> p (s h) d", d=2 * HD)
                    for x, y, n, before in ((qv, qr, "q", "q"), (kk, kr, "k", "kv_b")):
                        yv = y[:, :, :].rearrange("p s (h d) -> p (s h) d", d=HD)
                        c, s_ = bc(cos[:, :], 64, 1), bc(sin[:, :], 64, 1)
                        e.wait_ge(V.sem, V.at(t, before))
                        for a, b, half_, op in ((c, s_, 0, ALU.subtract), (s_, c, 1, ALU.add)):
                            na, nb = (f"{n}1c", f"{n}2s") if half_ == 0 else (f"{n}2c", f"{n}1s")
                            first, second = (x[:, :, 0:4], x[:, :, 4:8]) if half_ == 0 else (x[:, :, 4:8], x[:, :, 0:4])
                            if half_ or n == "k":
                                e.wait_ge(V.sem, V.at(t, f"{n}1" if half_ else "q2"))
                            e.tensor_tensor(ta[:, :, :], first, c, ALU.mult).then_inc(V.sem, V.one(na))
                            e.tensor_tensor(tb[:, :, :], second, s_, ALU.mult).then_inc(V.sem, V.one(nb))
                            e.wait_ge(V.sem, V.at(t, nb))
                            e.tensor_tensor(yv[:, :, 4 * half_:4 * half_ + 4], ta[:, :, :], tb[:, :, :], op).then_inc(V.sem, V.one(f"{n}{half_ + 1}"))
                    e.wait_ge(V.sem, V.at(t, "k2"))
                    for s in range(2):
                        score_product(e, s).then_inc(V.sem, V.one(f"prod{s}"))
                    for s in range(TILES):
                        if s < 2:
                            e.wait_ge(V.sem, V.at(t, f"prod{s}"))
                        else:
                            e.wait_ge(P.sem, P.at(t, f"prod{s}"))
                        e.tensor_reduce(S[:, s, :], prod[:, s, :].rearrange("p (a d) -> p a d", d=HD), AX, ALU.add).then_inc(V.sem, V.one(f"S{s}"))
                    e.wait_ge(V.sem, V.at(t, "S3"))
                    Sv = S[:, :, :].rearrange("p s (h g) -> p (s h) g", g=HEADS)
                    e.tensor_reduce(mx[:, :], Sv, AX, ALU.max).then_inc(V.sem, V.one("max"))
                    e.wait_ge(V.sem, V.at(t, "max"))
                    e.tensor_tensor(Sv, Sv, bc(mx[:, :], HEADS, 2), ALU.subtract).then_inc(V.sem, V.one("shifted"))
                    e.wait_ge(A.sem, A.at(t, "exp"))
                    e.tensor_reduce(den[:, :], Sv, AX, ALU.add).then_inc(V.sem, V.one("sum"))
                    e.wait_ge(V.sem, V.at(t, "sum"))
                    e.reciprocal(den[:, :], den[:, :]).then_inc(V.sem, V.one("inv"))
                    e.wait_ge(V.sem, V.at(t, "inv"))
                    e.tensor_tensor(Sv, Sv, bc(den[:, :], HEADS, 2), ALU.mult).then_inc(V.sem, V.one("P"))
                    e.wait_ge(V.sem, V.at(t, "P"))
                    for s in range(2):
                        value_product(e, s).then_inc(V.sem, V.one(f"vprod{s}"))
                    for s in range(TILES):
                        if s < 2:
                            e.wait_ge(V.sem, V.at(t, f"vprod{s}"))
                        else:
                            e.wait_ge(P.sem, P.at(t, f"vprod{s}"))
                        e.tensor_reduce(o[:, s, :], prod[:, s, :].rearrange("p (a g) -> p a g", g=HEADS), AX, ALU.add).then_inc(V.sem, V.one(f"o{s}"))
                    e.wait_ge(T.sem, T.at(t, "y_ps"))
                    e.tensor_tensor(r[:, :, :], ps4(5), bc(bout[:, :], TILES, 1), ALU.add).then_inc(V.sem, V.one("y_bias"))
                    e.wait_ge(V.sem, V.at(t, "y_bias"))
                    e.tensor_tensor(r[:, :, :], r[:, :, :], X[:, :, :], ALU.add).then_inc(V.sem, V.one("y_res"))
                    norm_vector(e, V, P, t, r, stats, mv, ve, rstd, xn, "y_res", x_stored)

            @block.gpsimd
            def _(e):
                with e.Fori(0, GROUPS) as t:
                    e.wait_ge(V.sem, V.at(t, "k2"))
                    for s in (2, 3):
                        score_product(e, s).then_inc(P.sem, P.one(f"prod{s}"))
                    e.wait_ge(V.sem, V.at(t, "P"))
                    for s in (2, 3):
                        value_product(e, s).then_inc(P.sem, P.one(f"vprod{s}"))
                    e.wait_ge(V.sem, V.at(t, "vareps"))
                    e.tensor_tensor(rstd[:, :], ve[:, :], half[0:TILE, :], ALU.pow).then_inc(P.sem, P.one("rstd"))
                    qprep_pool(e, P, A, t, qT, qh, qrest, qm, ql, qx, parity, q_stored)


def cross_attention(nc, bank, name, W, qx_dram, mask_rows, at_dram, den_dram, consts, I):
    UT = 2 * PAIRS
    TURNS = SEQS // 2
    LAG = 2
    SUM_AT, K_AT, V_AT = 1, (2, 3, 4), (5, 6, 7)
    SCORES, PV, MISC = 3, 6, 7
    Q = 2 * SEQ
    SHIFT = KBANKS - 1
    with Stage(nc, name) as g:
        wk, wv, bk = g.sb("wk", [D, D]), g.sb("wv", [D, D]), g.sb("bk", [D, 1])
        ctx = [g.sb(f"ctx{i}", [D, KEYS]) for i in range(2)]
        kf, krest = g.sb("kf", [D, KEYS]), g.sb("krest", [D, KB])
        kp = [g.sb(f"kparts{i}", [D, 4, KEYS], BF16) for i in range(2)]
        ks = [g.sb(f"kstack{i}", [STACK, PAIRS, KEYS], BF16) for i in range(2)]
        qs = [g.sb(f"qstack{i}", [STACK, PAIRS, Q], BF16) for i in range(2)]
        vs = [g.sb(f"v{i}", [CH, CHUNKS, PAIRS, 2 * PR]) for i in range(2)]
        pt = [g.sb(f"probs{i}", [CH, CB, Q]) for i in range(KBANKS)]
        mx3 = [g.sb(f"mx3_{i}", [Q, KBANKS]) for i in range(2)]
        nmx = [g.sb(f"nmx{i}", [Q, 1], BF16) for i in range(2)]
        pv = [g.sb(f"pv{i}", [D, PAIRS, 2, SEQ]) for i in range(2)]
        att = g.sb("att", [48, PAIRS * SEQ])
        identb, sumq = consts["identb"], consts["sumq"]
        S = {n: g.sem(n) for n in (
            "weights_loaded", "rows_loaded", "ones_set", "ctx_loaded0", "ctx_loaded1", "k_ps", "k_f32", "k_rounded", "v_ps",
            "v_copied", "q_loaded0", "q_loaded1", "max_ps", "bank_max", "unit_max", "shift_ps", "shift_row",
            "score_ps", "probs", "pv_ps", "pv_copied", "sum_ps", "summed", "bias_loaded_sums_stored")}
        k_stacked = [[g.sem(f"k_stacked{i}_half{j}") for j in range(2)] for i in range(2)]
        P = Steps(g.sem("split_steps"), " ".join(f"rest{n} m{n} l{n} hh{n}" for n in range(KBANKS)))
        KDMA = 16 * PAIRS
        QDMA = 48 if mask_rows is not None else 32

        def turns(e, slot):
            for w in range(UT):
                slot(e, 0, w, True, False)
            with e.Fori(1, TURNS - 1) as i:
                for w in range(UT):
                    slot(e, i, w, False, False)
            for w in range(UT):
                slot(e, TURNS - 1, w, False, True)

        def keys_matmul(e, b, n):
            e.matmul(bank[MISC][:, 0:KB], wk[:, :], ctx[b][:, n * KB:(n + 1) * KB],
                     start=True, stop=True).then_inc(S["k_ps"], 1)

        def values_matmul(e, b, n):
            for c in range(CB):
                lo = (n * CB + c) * CH
                m = e.matmul(bank[MISC][0:CH, c * D:(c + 1) * D], ctx[b][:, lo:lo + CH], wv[:, :], start=True, stop=True)
            m.then_inc(S["v_ps"], 1)

        def scores_matmul(e, u, b, j, k, first_unit):
            if k == 0:
                e.wait_ge(S["shift_row"], u + 1)
            if not first_unit:
                e.wait_ge(S["probs"], (u - 1) * KBANKS + k + 1)
            for c in range(CB):
                lo = (k * CB + c) * CH
                m = e.matmul(bank[SCORES + k][0:CH, c * Q:(c + 1) * Q], ks[b][:, j, lo:lo + CH], qs[b][:, j, :],
                             start=True, stop=True)
            m.then_inc(S["score_ps"], 1)

        def pv_matmul(e, u, b, j, k, first_unit):
            e.wait_ge(S["probs"], u * KBANKS + k + 1)
            if k == 0 and not first_unit:
                e.wait_ge(S["pv_copied"], u)
            for c in range(CB):
                m = e.matmul(bank[PV][32 * c:32 * c + 2 * PR, 0:Q], vs[b][:, k * CB + c, j, :], pt[k][:, c, :],
                             start=(k == 0), stop=(k == KBANKS - 1))
            m.then_inc(S["pv_ps"], 1)

        def shift_matmul(e, u, j):
            e.wait_ge(S["unit_max"], u + 1)
            e.matmul(bank[SHIFT][SHIFT_ROW:SHIFT_ROW + 1, 0:Q], nmx[j % 2][:, :], identb[0:Q, 0:Q],
                     start=True, stop=True).then_inc(S["shift_ps"], 1)

        def sum_matmul(e, b):
            for hh in range(2):
                m = e.matmul(bank[MISC][0:48, 0:PAIRS * SEQ], sumq[:, hh, :], pv[b][:, :, hh, :],
                             start=(hh == 0), stop=(hh == 1))
            m.then_inc(S["sum_ps"], 1)

        def tensor_slot(e, i, w, first, last):
            b, j = w // PAIRS, w % PAIRS
            seq, u = i * 2 + b, i * UT + w
            lb, lj, lu = (w - LAG) % UT // PAIRS, (w - LAG) % PAIRS, u - LAG
            pb, pj, pu = (w - LAG - 1) % UT // PAIRS, (w - LAG - 1) % PAIRS, lu - 1
            more = not (last and b == 1)
            for k in range(KBANKS):
                if k == 0:
                    if j % (PAIRS // 2) == 0:
                        e.wait_ge(k_stacked[b][j // (PAIRS // 2)], (i + 1) * KDMA)
                    if j == 0:
                        e.wait_ge(S[f"q_loaded{b}"], (i + 1) * QDMA)
                if not (first and w == 0):
                    e.wait_ge(S["bank_max"], (u - 1) * KBANKS + k + 1)
                    if k == SHIFT:
                        e.wait_ge(S["shift_row"], u)
                e.matmul(bank[k][0:Q, 0:KB], qs[b][:, j, :], ks[b][:, j, k * KB:(k + 1) * KB],
                         start=True, stop=True).then_inc(S["max_ps"], 1)
                if not (first and w < LAG):
                    scores_matmul(e, lu, lb, lj, k, first and w == LAG)
                if k < 2 and not (first and w < LAG + 1):
                    pv_matmul(e, pu, pb, pj, k + 1, first and w == LAG + 1)
                if k == 0 and not (first and w == 0):
                    shift_matmul(e, u - 1, (j - 1) % 2)
            if not (first and w == 0):
                spare_read(e, seq, b, j, first, last)
            if j in K_AT and not last:
                if j == K_AT[0]:
                    e.wait_ge(S[f"ctx_loaded{b}"], (i + 2) * 16)
                keys_matmul(e, b, K_AT.index(j))
            if j in V_AT and more:
                values_matmul(e, 1 - b, V_AT.index(j))
            if j == SUM_AT and not first:
                e.wait_ge(S["pv_copied"], (seq - 1) * PAIRS)
                sum_matmul(e, b)
            if not (first and w < LAG):
                if lj == 0:
                    e.wait_ge(S["v_copied"], (seq + 1) * KBANKS)
                pv_matmul(e, lu, lb, lj, 0, first and w == LAG)

        def spare_read(e, seq, b, j, first, last):
            if j - 1 == SUM_AT and not first:
                e.wait_ge(S["summed"], seq - 1)
            if j - 1 in K_AT and not last:
                e.wait_ge(S["k_f32"], (seq + 2) * KBANKS + K_AT.index(j - 1) + 1)
            if j - 1 in V_AT and not (last and b == 1):
                e.wait_ge(S["v_copied"], (seq + 1) * KBANKS + V_AT.index(j - 1) + 1)
            if j == 0:
                e.wait_ge(S["v_copied"], (seq + 1) * KBANKS)

        def key_copy(e, seq, n):
            e.wait_ge(S["k_ps"], seq * KBANKS + n + 1)
            if not (isinstance(seq, int) and seq == 0):
                e.wait_ge(P.sem, P.at(seq - 1, f"hh{n}"))
            e.activation(kf[:, n * KB:(n + 1) * KB], bank[MISC][:, 0:KB], ACT.Identity, bias=bk[:, :]).then_inc(S["k_f32"], 1)


        def value_copy(e, seq, b, n):
            e.wait_ge(S["v_ps"], seq * KBANKS + n + 1)
            e.copy(vs[b][:, n * CB:(n + 1) * CB, :, 0:PR],
                   bank[MISC][0:CH, :].rearrange("p (c j r) -> p c j r", c=CB, r=PR)).then_inc(S["v_copied"], 1)

        def exp_bank(e, u, k, first_unit):
            e.wait_ge(S["score_ps"], u * KBANKS + k + 1)
            if not first_unit:
                e.wait_ge(S["pv_ps"], (u - 1) * KBANKS + k + 1)
            e.activation(pt[k][:, :, :], bank[SCORES + k][0:CH, 0:CB * Q].rearrange("p (c q) -> p c q", c=CB),
                         ACT.Exp).then_inc(S["probs"], 1)

        def pv_copy(e, u, b, j):
            e.wait_ge(S["pv_ps"], (u + 1) * KBANKS)
            e.copy(pv[b][:, j, :, :], bank[PV][:, 0:Q].rearrange("p (h q) -> p h q", h=2)).then_inc(S["pv_copied"], 1)

        def sum_copy(e, seq):
            e.wait_ge(S["sum_ps"], seq + 1)
            e.wait_ge(S["bias_loaded_sums_stored"], 16 + seq * 32)
            e.copy(att[:, :], bank[MISC][0:48, 0:PAIRS * SEQ]).then_inc(S["summed"], 1)

        def scalar_slot(e, i, w, first, last):
            b, j = w // PAIRS, w % PAIRS
            seq, u = i * 2 + b, i * UT + w
            pb, pj, pu = (w - LAG - 1) % UT // PAIRS, (w - LAG - 1) % PAIRS, u - LAG - 1
            more = not (last and b == 1)
            for k in range(KBANKS):
                if not (first and w < LAG):
                    exp_bank(e, u - LAG, k, first and w == LAG)
                if k == 0:
                    if j == 0 and not (first and b == 0):
                        value_copy(e, seq, b, KBANKS - 1)
                    if j - 1 == SUM_AT and not first:
                        sum_copy(e, seq - 2)
                    if j - 1 in K_AT and not last:
                        key_copy(e, seq + 2, K_AT.index(j - 1))
                    if j - 1 in V_AT and more:
                        value_copy(e, seq + 1, 1 - b, V_AT.index(j - 1))
                if k == 1 and not (first and w < LAG + 1):
                    if pj == 0 and not first:
                        e.wait_ge(S["sum_ps"], seq - 1)
                    pv_copy(e, pu, pb, pj)

        def key_round(e, seq, b, n, turn):
            e.wait_ge(S["k_f32"], seq * KBANKS + n + 1)
            if turn is not None and n == 0:
                for half in range(2):
                    e.wait_ge(k_stacked[b][half], (turn + 1) * KDMA)
            e.tensor_copy(kp[b][:, 0, n * KB:(n + 1) * KB], kf[:, n * KB:(n + 1) * KB]).then_inc(S["k_rounded"], 1)

        def shift_copy(e, u, b, j):
            e.wait_ge(S["shift_ps"], u + 1)
            e.tensor_copy(qs[b][SHIFT_ROW:SHIFT_ROW + 1, j, :], bank[SHIFT][SHIFT_ROW:SHIFT_ROW + 1, 0:Q]).then_inc(S["shift_row"], 1)

        def vector_slot(e, i, w, first, last):
            b, j = w // PAIRS, w % PAIRS
            seq, u = i * 2 + b, i * UT + w
            for k in range(KBANKS):
                e.wait_ge(S["max_ps"], u * KBANKS + k + 1)
                e.tensor_reduce(mx3[w % 2][:, k:k + 1], bank[k][0:Q, 0:KB], AX, ALU.max).then_inc(S["bank_max"], 1)
                if k == 0 and not (first and w == 0):
                    shift_copy(e, u - 1, (w - 1) % UT // PAIRS, (w - 1) % PAIRS)
                if k == 1 and j - 1 in K_AT and not last:
                    key_round(e, seq + 2, b, K_AT.index(j - 1), i)
            e.wait_ge(S["bank_max"], (u + 1) * KBANKS)
            e.tensor_reduce(nmx[w % 2][:, :], mx3[w % 2][:, :], AX, ALU.max, negate=True).then_inc(S["unit_max"], 1)

        def split_keys(e, seq, b):
            for n in range(KBANKS):
                cols = slice(n * KB, (n + 1) * KB)
                hold(e, S["k_rounded"], seq * KBANKS + n + 1)
                e.tensor_tensor(krest[:, :], kf[:, cols], kp[b][:, 0, cols], ALU.subtract).then_inc(P.sem, P.one(f"rest{n}"))
                hold(e, P.sem, P.at(seq, f"rest{n}"))
                e.tensor_copy(kp[b][:, 1, cols], krest[:, :]).then_inc(P.sem, P.one(f"m{n}"))
                hold(e, P.sem, P.at(seq, f"m{n}"))
                e.tensor_tensor(kp[b][:, 3, cols], krest[:, :], kp[b][:, 1, cols], ALU.subtract).then_inc(P.sem, P.one(f"l{n}"))
                e.tensor_copy(kp[b][:, 2, cols], kp[b][:, 0, cols]).then_inc(P.sem, P.one(f"hh{n}"))
                hold(e, P.sem, P.at(seq, f"hh{n}"))

        def gpsimd_slot(e, i, w, first, last):
            b, j = w // PAIRS, w % PAIRS
            if j == 0 and not last:
                split_keys(e, i * 2 + b + 2, b)

        def load_queries(e, seq, b):
            e.dma_start(qs[b][0:SROWS, :, :], qx_dram[seq].rearrange("j r n -> r j n")).then_inc(S[f"q_loaded{b}"], 16)
            e.dma_start(qs[b][SHIFT_ROW:STACK, :, :], I["query_rows"]).then_inc(S[f"q_loaded{b}"], 16)
            if mask_rows is not None:
                e.dma_start(ks[b][MASK_ROW:STACK, :, :],
                            mask_rows[seq].rearrange("(a n) -> a n", a=1).unsqueeze(1).broadcast_to([1, PAIRS, KEYS])
                            ).then_inc(S[f"q_loaded{b}"], 16)

        def stack_keys(e, seq, b):
            hold(e, P.sem, P.turns(seq + 1))
            for j in range(PAIRS):
                for a in range(2):
                    e.dma_start(ks[b][a * SROWS // 2:(a + 1) * SROWS // 2, j, :],
                                kp[b][PR * j:PR * (j + 1), a:a + 3, :]).then_inc(k_stacked[b][j // (PAIRS // 2)], 16)

        def store(e, seq):
            hold(e, S["summed"], seq + 1)
            for dst, row in ((at_dram, 0), (den_dram, 32)):
                e.dma_start(dst.rearrange("(j r) t -> r j t", r=PR)[:, :, bass.ds(seq * SEQ, SEQ)],
                            att[row:row + PR, :].rearrange("r (j q) -> r j q", j=PAIRS)).then_inc(S["bias_loaded_sums_stored"], 16)

        def sync_seq(e, i, w, first, last):
            b, j = w // PAIRS, w % PAIRS
            if j:
                return
            seq = i * 2 + b
            if not last:
                hold(e, S["v_ps"], (seq + 1) * KBANKS)
                e.dma_start(ctx[b][:, :], I["ctxT"][seq + 2]).then_inc(S[f"ctx_loaded{b}"], 16)
            if not (last and b == 1):
                if not (first and b == 0):
                    hold(e, S["score_ps"], seq * PAIRS * KBANKS)
                load_queries(e, seq + 1, 1 - b)
                stack_keys(e, seq + 1, 1 - b)
            if not first:
                store(e, seq - 2)

        with nc.Block() as block:
            @block.sync
            def _(e):
                load_all(e, S["weights_loaded"], [(wk[:, :], I[W + "WkT"]), (wv[:, :], I[W + "WvT"])])
                e.dma_start(bk[:, :], column(I[W + "bk"])).then_inc(S["bias_loaded_sums_stored"], 16)
                for b in range(2):
                    e.dma_start(ctx[b][:, :], I["ctxT"][b]).then_inc(S[f"ctx_loaded{b}"], 16)
                for b in range(2):
                    e.dma_start(ks[b][SHIFT_ROW:STACK, :, :], I["key_rows"]).then_inc(S["rows_loaded"], 16)
                hold(e, S["rows_loaded"], 32)
                load_queries(e, 0, 0)
                stack_keys(e, 0, 0)
                turns(e, sync_seq)
                store(e, SEQS - 2)
                store(e, SEQS - 1)
                hold(e, S["bias_loaded_sums_stored"], 16 + SEQS * 32)

            @block.tensor
            def _(e):
                e.wait_ge(S["rows_loaded"], 32)
                e.wait_ge(S["ones_set"], 2)
                e.wait_ge(S["weights_loaded"], 32)
                e.wait_ge(S["ctx_loaded0"], 16)
                for n in range(KBANKS):
                    if n:
                        e.wait_ge(S["k_f32"], n)
                    keys_matmul(e, 0, n)
                e.wait_ge(S["k_f32"], KBANKS)
                for n in range(KBANKS):
                    if n:
                        e.wait_ge(S["v_copied"], n)
                    values_matmul(e, 0, n)
                e.wait_ge(S["v_copied"], KBANKS)
                e.wait_ge(S["ctx_loaded1"], 16)
                for n in range(KBANKS):
                    if n:
                        e.wait_ge(S["k_f32"], KBANKS + n)
                    keys_matmul(e, 1, n)
                e.wait_ge(S["k_f32"], 2 * KBANKS)
                turns(e, tensor_slot)
                last = SEQS * PAIRS
                e.wait_ge(S["bank_max"], last * KBANKS)
                shift_matmul(e, last - 1, 1)
                for k in (1, 2):
                    pv_matmul(e, last - LAG - 1, 1, (last - LAG - 1) % PAIRS, k, False)
                for u in range(last - LAG, last):
                    for k in range(KBANKS):
                        scores_matmul(e, u, 1, u % PAIRS, k, False)
                        pv_matmul(e, u, 1, u % PAIRS, k, False)
                e.wait_ge(S["pv_copied"], last - PAIRS)
                sum_matmul(e, 0)
                e.wait_ge(S["pv_copied"], last)
                e.wait_ge(S["summed"], SEQS - 1)
                sum_matmul(e, 1)

            @block.scalar
            def _(e):
                e.wait_ge(S["bias_loaded_sums_stored"], 16)
                for n in range(KBANKS):
                    key_copy(e, 0, n)
                e.wait_ge(S["ones_set"], 2)
                for n in range(KBANKS):
                    value_copy(e, 0, 0, n)
                for n in range(KBANKS):
                    key_copy(e, 1, n)
                turns(e, scalar_slot)
                last = SEQS * PAIRS
                pv_copy(e, last - LAG - 1, 1, (last - LAG - 1) % PAIRS)
                for u in range(last - LAG, last):
                    for k in range(KBANKS):
                        exp_bank(e, u, k, False)
                    pv_copy(e, u, 1, u % PAIRS)
                sum_copy(e, SEQS - 2)
                sum_copy(e, SEQS - 1)

            @block.vector
            def _(e):
                for b in range(2):
                    e.memset(vs[b][:, :, :, PR:2 * PR], 1.0).then_inc(S["ones_set"], 1)
                for seq in range(2):
                    for n in range(KBANKS):
                        key_round(e, seq, seq, n, None)
                turns(e, vector_slot)
                shift_copy(e, SEQS * PAIRS - 1, 1, PAIRS - 1)

            @block.gpsimd
            def _(e):
                for seq in range(2):
                    split_keys(e, seq, seq)
                turns(e, gpsimd_slot)


def project_and_route(nc, bank, name, layer, at_dram, den_dram, x_in, x_out, xT_dram, cT_dram, consts, I):
    W = f"L{layer}_xattn_"
    E = E0 if layer == 0 else E1
    with Stage(nc, name) as g:
        AT, DEN, X = g.sb("AT", [D, GROUP]), g.sb("DEN", [D, GROUP]), g.sb("X", [TILE, TILES, D])
        wo, wr = g.sb("wo", [D, D]), g.sb("wr", [D, E])
        bo, bv = g.sb("bo", [TILE, D]), g.sb("bv", [D, 1])
        r, xn, xT = g.sb("r", [TILE, TILES, D]), g.sb("xn", [TILE, TILES, D]), g.sb("xT", [D, GROUP])
        stats, mv, ve, rstd = g.sb("stats", [TILE, 4, 6]), g.sb("mv", [TILE, 4, 2]), g.sb("ve", [TILE, 4]), g.sb("rstd", [TILE, 4])
        sc, c, cT = g.sb("sc", [TILE, TILES, E]), g.sb("c", [TILE, TILES, E]), g.sb("cT", [E, GROUP])
        den = g.sb("den", [TILE, TILES])
        ident, half = consts["ident"], consts["minus_half"]
        if layer == 0:
            cb = g.sb("cb", [TILE, E])
            sfc, t8 = g.sb("sfc", [TILE, TILES, E]), g.sb("t8", [TILE, TILES, G0, 8])
            gs, gtop, gm = g.sb("gs", [TILE, TILES, 12]), g.sb("gtop", [TILE, TILES, 8]), g.sb("gm", [TILE, TILES, 12])
            masked, etop, em = g.sb("masked", [TILE, TILES, E]), g.sb("etop", [TILE, TILES, 8]), g.sb("em", [TILE, TILES, E])
            route = ("plus1 scores biased top2 gsum " + " ".join(f"gtop{s}" for s in range(4)) + " rep "
                     + " ".join(f"gpick{s}" for s in range(4)) + " gmask masked " + " ".join(f"etop{s}" for s in range(4)) + " "
                     + " ".join(f"epick{s}" for s in range(4)) + " emask chosen csum csum_eps cinv weights")
        else:
            top = g.sb("top", [TILE, TILES, 8])
            route = " ".join(f"gtop{s}" for s in range(4)) + " keep less kept csum cinv weights"
        weights, loaded = g.sem("weights_loaded"), g.sem("group_loaded")
        x_stored, xT_stored, cT_stored = g.sem("weight_loaded_x_stored"), g.sem("weight_loaded_xT_stored"), g.sem("weight_loaded_cT_stored")
        set_ = g.sem("sentinels_set") if layer == 0 else None
        T = Steps(g.sem("tensor_steps"), "y_ps xT_ps logits_ps cT_ps")
        A = Steps(g.sem("scalar_steps"), "AT xT exp cT")
        V = Steps(g.sem("vector_steps"), "inv_den divided y_bias y_res " + NORM_VEC + " " + route)
        P = Steps(g.sem("gpsimd_steps"), "rstd")
        nw = [0]
        with nc.Block() as block:
            @block.sync
            def _(e):
                ws = [(cb[:, :], rows_of(I["L0_ffn_correction_bias"]))] if layer == 0 else []
                nw[0] = load_all(e, weights, [(wo[:, :], I[W + "WoT"])] + ws)
                load_all(e, x_stored, [(bo[:, :], rows_of(I[W + "bo"]))])
                load_all(e, xT_stored, [(bv[:, :], column(I[W + "bv"]))])
                load_all(e, cT_stored, [(wr[:, :], I["router" + str(layer)])])

                def load(t):
                    e.dma_start(DEN[:, :], den_dram[:, bass.ds(t * GROUP, GROUP)]).then_inc(loaded, 16)
                    e.dma_start(AT[:, :], at_dram[:, bass.ds(t * GROUP, GROUP)]).then_inc(loaded, 16)
                    e.dma_start(X[:, :, :], tok_major(x_in, t)).then_inc(loaded, 16)

                def store(t):
                    e.dma_start(tok_major(x_out, t), xn[:, :, :]).then_inc(x_stored, 16)
                    hold(e, A.sem, A.at(t, "xT"))
                    e.dma_start(xT_dram[:, bass.ds(t * GROUP, GROUP)], xT[:, :]).then_inc(xT_stored, 16)
                    hold(e, A.sem, A.at(t, "cT"))
                    e.dma_start(cT_dram[0:E, bass.ds(t * GROUP, GROUP)], cT[:, :]).then_inc(cT_stored, 16)

                load(0)
                with e.Fori(0, GROUPS - 1) as t:
                    hold(e, V.sem, V.at(t, "normed3"))
                    load(t + 1)
                    store(t)
                hold(e, V.sem, V.at(GROUPS - 1, "normed3"))
                store(GROUPS - 1)
                for sem in (x_stored, xT_stored, cT_stored):
                    hold(e, sem, 16 * (1 + GROUPS))

            @block.tensor
            def _(e):
                e.wait_ge(weights, nw[0])
                e.wait_ge(cT_stored, 16)
                with e.Fori(0, GROUPS) as t:
                    e.wait_ge(loaded, (t + 1) * 48)
                    e.wait_ge(A.sem, A.at(t, "AT"))
                    for s in range(TILES):
                        m = e.matmul(bank[0][0:TILE, s * D:(s + 1) * D], AT[:, s * TILE:(s + 1) * TILE], wo[:, :], start=True, stop=True)
                    m.then_inc(T.sem, T.one("y_ps"))
                    e.wait_ge(V.sem, V.at(t, "normed3"))
                    for s in range(TILES):
                        m = e.transpose(bank[1][:, s * TILE:(s + 1) * TILE], xn[:, s, :], ident[0:TILE, 0:TILE])
                    m.then_inc(T.sem, T.one("xT_ps"))
                    e.wait_ge(A.sem, A.at(t, "xT"))
                    for s in range(TILES):
                        m = e.matmul(bank[2][0:TILE, s * E:(s + 1) * E], xT[:, s * TILE:(s + 1) * TILE], wr[:, :], start=True, stop=True)
                    m.then_inc(T.sem, T.one("logits_ps"))
                    hold(e, V.sem, V.at(t, "weights"))
                    for s in range(TILES):
                        m = e.transpose(bank[3][0:E, s * TILE:(s + 1) * TILE], c[:, s, :], ident[0:TILE, 0:TILE])
                    m.then_inc(T.sem, T.one("cT_ps"))

            @block.scalar
            def _(e):
                e.wait_ge(xT_stored, 16)
                with e.Fori(0, GROUPS) as t:
                    e.wait_ge(loaded, (t + 1) * 48)
                    e.wait_ge(V.sem, V.at(t, "divided"))
                    e.activation(AT[:, :], AT[:, :], ACT.Identity, bias=bv[:, :]).then_inc(A.sem, A.one("AT"))
                    e.wait_ge(T.sem, T.at(t, "xT_ps"))
                    e.wait_ge(xT_stored, 16 + t * 16)
                    e.copy(xT[:, :], bank[1][:, 0:GROUP]).then_inc(A.sem, A.one("xT"))
                    if layer == 0:
                        e.wait_ge(T.sem, T.at(t, "logits_ps"))
                        e.activation(sc[:, :, :], bank[2][0:TILE, 0:TILES * E].rearrange("p (s n) -> p s n", s=TILES), ACT.Exp, scale=-1.0).then_inc(A.sem, A.one("exp"))
                    else:
                        e.wait_ge(V.sem, V.at(t, "less"))
                        e.activation(sc[:, :, :], c[:, :, :], ACT.Exp).then_inc(A.sem, A.one("exp"))
                    e.wait_ge(T.sem, T.at(t, "cT_ps"))
                    e.wait_ge(cT_stored, 16 + t * 16)
                    e.copy(cT[:, :], bank[3][0:E, 0:GROUP]).then_inc(A.sem, A.one("cT"))

            @block.vector
            def _(e):
                e.wait_ge(weights, nw[0])
                e.wait_ge(x_stored, 16)
                if layer == 0:
                    e.memset(gs[:, :, 8:12], ABSENT).then_inc(set_, 1)
                    e.memset(gtop[:, :, :], ABSENT).then_inc(set_, 1)
                    e.wait_ge(set_, 2)

                def step(before, name, f):
                    e.wait_ge(V.sem, V.at(t, before))
                    return f().then_inc(V.sem, V.one(name))

                with e.Fori(0, GROUPS) as t:
                    e.wait_ge(loaded, (t + 1) * 48)
                    e.reciprocal(DEN[:, :], DEN[:, :]).then_inc(V.sem, V.one("inv_den"))
                    step("inv_den", "divided", lambda: e.tensor_tensor(AT[:, :], AT[:, :], DEN[:, :], ALU.mult))
                    e.wait_ge(T.sem, T.at(t, "y_ps"))
                    e.tensor_tensor(r[:, :, :], bank[0][0:TILE, :].rearrange("p (s d) -> p s d", s=TILES), bc(bo[:, :], TILES, 1), ALU.add).then_inc(V.sem, V.one("y_bias"))
                    e.wait_ge(V.sem, V.at(t, "y_bias"))
                    e.tensor_tensor(r[:, :, :], r[:, :, :], X[:, :, :], ALU.add).then_inc(V.sem, V.one("y_res"))
                    norm_vector(e, V, P, t, r, stats, mv, ve, rstd, xn, "y_res", x_stored)
                    if layer == 0:
                        e.wait_ge(A.sem, A.at(t, "exp"))
                        e.tensor_scalar(sc[:, :, :], sc[:, :, :], 1.0, None, ALU.add).then_inc(V.sem, V.one("plus1"))
                        step("plus1", "scores", lambda: e.reciprocal(sc[:, :, :], sc[:, :, :]))
                        step("scores", "biased", lambda: e.tensor_tensor(sfc[:, :, :], sc[:, :, :], bc(cb[:, :], TILES, 1), ALU.add))
                        hold(e, V.sem, V.at(t, "biased"))
                        for s in range(TILES):
                            for k in range(G0):
                                m = e.max(t8[:, s, k, :], sfc[:, s, k * 8:(k + 1) * 8])
                        m.then_inc(V.sem, V.one("top2"))
                        step("top2", "gsum", lambda: e.tensor_tensor(gs[:, :, 0:8], t8[:, :, :, 0], t8[:, :, :, 1], ALU.add))
                        hold(e, V.sem, V.at(t, "gsum"))
                        for s in range(TILES):
                            e.max(em[:, s, 0:8], gs[:, s, 0:8]).then_inc(V.sem, V.one(f"gtop{s}"))
                        step("gtop3", "rep", lambda: e.tensor_copy(gtop[:, :, 0:4], em[:, :, 0:4]))
                        hold(e, V.sem, V.at(t, "rep"))
                        for s in range(TILES):
                            e.match_replace(out=gm[:, s, :], in_to_replace=gtop[:, s, :], in_values=gs[:, s, :], imm_value=PICKED).then_inc(V.sem, V.one(f"gpick{s}"))
                        step("gpick3", "gmask", lambda: e.tensor_scalar(gm[:, :, 0:8], gm[:, :, 0:8], PICKED, None, ALU.is_ge))
                        step("gmask", "masked", lambda: e.tensor_tensor(masked[:, :, :].rearrange("p s (g n) -> p s g n", g=G0),
                             sfc[:, :, :].rearrange("p s (g n) -> p s g n", g=G0), bc(gm[:, :, 0:8], 8, 3), ALU.mult))
                        hold(e, V.sem, V.at(t, "masked"))
                        for s in range(TILES):
                            e.max(etop[:, s, :], masked[:, s, :]).then_inc(V.sem, V.one(f"etop{s}"))
                        hold(e, V.sem, V.at(t, "etop3"))
                        for s in range(TILES):
                            e.match_replace(out=em[:, s, :], in_to_replace=etop[:, s, :], in_values=masked[:, s, :], imm_value=PICKED).then_inc(V.sem, V.one(f"epick{s}"))
                        step("epick3", "emask", lambda: e.tensor_scalar(em[:, :, :], em[:, :, :], PICKED, None, ALU.is_ge))
                        step("emask", "chosen", lambda: e.tensor_tensor(c[:, :, :], em[:, :, :], sc[:, :, :], ALU.mult))
                        step("chosen", "csum", lambda: e.tensor_reduce(den[:, :], c[:, :, :], AX, ALU.add))
                        step("csum", "csum_eps", lambda: e.tensor_scalar(den[:, :], den[:, :], 1e-20, None, ALU.add))
                        step("csum_eps", "cinv", lambda: e.reciprocal(den[:, :], den[:, :]))
                        e.wait_ge(V.sem, V.at(t, "cinv"))
                        for s in range(TILES):
                            m = e.tensor_scalar(c[:, s, :], c[:, s, :], den[:, s:s + 1], 2.5, ALU.mult, ALU.mult)
                        m.then_inc(V.sem, V.one("weights"))
                    else:
                        gate = bank[2][0:TILE, 0:TILES * E].rearrange("p (s n) -> p s n", s=TILES)
                        hold(e, T.sem, T.at(t, "logits_ps"))
                        for s in range(TILES):
                            e.max(top[:, s, :], gate[:, s, :]).then_inc(V.sem, V.one(f"gtop{s}"))
                        step("gtop3", "keep", lambda: e.tensor_tensor(r[:, :, 0:E], gate, bc(top[:, :, 1], E, 2), ALU.is_ge))
                        e.tensor_tensor(c[:, :, :], gate, bc(top[:, :, 0], E, 2), ALU.subtract).then_inc(V.sem, V.one("less"))
                        e.wait_ge(A.sem, A.at(t, "exp"))
                        e.tensor_tensor(c[:, :, :], sc[:, :, :], r[:, :, 0:E], ALU.mult).then_inc(V.sem, V.one("kept"))
                        step("kept", "csum", lambda: e.tensor_reduce(den[:, :], c[:, :, :], AX, ALU.add))
                        step("csum", "cinv", lambda: e.reciprocal(den[:, :], den[:, :]))
                        e.wait_ge(V.sem, V.at(t, "cinv"))
                        for s in range(TILES):
                            m = e.tensor_scalar(c[:, s, :], c[:, s, :], den[:, s:s + 1], 1.0 / E1, ALU.mult, ALU.mult)
                        m.then_inc(V.sem, V.one("weights"))

            @block.gpsimd
            def _(e):
                with e.Fori(0, GROUPS) as t:
                    e.wait_ge(V.sem, V.at(t, "vareps"))
                    e.tensor_tensor(rstd[:, :], ve[:, :], half[0:TILE, :], ALU.pow).then_inc(P.sem, P.one("rstd"))


def experts(nc, bank, name, layer, xT_dram, cT_dram, yT_dram, consts, I):
    NCH, CPT = (NCH0, 4) if layer == 0 else (NCH1, 2 * I1 // 128)
    OFF = -NCH % CPT
    TURNS, UT, LAG, RING, BUFS = (NCH + OFF) // CPT, CPT * GROUPS, 3, 4, 4
    ACC, UP = 0, 4
    START = OFF * GROUPS
    with Stage(nc, name) as g:
        xT = g.sb("xT", [D, GROUPS, GROUP])
        wu = [g.sb(f"wu{i}", [D, D]) for i in range(BUFS)]
        wd = [g.sb(f"wd{i}", [D, D]) for i in range(BUFS)]
        cB = [g.sb(f"cB{i}", [D, GROUPS, GROUP]) for i in range(BUFS if layer == 0 else 2)]
        b1 = [g.sb(f"b1_{i}", [D, 1]) for i in range(BUFS)]
        hr = [g.sb(f"relu{i}", [D, GROUP]) for i in range(RING)]
        hc = [g.sb(f"weighted{i}", [D, GROUP]) for i in range(RING)]
        h2 = [g.sb(f"squared{i}", [D, GROUP]) for i in range(RING)] if layer == 0 else hc
        b2, cT = g.sb("b2", [E1, D]), g.sb("cT", [E1, GROUPS, GROUP])
        out = g.sb("out", [D, GROUPS, GROUP])
        S = {n: g.sem(n) for n in ["x_loaded", "up_ps", "relu", "weighted", "down_ps", "copied", "stored"]
             + (["squared", "bias_set", "ones_stored"] if layer == 0 else [])}
        chunk_sem = [g.sem(f"chunk_loaded{i}") for i in range(BUFS)]
        expert_sem = [g.sem(f"expert_loaded{i}") for i in range(2)] if layer else None
        done = S["squared"] if layer == 0 else S["weighted"]
        NL = 16 * (4 if layer == 0 else 3)

        def spread(dst, row, n):
            return (dst, cT_dram[row].rearrange("(a g n) -> a g n", a=1, g=GROUPS).broadcast_to([n, GROUPS, GROUP]))

        def load_chunk(e, i, cc):
            f, b = i * CPT + cc - OFF, cc % BUFS
            known = isinstance(i, int)
            if layer and cc % BUFS == 0:
                h = cc // BUFS
                if not (known and f < 2 * BUFS):
                    hold(e, S["down_ps"], (f - BUFS) * GROUPS)
                e.dma_start(*spread(cB[h][:, :, :], i * 2 + h, D)).then_inc(expert_sem[h], 16)
            if not (known and f < BUFS):
                hold(e, S["down_ps"], (f - BUFS + 1) * GROUPS)
            loads = [(wu[b][:, :], I[f"up{layer}"][f]), (wd[b][:, :], I[f"down{layer}"][f])]
            if layer == 0:
                loads += [spread(cB[b][64 * h:64 * h + 64, :, :], 2 * f + h, 64) for h in range(2)]
            else:
                loads += [(b1[b][:, :], I["b1"][f])]
            for dst, src in loads:
                e.dma_start(dst, src).then_inc(chunk_sem[b], 16)

        def chunk_loaded(e, i, cc):
            b = cc % BUFS
            before = cc // BUFS - (1 if b < OFF else 0)
            e.wait_ge(chunk_sem[b], (i * (CPT // BUFS) + before + 1) * NL)

        def expert_loaded(e, i, cc):
            e.wait_ge(expert_sem[cc // BUFS], (i + 1) * 16)

        def weight_of(w):
            cc = w // GROUPS
            return cB[cc % BUFS if layer == 0 else cc // BUFS][:, w % GROUPS, :]

        def tensor_unit(e, i, w, first):
            k = w % GROUPS
            u = i * UT + w - START
            if k == 0:
                chunk_loaded(e, i, w // GROUPS)
            if not (first and w < START + 4):
                e.wait_ge(S["relu"], u - 3)
            e.matmul(bank[UP + w % 4][:, 0:GROUP], wu[w // GROUPS % BUFS][:, :], xT[:, k, :], start=True, stop=True).then_inc(S["up_ps"], 1)
            if not (first and w < START + LAG):
                down(e, u - LAG, (w - LAG) % UT)

        def down(e, u, w):
            e.wait_ge(done, u + 1)
            e.matmul(bank[ACC + w % GROUPS][:, 0:GROUP], wd[w // GROUPS % BUFS][:, :], h2[w % RING][:, :],
                     start=False, stop=False, skip_group_check=True).then_inc(S["down_ps"], 1)

        def scalar_unit(e, i, w, first):
            u = i * UT + w - START
            e.wait_ge(S["up_ps"], u + 1)
            if not (first and w < START + RING):
                e.wait_ge(done, u - RING + 1)
            e.activation(hr[w % RING][:, :], bank[UP + w % 4][:, 0:GROUP], ACT.Relu,
                         bias=b1[w // GROUPS % BUFS if layer else 0][:, :]).then_inc(S["relu"], 1)

        def vector_unit(e, i, w, first):
            u = i * UT + w - START
            e.wait_ge(S["relu"], u + 1)
            if not (first and w < START + RING):
                e.wait_ge(S["squared"] if layer == 0 else S["down_ps"], u - RING + 1)
            e.tensor_tensor(hc[w % RING][:, :], hr[w % RING][:, :], weight_of(w), ALU.mult).then_inc(S["weighted"], 1)

        def gpsimd_unit(e, i, w, first):
            u = i * UT + w - START
            e.wait_ge(S["weighted"], u + 1)
            if not (first and w < START + RING):
                e.wait_ge(S["down_ps"], u - RING + 1)
            e.tensor_tensor(h2[w % RING][:, :], hc[w % RING][:, :], hr[w % RING][:, :], ALU.mult).then_inc(S["squared"], 1)

        def turns(e, unit):
            for w in range(START, UT):
                unit(e, 0, w, True)
            with e.Fori(1, TURNS) as i:
                for w in range(UT):
                    unit(e, i, w, False)

        with nc.Block() as block:
            @block.sync
            def _(e):
                if layer == 0:
                    e.dma_start(cT_dram[E0:E0 + SHARED // I0], I["ones_rows"]).then_inc(S["ones_stored"], 16)
                    hold(e, S["ones_stored"], 16)
                e.dma_start(xT[:, :, :], xT_dram.rearrange("d (g n) -> d g n", g=GROUPS)).then_inc(S["x_loaded"], 16)
                e.dma_start(b2[:, :], I["b2_or_zero" + str(layer)]).then_inc(S["x_loaded"], 16)
                e.dma_start(cT[:, :, :], cT_dram[0:E1].rearrange("c (g n) -> c g n", g=GROUPS)).then_inc(S["x_loaded"], 16)
                for i in range(2):
                    for cc in range(OFF if i == 0 else 0, CPT):
                        load_chunk(e, i, cc)
                with e.Fori(2, TURNS) as i:
                    for cc in range(CPT):
                        load_chunk(e, i, cc)
                hold(e, S["copied"], GROUPS)
                e.dma_start(yT_dram.rearrange("d (g n) -> d g n", g=GROUPS), out[:, :, :]).then_inc(S["stored"], 16)
                hold(e, S["stored"], 16)

            @block.tensor
            def _(e):
                e.wait_ge(S["x_loaded"], 48)
                for k in range(GROUPS):
                    e.matmul(bank[ACC + k][:, 0:GROUP], b2[:, :], cT[:, k, :], start=True, stop=False, skip_group_check=True)
                turns(e, tensor_unit)
                for w in range(UT - LAG, UT):
                    down(e, (TURNS - 1) * UT + w - START, w)

            @block.scalar
            def _(e):
                if layer == 0:
                    e.wait_ge(S["bias_set"], 1)

                def unit(e, i, w, first):
                    if layer and w % GROUPS == 0:
                        chunk_loaded(e, i, w // GROUPS)
                    scalar_unit(e, i, w, first)
                turns(e, unit)

            @block.vector
            def _(e):
                if layer == 0:
                    e.memset(b1[0][:, :], 0.0).then_inc(S["bias_set"], 1)

                def unit(e, i, w, first):
                    if layer == 0 and w % GROUPS == 0:
                        chunk_loaded(e, i, w // GROUPS)
                    if layer and w % (GROUPS * BUFS) == 0:
                        expert_loaded(e, i, w // GROUPS)
                    vector_unit(e, i, w, first)
                turns(e, unit)
                e.wait_ge(S["down_ps"], NCH * GROUPS)
                for k in range(GROUPS):
                    e.tensor_copy(out[:, k, :], bank[ACC + k][:, 0:GROUP]).then_inc(S["copied"], 1)

            if layer == 0:
                @block.gpsimd
                def _(e):
                    turns(e, gpsimd_unit)


def norm_and_project_1(nc, bank, yT_dram, x_in, x3, qkT_dram, v_dram, consts, I):
    with Stage(nc, "np1") as g:
        YT, X = g.sb("YT", [D, GROUP]), g.sb("X", [TILE, TILES, D])
        w = g.sb("w", [D, 3, D])
        qks = g.sb("qks", [D, 2])
        ident, half, ones8 = consts["ident"], consts["minus_half"], g.sb("ones8", [D, D])
        r, xn, xT = g.sb("r", [TILE, TILES, D]), g.sb("xn", [TILE, TILES, D]), g.sb("xT", [D, GROUP])
        stats, mv, ve, rstd = g.sb("stats", [TILE, 4, 6]), g.sb("mv", [TILE, 4, 2]), g.sb("ve", [TILE, 4]), g.sb("rstd", [TILE, 4])
        qk, sig, sq, nrm = [g.sb(n, [D, 2, GROUP]) for n in ("qk", "sig", "sq", "nrm")]
        v, sv = g.sb("v", [TILE, TILES, D]), g.sb("sv", [TILE, TILES, D])
        weights, loaded = g.sem("weights_loaded"), g.sem("group_loaded")
        x_stored, v_stored, qk_stored = g.sem("weight_loaded_x_stored"), g.sem("weight_loaded_v_stored"), g.sem("weight_loaded_qk_stored")
        T = Steps(g.sem("tensor_steps"), "y_ps xT_ps q_ps k_ps v_ps norms_ps")
        A = Steps(g.sem("scalar_steps"), "xT expq expk expv norms")
        V = Steps(g.sem("vector_steps"), "y_res " + NORM_VEC + " plus1 inv silu_q silu_k squares vplus1 vinv silu_v r_eps r_inv ratio scaled_q scaled_k")
        P = Steps(g.sem("gpsimd_steps"), "rstd")
        with nc.Block() as block:
            @block.sync
            def _(e):
                load_all(e, weights, [(w[:, n, :], I[f"L1_attn_W{c}T"]) for n, c in enumerate("qkv")])
                load_all(e, x_stored, [(ones8[:, :], I["ones8"])])
                load_all(e, v_stored, [(qks[:, 0:1], column(I["q_scale_rows"]))])
                load_all(e, qk_stored, [(qks[:, 1:2], column(I["k_scale_rows"]))])

                def load(t):
                    e.dma_start(YT[:, :], yT_dram[:, bass.ds(t * GROUP, GROUP)]).then_inc(loaded, 16)
                    e.dma_start(X[:, :, :], tok_major(x_in, t)).then_inc(loaded, 16)

                def store(t):
                    e.dma_start(tok_major(x3, t), xn[:, :, :]).then_inc(x_stored, 16)
                    hold(e, V.sem, V.at(t, "silu_v"))
                    e.dma_start(tok_major(v_dram, t), v[:, :, :]).then_inc(v_stored, 16)
                    hold(e, V.sem, V.at(t, "scaled_k"))
                    e.dma_start(qkT_dram[:, :, bass.ds(t * GROUP, GROUP)], qk[:, :, :]).then_inc(qk_stored, 16)

                load(0)
                with e.Fori(0, GROUPS - 1) as t:
                    hold(e, V.sem, V.at(t, "normed3"))
                    load(t + 1)
                    store(t)
                hold(e, V.sem, V.at(GROUPS - 1, "normed3"))
                store(GROUPS - 1)
                for sem in (x_stored, v_stored, qk_stored):
                    hold(e, sem, 16 * (1 + GROUPS))

            @block.tensor
            def _(e):
                e.wait_ge(weights, 48)
                e.wait_ge(x_stored, 16)
                with e.Fori(0, GROUPS) as t:
                    e.wait_ge(loaded, (t + 1) * 32)
                    for s in range(TILES):
                        m = e.transpose(bank[0][0:TILE, s * D:(s + 1) * D], YT[:, s * TILE:(s + 1) * TILE], ident[:, :])
                    m.then_inc(T.sem, T.one("y_ps"))
                    e.wait_ge(V.sem, V.at(t, "normed3"))
                    for s in range(TILES):
                        m = e.transpose(bank[1][:, s * TILE:(s + 1) * TILE], xn[:, s, :], ident[0:TILE, 0:TILE])
                    m.then_inc(T.sem, T.one("xT_ps"))
                    e.wait_ge(A.sem, A.at(t, "xT"))
                    for n, c in enumerate("qk"):
                        e.matmul(bank[2 + n][:, 0:GROUP], w[:, n, :], xT[:, :], start=True, stop=True).then_inc(T.sem, T.one(f"{c}_ps"))
                    for s in range(TILES):
                        m = e.matmul(bank[4][0:TILE, s * D:(s + 1) * D], xT[:, s * TILE:(s + 1) * TILE], w[:, 2, :], start=True, stop=True)
                    m.then_inc(T.sem, T.one("v_ps"))
                    e.wait_ge(V.sem, V.at(t, "squares"))
                    for n in range(2):
                        m = e.matmul(bank[5 + n][:, 0:GROUP], ones8[:, :], sq[:, n, :], start=True, stop=True)
                    m.then_inc(T.sem, T.one("norms_ps"))

            @block.scalar
            def _(e):
                with e.Fori(0, GROUPS) as t:
                    e.wait_ge(loaded, (t + 1) * 32)
                    e.wait_ge(T.sem, T.at(t, "xT_ps"))
                    e.copy(xT[:, :], bank[1][:, 0:GROUP]).then_inc(A.sem, A.one("xT"))
                    for n, c in enumerate("qk"):
                        e.wait_ge(T.sem, T.at(t, f"{c}_ps"))
                        e.activation(sig[:, n, :], bank[2 + n][:, 0:GROUP], ACT.Exp, scale=-1.0).then_inc(A.sem, A.one(f"exp{c}"))
                    e.wait_ge(T.sem, T.at(t, "v_ps"))
                    e.activation(sv[:, :, :], bank[4][0:TILE, :].rearrange("p (s d) -> p s d", s=TILES), ACT.Exp, scale=-1.0).then_inc(A.sem, A.one("expv"))
                    e.wait_ge(T.sem, T.at(t, "norms_ps"))
                    for n in range(2):
                        m = e.activation(nrm[:, n, :], bank[5 + n][:, 0:GROUP], ACT.Sqrt)
                    m.then_inc(A.sem, A.one("norms"))

            @block.vector
            def _(e):
                for sem in (v_stored, qk_stored):
                    e.wait_ge(sem, 16)

                def step(before, name, f):
                    e.wait_ge(V.sem, V.at(t, before))
                    return f().then_inc(V.sem, V.one(name))

                with e.Fori(0, GROUPS) as t:
                    e.wait_ge(loaded, (t + 1) * 32)
                    e.wait_ge(T.sem, T.at(t, "y_ps"))
                    e.tensor_tensor(r[:, :, :], bank[0][0:TILE, :].rearrange("p (s d) -> p s d", s=TILES), X[:, :, :], ALU.add).then_inc(V.sem, V.one("y_res"))
                    norm_vector(e, V, P, t, r, stats, mv, ve, rstd, xn, "y_res", x_stored)
                    e.wait_ge(A.sem, A.at(t, "expk"))
                    e.tensor_scalar(sig[:, :, :], sig[:, :, :], 1.0, None, ALU.add).then_inc(V.sem, V.one("plus1"))
                    step("plus1", "inv", lambda: e.reciprocal(sig[:, :, :], sig[:, :, :]))
                    e.wait_ge(V.sem, V.at(t, "inv"))
                    e.wait_ge(qk_stored, 16 + t * 16)
                    for n, c in enumerate("qk"):
                        e.tensor_tensor(qk[:, n, :], sig[:, n, :], bank[2 + n][:, 0:GROUP], ALU.mult).then_inc(V.sem, V.one(f"silu_{c}"))
                    step("silu_k", "squares", lambda: e.tensor_tensor(sq[:, :, :], qk[:, :, :], qk[:, :, :], ALU.mult))
                    e.wait_ge(A.sem, A.at(t, "expv"))
                    e.tensor_scalar(sv[:, :, :], sv[:, :, :], 1.0, None, ALU.add).then_inc(V.sem, V.one("vplus1"))
                    step("vplus1", "vinv", lambda: e.reciprocal(sv[:, :, :], sv[:, :, :]))
                    e.wait_ge(v_stored, 16 + t * 16)
                    step("vinv", "silu_v", lambda: e.tensor_tensor(v[:, :, :], sv[:, :, :], bank[4][0:TILE, :].rearrange("p (s d) -> p s d", s=TILES), ALU.mult))
                    e.wait_ge(A.sem, A.at(t, "norms"))
                    e.tensor_scalar(sig[:, :, :], nrm[:, :, :], 1e-6, None, ALU.add).then_inc(V.sem, V.one("r_eps"))
                    step("r_eps", "r_inv", lambda: e.reciprocal(sig[:, :, :], sig[:, :, :]))
                    step("r_inv", "ratio", lambda: e.tensor_tensor(sig[:, :, :], sig[:, :, :], nrm[:, :, :], ALU.mult))
                    e.wait_ge(V.sem, V.at(t, "ratio"))
                    for n, c in enumerate("qk"):
                        e.scalar_tensor_tensor(out=qk[:, n, :], in0=qk[:, n, :], scalar=qks[:, n:n + 1], in1=sig[:, n, :], op0=ALU.mult, op1=ALU.mult).then_inc(V.sem, V.one(f"scaled_{c}"))

            @block.gpsimd
            def _(e):
                with e.Fori(0, GROUPS) as t:
                    e.wait_ge(V.sem, V.at(t, "vareps"))
                    e.tensor_tensor(rstd[:, :], ve[:, :], half[0:TILE, :], ALU.pow).then_inc(P.sem, P.one("rstd"))


def causal_attention(nc, bank, qkT_dram, v_dram, oT_dram, consts, I):
    N = HEADS * SEQ
    HH, HQ = HEADS // 2, HEADS // 4
    ROWS = 64 + SEQ
    TURNS = SEQS // 4
    with Stage(nc, "ca") as g:
        qk = [g.sb(f"qk{i}", [D, 2, 2, SEQ]) for i in range(2)]
        v = [g.sb(f"v{i}", [SEQ, 2, D]) for i in range(2)]
        kx = [g.sb(f"kx{i}", [D, 2, HEADS, SEQ]) for i in range(2)]
        p = [g.sb(f"p{i}", [ROWS, HEADS, SEQ]) for i in range(2)]
        pT = [g.sb(f"pT{i}", [SEQ, HEADS, ROWS]) for i in range(2)]
        mx, den = [g.sb(f"mx{i}", [ROWS, HEADS]) for i in range(2)], [g.sb(f"den{i}", [ROWS, HEADS]) for i in range(2)]
        o, oT = [g.sb(f"o{i}", [ROWS, D]) for i in range(2)], [g.sb(f"oT{i}", [D, 2, SEQ]) for i in range(2)]
        causal, headmask, ident = g.sb("causal", [ROWS, SEQ]), g.sb("headmask", [D, HEADS]), consts["ident"]
        banks_set = g.sem("banks_set")
        loaded = [g.sem(f"couple_loaded{i}") for i in range(2)]
        stored = [g.sem(f"constant_loaded_couple_stored{i}") for i in range(2)]
        T = [Steps(g.sem(f"tensor_steps{i}"), "s_ps pT_ps o_ps oT_ps") for i in range(2)]
        A = [Steps(g.sem(f"scalar_steps{i}"), "exp pT_0 pT_1 pT_2 pT_3 o oT") for i in range(2)]
        V = [Steps(g.sem(f"vector_steps{i}"), "masked_a masked_b max sum inv") for i in range(2)]
        P = [Steps(g.sem(f"gpsimd_steps{i}"), "kx0 kx1 shifted probs") for i in range(2)]
        with nc.Block() as block:
            @block.sync
            def _(e):
                load_all(e, stored[0], [(causal[:, :], I["causal"])])
                load_all(e, stored[1], [(headmask[:, :], I["headmask"])])

                def load(t, b):
                    at = (t * 2 + b) * 2 * SEQ
                    e.dma_start(qk[b][:, :, :, :], qkT_dram[:, :, bass.ds(at, 2 * SEQ)].rearrange("d a (s n) -> d a s n", s=2)).then_inc(loaded[b], 16)
                    e.dma_start(v[b][:, :, :], v_dram[bass.ds(at, 2 * SEQ), :].rearrange("(s p) d -> p s d", s=2)).then_inc(loaded[b], 16)

                def store(t, b):
                    hold(e, A[b].sem, A[b].at(t, "oT"))
                    e.dma_start(oT_dram[:, bass.ds((t * 2 + b) * 2 * SEQ, 2 * SEQ)], oT[b][:, :, :].rearrange("d s n -> d (s n)")).then_inc(stored[b], 16)

                for b in range(2):
                    load(0, b)
                with e.Fori(0, TURNS - 1) as t:
                    for b in range(2):
                        hold(e, T[b].sem, T[b].at(t, "o_ps"))
                        load(t + 1, b)
                    for b in range(2):
                        store(t, b)
                for b in range(2):
                    store(TURNS - 1, b)
                for b in range(2):
                    hold(e, stored[b], 16 * (1 + TURNS))

            @block.tensor
            def _(e):
                e.wait_ge(banks_set, 4)
                with e.Fori(0, TURNS) as t:
                    for b in range(2):
                        hold(e, loaded[b], (t + 1) * 32)
                        hold(e, P[b].sem, P[b].at(t, "kx1"))
                        for s in range(2):
                            for h in range(2):
                                m = e.matmul(bank[4 * b + h][64 * s:64 * s + SEQ, 0:N // 2], qk[b][:, 0, s, :],
                                             kx[b][:, s, h * HH:(h + 1) * HH, :], start=True, stop=True)
                        m.then_inc(T[b].sem, T[b].one("s_ps"))
                    for b in range(2):
                        hold(e, P[b].sem, P[b].at(t, "probs"))
                        for h in range(HEADS):
                            m = e.transpose(bank[4 * b + h // HQ][0:SEQ, h % HQ * ROWS:(h % HQ + 1) * ROWS],
                                            p[b][:, h, :], ident[0:ROWS, 0:ROWS])
                        m.then_inc(T[b].sem, T[b].one("pT_ps"))
                    for b in range(2):
                        hold(e, A[b].sem, A[b].at(t, "pT_3"))
                        for s in range(2):
                            for h in range(HEADS):
                                m = e.matmul(bank[4 * b][64 * s:64 * s + SEQ, h * HD:(h + 1) * HD], pT[b][:, h, 64 * s:64 * s + SEQ],
                                             v[b][:, s, h * HD:(h + 1) * HD], start=True, stop=True)
                        m.then_inc(T[b].sem, T[b].one("o_ps"))
                    for b in range(2):
                        hold(e, A[b].sem, A[b].at(t, "o"))
                        e.transpose(bank[4 * b + 3][:, 0:ROWS], o[b][:, :], ident[0:ROWS, 0:ROWS]).then_inc(T[b].sem, T[b].one("oT_ps"))

            @block.scalar
            def _(e):
                for b in range(2):
                    e.wait_ge(stored[b], 16)
                with e.Fori(0, TURNS) as t:
                    for b in range(2):
                        e.wait_ge(P[b].sem, P[b].at(t, "shifted"))
                        e.activation(p[b][:, :, :], p[b][:, :, :], ACT.Exp).then_inc(A[b].sem, A[b].one("exp"))
                    for b in range(2):
                        e.wait_ge(T[b].sem, T[b].at(t, "pT_ps"))
                        for h in range(4):
                            e.copy(pT[b][:, h * HQ:(h + 1) * HQ, :], bank[4 * b + h][0:SEQ, 0:HQ * ROWS].rearrange("p (h q) -> p h q", h=HQ)
                                   ).then_inc(A[b].sem, A[b].one(f"pT_{h}"))
                    for b in range(2):
                        e.wait_ge(T[b].sem, T[b].at(t, "o_ps"))
                        e.copy(o[b][:, :], bank[4 * b][0:ROWS, 0:D]).then_inc(A[b].sem, A[b].one("o"))
                    for b in range(2):
                        e.wait_ge(stored[b], 16 + t * 16)
                        e.wait_ge(T[b].sem, T[b].at(t, "oT_ps"))
                        e.copy(oT[b][:, :, :], bank[4 * b + 3][:, 0:2 * 64].rearrange("p (s q) -> p s q", s=2)[:, :, 0:SEQ]).then_inc(A[b].sem, A[b].one("oT"))

            @block.vector
            def _(e):
                for k in (0, 1, 4, 5):
                    e.memset(bank[k][:, :], 0.0).then_inc(banks_set, 1)
                e.wait_ge(stored[0], 16)
                with e.Fori(0, TURNS) as t:
                    for b in range(2):
                        e.wait_ge(T[b].sem, T[b].at(t, "s_ps"))
                        for h in range(2):
                            e.tensor_tensor(p[b][:, h * HH:(h + 1) * HH, :], bank[4 * b + h][0:ROWS, 0:N // 2].rearrange("p (h k) -> p h k", h=HH),
                                            bc(causal[:, :], HH, 1), ALU.add).then_inc(V[b].sem, V[b].one(f"masked_{'ab'[h]}"))
                        e.wait_ge(V[b].sem, V[b].at(t, "masked_b"))
                        e.tensor_reduce(mx[b][:, :], p[b][:, :, :], AX, ALU.max).then_inc(V[b].sem, V[b].one("max"))
                    for b in range(2):
                        e.wait_ge(A[b].sem, A[b].at(t, "exp"))
                        e.tensor_reduce(den[b][:, :], p[b][:, :, :], AX, ALU.add).then_inc(V[b].sem, V[b].one("sum"))
                        e.wait_ge(V[b].sem, V[b].at(t, "sum"))
                        e.reciprocal(den[b][:, :], den[b][:, :]).then_inc(V[b].sem, V[b].one("inv"))

            @block.gpsimd
            def _(e):
                e.wait_ge(stored[1], 16)
                with e.Fori(0, TURNS) as t:
                    for b in range(2):
                        e.wait_ge(loaded[b], (t + 1) * 32)
                        for s in range(2):
                            e.tensor_tensor(kx[b][:, s, :, :], bc(qk[b][:, 1, s, :], HEADS, 1), bc(headmask[:, :], SEQ, 2), ALU.mult).then_inc(P[b].sem, P[b].one(f"kx{s}"))
                    for b in range(2):
                        e.wait_ge(V[b].sem, V[b].at(t, "max"))
                        e.tensor_tensor(p[b][:, :, :], p[b][:, :, :], bc(mx[b][:, :], SEQ, 2), ALU.subtract).then_inc(P[b].sem, P[b].one("shifted"))
                    for b in range(2):
                        e.wait_ge(V[b].sem, V[b].at(t, "inv"))
                        e.tensor_tensor(p[b][:, :, :], p[b][:, :, :], bc(den[b][:, :], SEQ, 2), ALU.mult).then_inc(P[b].sem, P[b].one("probs"))


def project_1(nc, bank, oT_dram, x_in, x_out, qx_dram, consts, I):
    with Stage(nc, "pr1") as g:
        OT, X = g.sb("OT", [D, GROUP]), g.sb("X", [TILE, TILES, D])
        wo, wq, bq, bqs = g.sb("wo", [D, D]), g.sb("wq", [D, D]), g.sb("bq", [D, 1]), g.sb("bqs", [D, 1])
        ident, half, parity = consts["ident"], consts["minus_half"], consts["parity"]
        r, xn, xT, qT = g.sb("r", [TILE, TILES, D]), g.sb("xn", [TILE, TILES, D]), g.sb("xT", [D, GROUP]), g.sb("qT", [D, GROUP])
        stats, mv, ve, rstd = g.sb("stats", [TILE, 4, 6]), g.sb("mv", [TILE, 4, 2]), g.sb("ve", [TILE, 4]), g.sb("rstd", [TILE, 4])
        qh, qm, ql, qrest = g.sb("qh", [D, GROUP], BF16), g.sb("qm", [D, GROUP], BF16), g.sb("ql", [D, GROUP], BF16), g.sb("qrest", [D, GROUP])
        qx = g.sb("qx", [D, GSEQS, PROD, 2, SEQ], BF16)
        loaded, bias_loaded, scaled = g.sem("group_loaded"), g.sem("bias_loaded"), g.sem("bias_scaled")
        x_stored, q_stored = g.sem("weight_loaded_x_stored"), g.sem("weight_loaded_queries_stored")
        T = Steps(g.sem("tensor_steps"), "y_ps xT_ps qT_ps")
        A = Steps(g.sem("scalar_steps"), "xT qT")
        V = Steps(g.sem("vector_steps"), "y_res " + NORM_VEC)
        P = Steps(g.sem("gpsimd_steps"), "rstd " + QPREP_POOL)
        with nc.Block() as block:
            @block.sync
            def _(e):
                load_all(e, x_stored, [(wo[:, :], I["L1_attn_WoT"])])
                load_all(e, q_stored, [(wq[:, :], I["L1_xattn_Wq"])])
                load_all(e, bias_loaded, [(bq[:, :], column(I["L1_xattn_bq"]))])

                def load(t):
                    e.dma_start(OT[:, :], oT_dram[:, bass.ds(t * GROUP, GROUP)]).then_inc(loaded, 16)
                    e.dma_start(X[:, :, :], tok_major(x_in, t)).then_inc(loaded, 16)

                def store(t):
                    e.dma_start(tok_major(x_out, t), xn[:, :, :]).then_inc(x_stored, 16)
                    hold(e, P.sem, P.at(t, "x_h2"))
                    store_queries(e, q_stored, t, qx_dram, qx)

                load(0)
                with e.Fori(0, GROUPS - 1) as t:
                    hold(e, V.sem, V.at(t, "normed3"))
                    load(t + 1)
                    store(t)
                hold(e, V.sem, V.at(GROUPS - 1, "normed3"))
                store(GROUPS - 1)
                hold(e, x_stored, 16 * (1 + GROUPS))
                hold(e, q_stored, 16 + GROUPS * QUERY_STORES)

            @block.tensor
            def _(e):
                for sem in (x_stored, q_stored):
                    e.wait_ge(sem, 16)
                with e.Fori(0, GROUPS) as t:
                    e.wait_ge(loaded, (t + 1) * 32)
                    for s in range(TILES):
                        m = e.matmul(bank[0][0:TILE, s * D:(s + 1) * D], OT[:, s * TILE:(s + 1) * TILE], wo[:, :], start=True, stop=True)
                    m.then_inc(T.sem, T.one("y_ps"))
                    e.wait_ge(V.sem, V.at(t, "normed3"))
                    for s in range(TILES):
                        m = e.transpose(bank[1][:, s * TILE:(s + 1) * TILE], xn[:, s, :], ident[0:TILE, 0:TILE])
                    m.then_inc(T.sem, T.one("xT_ps"))
                    e.wait_ge(A.sem, A.at(t, "xT"))
                    e.matmul(bank[2][:, 0:GROUP], wq[:, :], xT[:, :], start=True, stop=True).then_inc(T.sem, T.one("qT_ps"))

            @block.scalar
            def _(e):
                e.wait_ge(scaled, 1)
                with e.Fori(0, GROUPS) as t:
                    e.wait_ge(loaded, (t + 1) * 32)
                    e.wait_ge(T.sem, T.at(t, "xT_ps"))
                    e.copy(xT[:, :], bank[1][:, 0:GROUP]).then_inc(A.sem, A.one("xT"))
                    e.wait_ge(T.sem, T.at(t, "qT_ps"))
                    e.activation(qT[:, :], bank[2][:, 0:GROUP], ACT.Identity, bias=bqs[:, :], scale=HD ** -0.5).then_inc(A.sem, A.one("qT"))

            @block.vector
            def _(e):
                e.wait_ge(bias_loaded, 16)
                e.tensor_scalar(bqs[:, :], bq[:, :], HD ** -0.5, None, ALU.mult).then_inc(scaled, 1)
                with e.Fori(0, GROUPS) as t:
                    e.wait_ge(loaded, (t + 1) * 32)
                    e.wait_ge(T.sem, T.at(t, "y_ps"))
                    e.tensor_tensor(r[:, :, :], bank[0][0:TILE, :].rearrange("p (s d) -> p s d", s=TILES), X[:, :, :], ALU.add).then_inc(V.sem, V.one("y_res"))
                    norm_vector(e, V, P, t, r, stats, mv, ve, rstd, xn, "y_res", x_stored)

            @block.gpsimd
            def _(e):
                with e.Fori(0, GROUPS) as t:
                    e.wait_ge(V.sem, V.at(t, "vareps"))
                    e.tensor_tensor(rstd[:, :], ve[:, :], half[0:TILE, :], ALU.pow).then_inc(P.sem, P.one("rstd"))
                    qprep_pool(e, P, A, t, qT, qh, qrest, qm, ql, qx, parity, q_stored)


def final_norm(nc, bank, yT_dram, x_in, out, consts):
    with Stage(nc, "fin") as g:
        YT, X = g.sb("YT", [D, GROUP]), g.sb("X", [TILE, TILES, D])
        r, xn = g.sb("r", [TILE, TILES, D]), g.sb("xn", [TILE, TILES, D])
        stats, mv, ve, rstd = g.sb("stats", [TILE, 4, 6]), g.sb("mv", [TILE, 4, 2]), g.sb("ve", [TILE, 4]), g.sb("rstd", [TILE, 4])
        ident, half = consts["ident"], consts["minus_half"]
        loaded, x_stored = g.sem("group_loaded"), g.sem("first_x_loaded_x_stored")
        T = Steps(g.sem("tensor_steps"), "y_ps")
        V = Steps(g.sem("vector_steps"), "y_res " + NORM_VEC)
        P = Steps(g.sem("gpsimd_steps"), "rstd")
        with nc.Block() as block:
            @block.sync
            def _(e):

                def load(t):
                    e.dma_start(YT[:, :], yT_dram[:, bass.ds(t * GROUP, GROUP)]).then_inc(loaded, 16)
                    e.dma_start(X[:, :, :], tok_major(x_in, t)).then_inc(x_stored if isinstance(t, int) and t == 0 else loaded, 16)

                def store(t):
                    e.dma_start(tok_major(out, t), xn[:, :, :]).then_inc(x_stored, 16)

                load(0)
                with e.Fori(0, GROUPS - 1) as t:
                    hold(e, V.sem, V.at(t, "normed3"))
                    load(t + 1)
                    store(t)
                hold(e, V.sem, V.at(GROUPS - 1, "normed3"))
                store(GROUPS - 1)
                hold(e, x_stored, 16 * (1 + GROUPS))

            @block.tensor
            def _(e):
                with e.Fori(0, GROUPS) as t:
                    e.wait_ge(loaded, t * 32 + 16)
                    for s in range(TILES):
                        m = e.transpose(bank[0][0:TILE, s * D:(s + 1) * D], YT[:, s * TILE:(s + 1) * TILE], ident[:, :])
                    m.then_inc(T.sem, T.one("y_ps"))

            @block.vector
            def _(e):
                e.wait_ge(x_stored, 16)
                with e.Fori(0, GROUPS) as t:
                    e.wait_ge(loaded, t * 32 + 16)
                    e.wait_ge(T.sem, T.at(t, "y_ps"))
                    e.tensor_tensor(r[:, :, :], bank[0][0:TILE, :].rearrange("p (s d) -> p s d", s=TILES), X[:, :, :], ALU.add).then_inc(V.sem, V.one("y_res"))
                    norm_vector(e, V, P, t, r, stats, mv, ve, rstd, xn, "y_res", x_stored)

            @block.gpsimd
            def _(e):
                with e.Fori(0, GROUPS) as t:
                    e.wait_ge(V.sem, V.at(t, "vareps"))
                    e.tensor_tensor(rstd[:, :], ve[:, :], half[0:TILE, :], ALU.pow).then_inc(P.sem, P.one("rstd"))


def set_up(nc, consts, mask_dram, I):
    with Stage(nc, "set") as g:
        m8, mf, mb = g.sb("m8", [SEQS, KEYS // 4], mybir.dt.int32), g.sb("mf", [SEQS, KEYS]), g.sb("mb", [SEQS, KEYS], BF16)
        loaded, turned, stored = g.sem("loaded"), g.sem("mask_turned"), g.sem("mask_stored")
        with nc.Block() as block:
            @block.sync
            def _(e):
                load_all(e, loaded, [(m8[:, :], I["mask"]), (consts["ident"][:, :], I["ident"]),
                                     (consts["parity"][:, :], I["parity"]), (consts["sumq"][:, :, :], I["sumq"])])
                hold(e, turned, 3)
                e.dma_start(mask_dram, mb[:, :]).then_inc(stored, 16)
                hold(e, stored, 16)

            @block.vector
            def _(e):
                e.memset(consts["minus_half"][:, :], -0.5)
                e.wait_ge(loaded, 64)
                e.tensor_copy(consts["identb"][:, :], consts["ident"][:, :]).then_inc(turned, 1)
                e.tensor_copy(mf[:, :], m8[:, :].bitcast(U8)).then_inc(turned, 1)
                e.wait_ge(turned, 2)
                e.tensor_scalar(mb[:, :], mf[:, :], -1.0, PICKED, ALU.add, ALU.mult).then_inc(turned, 1)


def decoder(nc, I, out):
    with ExitStack() as ctx:
        bank = [ctx.enter_context(nc.psum_tensor(f"bank{i}", [128, 512], F32)) for i in range(8)]
        sb = lambda n, shape, dt=F32: ctx.enter_context(nc.sbuf_tensor(n, shape, dt))
        consts = {"ident": sb("ident_sb", [128, 128]), "identb": sb("identb_sb", [128, 128], BF16),
                  "parity": sb("parity_sb", [128, 2]), "sumq": sb("sumq_sb", [128, 2, 48]), "minus_half": sb("minus_half_sb", [128, 4])}
        dram = lambda n, shape, dt=F32: nc.dram_tensor(n, shape, dt, kind="Internal").ap()
        x = [dram(f"x_after{i}", (TOKENS, D)) for i in range(5)]
        qx = [dram(f"query_operands{i}", (SEQS, PAIRS, SROWS, 2 * SEQ), BF16) for i in range(2)]
        at = [dram(f"attended{i}", (D, TOKENS)) for i in range(2)]
        denominators = dram("attention_denominators", (D, TOKENS))
        xT = [dram(f"xT{i}", (D, TOKENS)) for i in range(2)]
        yT = [dram(f"yT{i}", (D, TOKENS)) for i in range(2)]
        cT = [dram("expert_weights0", (E0 + SHARED // I0, TOKENS)), dram("expert_weights1", (E1, TOKENS))]
        mask, qkT, v, oT = dram("mask_rows", (SEQS, KEYS), BF16), dram("qkT", (D, 2, TOKENS)), dram("v1", (TOKENS, D)), dram("oT1", (D, TOKENS))
        set_up(nc, consts, mask, I)
        self_attention_0(nc, bank, I, x[0], qx[0], consts)
        cross_attention(nc, bank, "xa0", "L0_xattn_", qx[0], None, at[0], denominators, consts, I)
        project_and_route(nc, bank, "rt0", 0, at[0], denominators, x[0], x[1], xT[0], cT[0], consts, I)
        experts(nc, bank, "ex0", 0, xT[0], cT[0], yT[0], consts, I)
        norm_and_project_1(nc, bank, yT[0], x[1], x[2], qkT, v, consts, I)
        causal_attention(nc, bank, qkT, v, oT, consts, I)
        project_1(nc, bank, oT, x[2], x[3], qx[1], consts, I)
        cross_attention(nc, bank, "xa1", "L1_xattn_", qx[1], mask, at[1], denominators, consts, I)
        project_and_route(nc, bank, "rt1", 1, at[1], denominators, x[3], x[4], xT[1], cT[1], consts, I)
        experts(nc, bank, "ex1", 1, xT[1], cT[1], yT[1], consts, I)
        final_norm(nc, bank, yT[1], x[4], out, consts)


def shape_constants():
    f = np.float32
    pos = (np.arange(TILE) % SEQ).astype(f)
    inv = (f(1.0) / np.power(f(10000.0), np.arange(0, HD, 2, dtype=f) / f(HD))).astype(f)
    ang = pos[:, None] * inv[None, :]
    rows = np.arange(D)
    sumq = np.zeros((D, 2, 48), f)
    for p in range(D):
        r = p % 32
        if r < PR:
            sumq[p, r // HD, r] = 1
        else:
            sumq[p, (r - PR) // HD, 32 + r - PR] = 1
    causal = np.zeros((64 + SEQ, SEQ), f)
    causal[:SEQ] = causal[64:] = np.where(np.tril(np.ones((SEQ, SEQ), bool)), 0, -PICKED)
    bf = mybir.dt.np(BF16)
    return {
        "rope_cos": np.cos(ang).astype(f), "rope_sin": np.sin(ang).astype(f), "ident": np.eye(D, dtype=f),
        "parity": (rows[:, None] // HD % 2 == np.arange(2)[None]).astype(f), "sumq": sumq,
        "headmask": (rows[:, None] // HD == np.arange(HEADS)[None]).astype(f),
        "ones8": (rows[:, None] // HD == rows[None] // HD).astype(f),
        "causal": causal,
        "query_rows": np.stack([np.zeros((PAIRS, 2 * SEQ)), np.ones((PAIRS, 2 * SEQ))]).astype(bf),
        "key_rows": np.stack([np.ones((PAIRS, KEYS)), np.zeros((PAIRS, KEYS))]).astype(bf),
        "ones_rows": np.ones((SHARED // I0, TOKENS), f), "b2_or_zero0": np.zeros((E1, D), f),
    }


def kernel(**inputs):
    import concourse.bacc as bacc
    from concourse.bass_utils import run_bass_kernel_spmd

    a = {k: np.asarray(v) for k, v in inputs.items()}
    c = np.ascontiguousarray
    I = shape_constants()
    x = a["x"].reshape(TOKENS, D)
    I.update(x=c(x), xT=c(x.T), ctxT=c(a["ctx_1024"].transpose(0, 2, 1)), mask=c(a["mask_BxS2_bk0"]).view(np.int32))
    for n in ("L0_attn_Wq", "L0_attn_bq", "L0_attn_Wdown", "L0_attn_bdown", "L0_attn_Wup", "L0_attn_bup", "L0_attn_Wout",
              "L0_attn_bout", "L0_xattn_bq", "L0_xattn_bk", "L0_xattn_bv", "L0_xattn_bo", "L0_ffn_correction_bias",
              "L1_xattn_Wq", "L1_xattn_bq", "L1_xattn_bk", "L1_xattn_bv", "L1_xattn_bo"):
        I[n] = c(a[n])
    for n in ("L0_xattn_Wq", "L0_xattn_Wk", "L0_xattn_Wv", "L0_xattn_Wo", "L1_attn_Wq", "L1_attn_Wk", "L1_attn_Wv", "L1_attn_Wo"):
        I[n + "T"] = c(a[n].T)
    for n in ("Wk", "Wv", "Wo"):
        I[f"L1_xattn_{n}T"] = c(a[f"L1_xattn_{n}"])
    I["temperature_rows"] = np.repeat(a["L0_xattn_temperature"].reshape(HEADS), HD)
    I["q_scale_rows"], I["k_scale_rows"] = np.repeat(a["L1_attn_q_scale"], HD), np.repeat(a["L1_attn_k_scale"], HD)
    I["router0"], I["router1"] = c(a["L0_ffn_router_w"].T), c(a["L1_ffn_W_gate"])
    up = np.concatenate([a["L0_ffn_up_w"].transpose(1, 0, 2).reshape(D, E0 * I0), a["L0_ffn_shared_up_w"]], axis=1)
    I["up0"] = c(up.reshape(D, NCH0, 128).transpose(1, 0, 2))
    I["down0"] = np.concatenate([a["L0_ffn_down_w"].reshape(E0 * I0, D), a["L0_ffn_shared_down_w"]]).reshape(NCH0, 128, D)
    n = I1 // 128
    I["up1"] = c(a["L1_ffn_W1"].reshape(E1, D, n, 128).transpose(0, 2, 1, 3).reshape(NCH1, D, 128))
    I["down1"] = c(a["L1_ffn_W2"].reshape(NCH1, 128, D))
    I["b1"] = c(a["L1_ffn_b1"].reshape(NCH1, 128, 1))
    I["b2_or_zero1"] = c(a["L1_ffn_b2"])

    nc = bacc.Bacc("TRN2", target_bir_lowering=False, num_devices=1)
    arrays = {f"in_{k}": v for k, v in I.items()}
    aps = {k: nc.dram_tensor(f"in_{k}", v.shape, mybir.dt.from_np(v.dtype), kind="ExternalInput").ap() for k, v in I.items()}
    out = nc.dram_tensor("out_0", (TOKENS, D), F32, kind="ExternalOutput").ap()
    decoder(nc, aps, out)
    r = run_bass_kernel_spmd(nc, [arrays], core_ids=[0])
    return r.results[0]["out_0"].reshape(SEQS, SEQ, D)
```

```python
from contextlib import ExitStack

import numpy as np

import concourse.bass as bass
from concourse import mybir

F32 = mybir.dt.float32
BF16 = mybir.dt.bfloat16
U8 = mybir.dt.uint8
ACT = mybir.ActivationFunctionType
ALU = mybir.AluOpType
AX = mybir.AxisListType.X

SEQS, SEQ, D = 32, 56, 128
HEADS, HD = 16, 8
KEYS = 1500
TOKENS = SEQS * SEQ
TILE = 2 * SEQ
TILES = 4
GROUP = TILE * TILES
GROUPS = TOKENS // GROUP
GSEQS = GROUP // SEQ
LANES = 2
TURNS = GROUPS // LANES
PAIRS = HEADS // 2
PR = 2 * HD
CH = 125
CHUNKS = KEYS // CH
KB = 500
KBANKS = KEYS // KB
CB = CHUNKS // KBANKS
PROD = 6
SROWS = PR * PROD
SHIFT_ROW, MASK_ROW = SROWS, SROWS + 1
STACK = SROWS + 2
E0, I0, K0, G0 = 64, 64, 8, 8
SHARED = 256
NCH0 = (E0 * I0 + SHARED) // 128
E1, I1 = 8, 512
NCH1 = E1 * I1 // 128
EPS = 1e-5
PICKED = 1e30
ABSENT = -3e38


class Steps:

    def __init__(self, sem, names):
        self.sem, self.names, self.k = sem, names.split(), 0
        assert len(set(self.names)) == len(self.names)
        self.per = len(self.names)

    def at(self, t, name):
        return t * self.per + (self.names.index(name) + 1)

    def one(self, name):
        assert self.names[self.k % self.per] == name, (self.names[self.k % self.per], name)
        self.k += 1
        return 1

    def turns(self, t):
        return t * self.per


class LaneSteps:

    def __init__(self, sem, names):
        order = [f"{n}.{b}" for part in names.split("|") for b in range(LANES) for n in part.split()]
        self.steps = Steps(sem, " ".join(order))

    def lane(self, b):
        return OneLane(self.steps, b)


class OneLane:

    def __init__(self, steps, b):
        self.steps, self.sem, self.b = steps, steps.sem, b

    def at(self, t, name):
        return self.steps.at(t, f"{name}.{self.b}")

    def one(self, name):
        return self.steps.one(f"{name}.{self.b}")


def bc(ap, n, axis):
    shape = list(ap.shape)
    shape.insert(axis, n)
    return ap.unsqueeze(axis).broadcast_to(shape)


class Stage:

    def __init__(self, nc, name):
        self.nc, self.name, self.ctx = nc, name, ExitStack()

    def sb(self, name, shape, dt=F32):
        return self.ctx.enter_context(self.nc.sbuf_tensor(f"{self.name}_{name}", shape, dt))

    def sem(self, name):
        return self.ctx.enter_context(self.nc.semaphore(f"{self.name}_{name}"))

    def __enter__(self):
        return self

    def __exit__(self, *a):
        self.ctx.close()


def hold(e, sem, value):
    e.wait_ge(sem, value)
    e.nop(nofuse=True)


def tok_major(dram, t):
    return dram[bass.ds(t * GROUP, GROUP), :].rearrange("(s p) d -> p s d", p=TILE)


NORM_STATS, NORMED = "stats0 stats1 stats2 stats3 aggr0 aggr1 aggr2 aggr3 vareps", "normed0 normed1 normed2 normed3"


def norm_stats(v, V, t, r, stats, mv, ve):
    v.wait_ge(V.sem, V.at(t, "y_res"))
    for s in range(TILES):
        v.bn_stats(stats[:, s, :], r[:, s, :]).then_inc(V.sem, V.one(f"stats{s}"))
    hold(v, V.sem, V.at(t, "stats3"))
    for s in range(TILES):
        v.bn_aggr(mv[:, s, :], stats[:, s, :]).then_inc(V.sem, V.one(f"aggr{s}"))
    v.wait_ge(V.sem, V.at(t, "aggr3"))
    v.tensor_scalar(ve[:, :], mv[:, :, 1], EPS, None, ALU.add).then_inc(V.sem, V.one("vareps"))


def norm_apply(v, V, P, t, r, mv, rstd, out, x_stored):
    v.wait_ge(P.sem, P.at(t, "rstd"))
    v.wait_ge(x_stored, 16 + t * 16 * LANES)
    for s in range(TILES):
        v.tensor_scalar(out[:, s, :], r[:, s, :], mv[:, s, 0:1], rstd[:, s:s + 1], ALU.subtract,
                        ALU.mult).then_inc(V.sem, V.one(f"normed{s}"))


QUERY_STORES = 16 * 2 * GSEQS * LANES
FACTORS = "x_h x_m x_l x_h2"


def round_queries(a, A, P, t, qT, qh, qr, qm):
    a.wait_ge(A.sem, A.at(t, "qT"))
    a.copy(qh[:, :], qT[:, :]).then_inc(A.sem, A.one("q_h"))
    a.wait_ge(P.sem, P.at(t, "q_rest"))
    a.copy(qm[:, :], qr[:, :]).then_inc(A.sem, A.one("q_m"))


def rest_of_queries(p, P, A, t, qT, qh, qr, qm, ql):
    hold(p, A.sem, A.at(t, "q_h"))
    p.tensor_tensor(qr[:, :], qT[:, :], qh[:, :], ALU.subtract).then_inc(P.sem, P.one("q_rest"))
    hold(p, A.sem, A.at(t, "q_m"))
    p.tensor_tensor(ql[:, :], qr[:, :], qm[:, :], ALU.subtract).then_inc(P.sem, P.one("q_l"))


def expand_queries(e, E, A, P, t, qh, qm, ql, qx, parity, q_stored):
    hold(e, q_stored, 16 + t * QUERY_STORES)
    for part, c, n, name, S, after in ((qh, 0, 2, "x_h", A, "q_h"), (qm, 2, 2, "x_m", A, "q_m"),
                                       (ql, 4, 1, "x_l", P, "q_l"), (qh, 5, 1, "x_h2", A, "q_h")):
        hold(e, S.sem, S.at(t, after))
        for k in range(n):
            if E is P:
                last = e.tensor_tensor(qx[:, :, c + k, :, :].rearrange("p b h q -> p h b q"),
                                       bc(part[:, :].rearrange("p (b q) -> p b q", q=SEQ), 2, 1),
                                       bc(bc(parity[:, :], GSEQS, 2), SEQ, 3), ALU.mult)
            else:
                for h in range(2):
                    last = e.mul(qx[:, :, c + k, h, :], part[:, :].rearrange("p (b q) -> p b q", q=SEQ), parity[:, h:h + 1])
        last.then_inc(E.sem, E.one(name))


def store_queries(e, stored, t, qx_dram, qx):
    for b in range(GSEQS):
        for a in range(2):
            e.dma_start(qx_dram[t * GSEQS + b].rearrange("j (a r c) n -> a j r (c n)", a=2, r=PR)[a],
                        qx[:, b, 3 * a:3 * a + 3, :, :].rearrange("p c h q -> p (c h q)")).then_inc(stored, 16)


def load_all(e, sem, pairs):
    for dst, src in pairs:
        e.dma_start(dst, src).then_inc(sem, 16)
    return 16 * len(pairs)


def rows_of(vec, n=TILE):
    return vec.rearrange("(a d) -> a d", a=1).broadcast_to([n, vec.shape[0]])


def column(vec):
    return vec.rearrange("(d a) -> d a", a=1)


def self_attention_0(nc, bank, I, x1, qx_dram, consts):
    with Stage(nc, "sa0") as g:
        wq, wdn, wup, wout = g.sb("wq", [D, D]), g.sb("wdn", [D, 32]), g.sb("wup", [32, 2 * D]), g.sb("wout", [D, D])
        bq, bup, bout = g.sb("bq", [TILE, D]), g.sb("bup", [TILE, 2 * D]), g.sb("bout", [TILE, D])
        bdn, wq1 = g.sb("bdn", [32, 1]), g.sb("wq1", [D, D])
        cos, sin = g.sb("cos", [TILE, 4]), g.sb("sin", [TILE, 4])
        qb1, temp, qs, qbs = g.sb("qb1", [D, 1]), g.sb("temp", [D, 1]), g.sb("qs", [D, 1]), g.sb("qbs", [D, 1])
        parity, ident = consts["parity"], consts["ident"]
        ta, tb = g.sb("ta", [TILE, 64, 4]), g.sb("tb", [TILE, 64, 4])
        half = consts["minus_half"]
        weights, loaded = g.sem("weights_loaded"), g.sem("group_loaded")
        x_stored, q_stored = g.sem("weight_loaded_x_stored"), g.sem("weight_loaded_queries_stored")
        consts_ready = g.sem("query_scale_ready")
        T = LaneSteps(g.sem("tensor_steps"), "q_ps lat_ps | kv_ps | oT_ps | y_ps | xT_ps | qT_ps")
        A = LaneSteps(g.sem("scalar_steps"), "lat | exp | oT | xT | qT q_h q_m")
        V = LaneSteps(g.sem("vector_steps"), "q | kv_a kv_b q1c q2s q1 q2c q1s q2 k1c k2s k1 k2c k1s k2 prod0 prod1 "
                  "| S0 S1 S2 S3 max shifted | sum inv P vprod0 vprod1 | o0 o1 o2 o3 | y_bias y_res " + NORM_STATS + " | " + NORMED)
        P = LaneSteps(g.sem("gpsimd_steps"), "prod2 prod3 | vprod2 vprod3 | rstd | q_rest q_l " + FACTORS)
        nw = [0]
        lanes = [dict(T=T.lane(b), A=A.lane(b), V=V.lane(b), P=P.lane(b), bank=bank[4 * b:4 * b + 4],
                      **{n: g.sb(f"{n}{b}", *shape) for n, shape in {
                          "X": ([TILE, TILES, D],), "XT": ([D, GROUP],), "lat": ([32, GROUP],), "q": ([TILE, TILES, D],), "kv": ([TILE, TILES, 2 * D],),
                          "qr": ([TILE, TILES, D],), "kr": ([TILE, TILES, D],), "prod": ([TILE, TILES, 2048],), "S": ([TILE, TILES, 256],),
                          "mx": ([TILE, 64],), "den": ([TILE, 64],), "o": ([TILE, TILES, D],), "oT": ([D, GROUP],), "r": ([TILE, TILES, D],), "xn": ([TILE, TILES, D],),
                          "xT1": ([D, GROUP],), "qT": ([D, GROUP],), "qh": ([D, GROUP], BF16), "qm": ([D, GROUP], BF16), "ql": ([D, GROUP], BF16), "qrest": ([D, GROUP],),
                          "qx": ([D, GSEQS, PROD, 2, SEQ], BF16), "stats": ([TILE, 4, 6],), "mv": ([TILE, 4, 2],), "ve": ([TILE, 4],), "rstd": ([TILE, 4],),
                      }.items()}) for b in range(LANES)]
        with nc.Block() as block:
            @block.sync
            def _(e):
                nw[0] = load_all(e, weights, [
                    (wq[:, :], I["L0_attn_Wq"]), (wdn[:, :], I["L0_attn_Wdown"]), (wup[:, :], I["L0_attn_Wup"]),
                    (bq[:, :], rows_of(I["L0_attn_bq"])),
                    (bup[:, :], rows_of(I["L0_attn_bup"])), (bout[:, :], rows_of(I["L0_attn_bout"])),
                    (bdn[:, :], column(I["L0_attn_bdown"])),
                    (cos[:, :], I["rope_cos"]), (sin[:, :], I["rope_sin"]), (qb1[:, :], column(I["L0_xattn_bq"])),
                    (temp[:, :], column(I["temperature_rows"]))])
                load_all(e, x_stored, [(wout[:, :], I["L0_attn_Wout"])])
                load_all(e, q_stored, [(wq1[:, :], I["L0_xattn_WqT"])])

                def load(t, b, c):
                    at = t * LANES + b
                    e.dma_start(c["X"][:, :, :], tok_major(I["x"], at)).then_inc(loaded, 16)
                    e.dma_start(c["XT"][:, :], I["xT"][:, bass.ds(at * GROUP, GROUP)]).then_inc(loaded, 16)

                def store_x(t, b, c):
                    hold(e, c["V"].sem, c["V"].at(t, "normed3"))
                    e.dma_start(tok_major(x1, t * LANES + b), c["xn"][:, :, :]).then_inc(x_stored, 16)

                def store_rest(t, b, c):
                    at = t * LANES + b
                    hold(e, c["P"].sem, c["P"].at(t, "x_h2"))
                    store_queries(e, q_stored, at, qx_dram, c["qx"])

                for b, c in enumerate(lanes):
                    load(0, b, c)
                with e.Fori(0, TURNS - 1) as t:
                    for b, c in enumerate(lanes):
                        hold(e, c["V"].sem, c["V"].at(t, "y_res"))
                        load(t + 1, b, c)
                    for b, c in enumerate(lanes):
                        store_x(t, b, c)
                    for b, c in enumerate(lanes):
                        store_rest(t, b, c)
                for b, c in enumerate(lanes):
                    store_x(TURNS - 1, b, c)
                for b, c in enumerate(lanes):
                    store_rest(TURNS - 1, b, c)
                hold(e, x_stored, 16 * (1 + GROUPS))
                hold(e, q_stored, 16 + TURNS * QUERY_STORES)

            @block.tensor
            def _(e):
                e.wait_ge(weights, nw[0])
                for sem in (x_stored, q_stored):
                    e.wait_ge(sem, 16)
                with e.Fori(0, TURNS) as t:
                    for c in lanes:
                        e.wait_ge(loaded, (t + 1) * 32 * LANES)
                        for s in range(TILES):
                            m = e.matmul(c["bank"][0][0:TILE, s * D:(s + 1) * D], c["XT"][:, s * TILE:(s + 1) * TILE], wq[:, :], start=True, stop=True)
                        m.then_inc(c["T"].sem, c["T"].one("q_ps"))
                        e.matmul(c["bank"][1][0:32, 0:GROUP], wdn[:, :], c["XT"][:, :], start=True, stop=True).then_inc(c["T"].sem, c["T"].one("lat_ps"))
                    for c in lanes:
                        e.wait_ge(c["A"].sem, c["A"].at(t, "lat"))
                        for s in range(TILES):
                            m = e.matmul(c["bank"][2 + s // 2][0:TILE, s % 2 * 256:s % 2 * 256 + 256], c["lat"][:, s * TILE:(s + 1) * TILE], wup[:, :], start=True, stop=True)
                        m.then_inc(c["T"].sem, c["T"].one("kv_ps"))
                    for c in lanes:
                        e.wait_ge(c["V"].sem, c["V"].at(t, "o3"))
                        for s in range(TILES):
                            m = e.transpose(c["bank"][0][:, s * TILE:(s + 1) * TILE], c["o"][:, s, :], ident[0:TILE, 0:TILE])
                        m.then_inc(c["T"].sem, c["T"].one("oT_ps"))
                    for c in lanes:
                        e.wait_ge(c["A"].sem, c["A"].at(t, "oT"))
                        for s in range(TILES):
                            m = e.matmul(c["bank"][1][0:TILE, s * D:(s + 1) * D], c["oT"][:, s * TILE:(s + 1) * TILE], wout[:, :], start=True, stop=True)
                        m.then_inc(c["T"].sem, c["T"].one("y_ps"))
                    for c in lanes:
                        e.wait_ge(c["V"].sem, c["V"].at(t, "normed3"))
                        for s in range(TILES):
                            m = e.transpose(c["bank"][2][:, s * TILE:(s + 1) * TILE], c["xn"][:, s, :], ident[0:TILE, 0:TILE])
                        m.then_inc(c["T"].sem, c["T"].one("xT_ps"))
                    for c in lanes:
                        e.wait_ge(c["A"].sem, c["A"].at(t, "xT"))
                        e.matmul(c["bank"][3][:, 0:GROUP], wq1[:, :], c["xT1"][:, :], start=True, stop=True).then_inc(c["T"].sem, c["T"].one("qT_ps"))

            @block.scalar
            def _(e):
                e.wait_ge(weights, nw[0])
                e.wait_ge(consts_ready, 3)
                with e.Fori(0, TURNS) as t:
                    for c in lanes:
                        e.wait_ge(loaded, (t + 1) * 32 * LANES)
                        e.wait_ge(c["T"].sem, c["T"].at(t, "lat_ps"))
                        e.activation(c["lat"][:, :], c["bank"][1][0:32, 0:GROUP], ACT.Identity, bias=bdn[:, :]).then_inc(c["A"].sem, c["A"].one("lat"))
                    for c in lanes:
                        e.wait_ge(c["V"].sem, c["V"].at(t, "shifted"))
                        e.activation(c["S"][:, :, :], c["S"][:, :, :], ACT.Exp, scale=HD ** -0.5).then_inc(c["A"].sem, c["A"].one("exp"))
                    for c in lanes:
                        e.wait_ge(c["T"].sem, c["T"].at(t, "oT_ps"))
                        e.copy(c["oT"][:, :], c["bank"][0][:, 0:GROUP]).then_inc(c["A"].sem, c["A"].one("oT"))
                    for c in lanes:
                        e.wait_ge(c["T"].sem, c["T"].at(t, "xT_ps"))
                        e.copy(c["xT1"][:, :], c["bank"][2][:, 0:GROUP]).then_inc(c["A"].sem, c["A"].one("xT"))
                    for c in lanes:
                        e.wait_ge(c["T"].sem, c["T"].at(t, "qT_ps"))
                        e.activation(c["qT"][:, :], c["bank"][3][:, 0:GROUP], ACT.Identity, bias=qbs[:, :], scale=qs[:, :]).then_inc(c["A"].sem, c["A"].one("qT"))
                        round_queries(e, c["A"], c["P"], t, c["qT"], c["qh"], c["qrest"], c["qm"])

            def per_head(S):
                return S[:, :, :].rearrange("p s (h g) -> p (s h) g", g=HEADS)

            def head_view(x, s):
                return x[:, s, :].rearrange("p (h d) -> p h d", d=HD)

            def score_product(e, c, s):
                return e.tensor_tensor(c["prod"][:, s, :].rearrange("p (h g d) -> p h g d", h=HEADS, g=HEADS),
                                       bc(head_view(c["qr"], s), HEADS, 2), bc(head_view(c["kr"], s), HEADS, 1), ALU.mult)

            def value_product(e, c, s):
                v = c["kv"][:, s, :].rearrange("p (g d) -> p d g", d=2 * HD)[:, HD:2 * HD, :]
                return e.tensor_tensor(c["prod"][:, s, :].rearrange("p (h d g) -> p h d g", h=HEADS, d=HD),
                                       bc(c["S"][:, s, :].rearrange("p (h g) -> p h g", g=HEADS), HD, 2), bc(v, HEADS, 1), ALU.mult)

            @block.vector
            def _(e):
                e.wait_ge(weights, nw[0])
                e.reciprocal(temp[:, :], temp[:, :]).then_inc(consts_ready, 1)
                e.wait_ge(consts_ready, 1)
                e.tensor_scalar(qs[:, :], temp[:, :], HD ** -0.5, None, ALU.mult).then_inc(consts_ready, 1)
                e.wait_ge(consts_ready, 2)
                e.tensor_tensor(qbs[:, :], qb1[:, :], qs[:, :], ALU.mult).then_inc(consts_ready, 1)
                with e.Fori(0, TURNS) as t:
                    for c in lanes:
                        e.wait_ge(loaded, (t + 1) * 32 * LANES)
                        e.wait_ge(c["T"].sem, c["T"].at(t, "q_ps"))
                        ps4 = lambda b: c["bank"][b][0:TILE, :].rearrange("p (s d) -> p s d", s=TILES)
                        e.tensor_tensor(c["q"][:, :, :], ps4(0), bc(bq[:, :], TILES, 1), ALU.add).then_inc(c["V"].sem, c["V"].one("q"))
                    for c in lanes:
                        e.wait_ge(c["T"].sem, c["T"].at(t, "kv_ps"))
                        for i, n in enumerate(("kv_a", "kv_b")):
                            e.tensor_tensor(c["kv"][:, 2 * i:2 * i + 2, :], c["bank"][2 + i][0:TILE, :].rearrange("p (s d) -> p s d", s=2),
                                            bc(bup[:, :], 2, 1), ALU.add).then_inc(c["V"].sem, c["V"].one(n))
                        qv = c["q"][:, :, :].rearrange("p s (h d) -> p (s h) d", d=HD)
                        kk = c["kv"][:, :, :].rearrange("p s (h d) -> p (s h) d", d=2 * HD)
                        for x, y, n, before in ((qv, c["qr"], "q", "q"), (kk, c["kr"], "k", "kv_b")):
                            yv = y[:, :, :].rearrange("p s (h d) -> p (s h) d", d=HD)
                            cs, sn = bc(cos[:, :], 64, 1), bc(sin[:, :], 64, 1)
                            e.wait_ge(c["V"].sem, c["V"].at(t, before))
                            for _, _, half_, op in ((cs, sn, 0, ALU.subtract), (sn, cs, 1, ALU.add)):
                                na, nb = (f"{n}1c", f"{n}2s") if half_ == 0 else (f"{n}2c", f"{n}1s")
                                first, second = (x[:, :, 0:4], x[:, :, 4:8]) if half_ == 0 else (x[:, :, 4:8], x[:, :, 0:4])
                                if half_ or n == "k":
                                    e.wait_ge(c["V"].sem, c["V"].at(t, f"{n}1" if half_ else "q2"))
                                e.tensor_tensor(ta[:, :, :], first, cs, ALU.mult).then_inc(c["V"].sem, c["V"].one(na))
                                e.tensor_tensor(tb[:, :, :], second, sn, ALU.mult).then_inc(c["V"].sem, c["V"].one(nb))
                                e.wait_ge(c["V"].sem, c["V"].at(t, nb))
                                e.tensor_tensor(yv[:, :, 4 * half_:4 * half_ + 4], ta[:, :, :], tb[:, :, :], op).then_inc(c["V"].sem, c["V"].one(f"{n}{half_ + 1}"))
                        e.wait_ge(c["V"].sem, c["V"].at(t, "k2"))
                        for s in range(2):
                            score_product(e, c, s).then_inc(c["V"].sem, c["V"].one(f"prod{s}"))
                    for c in lanes:
                        for s in range(TILES):
                            if s < 2:
                                e.wait_ge(c["V"].sem, c["V"].at(t, f"prod{s}"))
                            else:
                                e.wait_ge(c["P"].sem, c["P"].at(t, f"prod{s}"))
                            e.tensor_reduce(c["S"][:, s, :], c["prod"][:, s, :].rearrange("p (a d) -> p a d", d=HD), AX, ALU.add).then_inc(c["V"].sem, c["V"].one(f"S{s}"))
                        e.wait_ge(c["V"].sem, c["V"].at(t, "S3"))
                        e.tensor_reduce(c["mx"][:, :], per_head(c["S"]), AX, ALU.max).then_inc(c["V"].sem, c["V"].one("max"))
                        e.wait_ge(c["V"].sem, c["V"].at(t, "max"))
                        e.tensor_tensor(per_head(c["S"]), per_head(c["S"]), bc(c["mx"][:, :], HEADS, 2), ALU.subtract).then_inc(c["V"].sem, c["V"].one("shifted"))
                    for c in lanes:
                        e.wait_ge(c["A"].sem, c["A"].at(t, "exp"))
                        e.tensor_reduce(c["den"][:, :], per_head(c["S"]), AX, ALU.add).then_inc(c["V"].sem, c["V"].one("sum"))
                        e.wait_ge(c["V"].sem, c["V"].at(t, "sum"))
                        e.reciprocal(c["den"][:, :], c["den"][:, :]).then_inc(c["V"].sem, c["V"].one("inv"))
                        e.wait_ge(c["V"].sem, c["V"].at(t, "inv"))
                        e.tensor_tensor(per_head(c["S"]), per_head(c["S"]), bc(c["den"][:, :], HEADS, 2), ALU.mult).then_inc(c["V"].sem, c["V"].one("P"))
                        e.wait_ge(c["V"].sem, c["V"].at(t, "P"))
                        for s in range(2):
                            value_product(e, c, s).then_inc(c["V"].sem, c["V"].one(f"vprod{s}"))
                    for c in lanes:
                        for s in range(TILES):
                            if s < 2:
                                e.wait_ge(c["V"].sem, c["V"].at(t, f"vprod{s}"))
                            else:
                                e.wait_ge(c["P"].sem, c["P"].at(t, f"vprod{s}"))
                            e.tensor_reduce(c["o"][:, s, :], c["prod"][:, s, :].rearrange("p (a g) -> p a g", g=HEADS), AX, ALU.add).then_inc(c["V"].sem, c["V"].one(f"o{s}"))
                    for c in lanes:
                        e.wait_ge(c["T"].sem, c["T"].at(t, "y_ps"))
                        e.tensor_tensor(c["r"][:, :, :], ps4(1), bc(bout[:, :], TILES, 1), ALU.add).then_inc(c["V"].sem, c["V"].one("y_bias"))
                        e.wait_ge(c["V"].sem, c["V"].at(t, "y_bias"))
                        e.tensor_tensor(c["r"][:, :, :], c["r"][:, :, :], c["X"][:, :, :], ALU.add).then_inc(c["V"].sem, c["V"].one("y_res"))
                        norm_stats(e, c["V"], t, c["r"], c["stats"], c["mv"], c["ve"])
                    for c in lanes:
                        norm_apply(e, c["V"], c["P"], t, c["r"], c["mv"], c["rstd"], c["xn"], x_stored)

            @block.gpsimd
            def _(e):
                with e.Fori(0, TURNS) as t:
                    for c in lanes:
                        e.wait_ge(c["V"].sem, c["V"].at(t, "k2"))
                        for s in (2, 3):
                            score_product(e, c, s).then_inc(c["P"].sem, c["P"].one(f"prod{s}"))
                    for c in lanes:
                        e.wait_ge(c["V"].sem, c["V"].at(t, "P"))
                        for s in (2, 3):
                            value_product(e, c, s).then_inc(c["P"].sem, c["P"].one(f"vprod{s}"))
                    for c in lanes:
                        e.wait_ge(c["V"].sem, c["V"].at(t, "vareps"))
                        e.tensor_tensor(c["rstd"][:, :], c["ve"][:, :], half[0:TILE, :], ALU.pow).then_inc(c["P"].sem, c["P"].one("rstd"))
                    for c in lanes:
                        rest_of_queries(e, c["P"], c["A"], t, c["qT"], c["qh"], c["qrest"], c["qm"], c["ql"])
                        expand_queries(e, c["P"], c["A"], c["P"], t, c["qh"], c["qm"], c["ql"], c["qx"], parity, q_stored)


def cross_attention(nc, bank, name, W, qx_dram, mask_rows, at_dram, den_dram, consts, I):
    UT = 2 * PAIRS
    TURNS = SEQS // 2
    LAG = 2
    SUM_AT, K_AT, V_AT = 1, (2, 3, 4), (5, 6, 7)
    SCORES, PV, MISC = 3, 6, 7
    Q = 2 * SEQ
    SHIFT = KBANKS - 1
    with Stage(nc, name) as g:
        wk, wv, bk = g.sb("wk", [D, D]), g.sb("wv", [D, D]), g.sb("bk", [D, 1])
        ctx = [g.sb(f"ctx{i}", [D, KEYS]) for i in range(2)]
        kf, krest = g.sb("kf", [D, KEYS]), g.sb("krest", [D, KB])
        kp = [g.sb(f"kparts{i}", [D, 4, KEYS], BF16) for i in range(2)]
        ks = [g.sb(f"kstack{i}", [STACK, PAIRS, KEYS], BF16) for i in range(2)]
        qs = [g.sb(f"qstack{i}", [STACK, PAIRS, Q], BF16) for i in range(2)]
        vs = [g.sb(f"v{i}", [CH, CHUNKS, PAIRS, 2 * PR]) for i in range(2)]
        pt = [g.sb(f"probs{i}", [CH, CB, Q]) for i in range(KBANKS)]
        mx3 = [g.sb(f"mx3_{i}", [Q, KBANKS]) for i in range(2)]
        nmx = [g.sb(f"nmx{i}", [Q, 1], BF16) for i in range(2)]
        pv = [g.sb(f"pv{i}", [D, PAIRS, 2, SEQ]) for i in range(2)]
        att = g.sb("att", [48, PAIRS * SEQ])
        identb, sumq = consts["identb"], consts["sumq"]
        S = {n: g.sem(n) for n in (
            "weights_loaded", "rows_loaded", "ones_set", "ctx_loaded0", "ctx_loaded1", "k_ps", "k_f32", "k_rounded", "v_ps",
            "v_copied", "q_loaded0", "q_loaded1", "max_ps", "bank_max", "unit_max", "shift_ps", "shift_row",
            "score_ps", "probs", "pv_ps", "pv_copied", "sum_ps", "summed", "bias_loaded_sums_stored")}
        k_stacked = [[g.sem(f"k_stacked{i}_half{j}") for j in range(2)] for i in range(2)]
        P = Steps(g.sem("split_steps"), " ".join(f"rest{n} m{n} l{n} hh{n}" for n in range(KBANKS)))
        KDMA = 16 * PAIRS
        QDMA = 48 if mask_rows is not None else 32

        def turns(e, slot):
            for w in range(UT):
                slot(e, 0, w, True, False)
            with e.Fori(1, TURNS - 1) as i:
                for w in range(UT):
                    slot(e, i, w, False, False)
            for w in range(UT):
                slot(e, TURNS - 1, w, False, True)

        def keys_matmul(e, b, n):
            e.matmul(bank[MISC][:, 0:KB], wk[:, :], ctx[b][:, n * KB:(n + 1) * KB],
                     start=True, stop=True).then_inc(S["k_ps"], 1)

        def values_matmul(e, b, n):
            for c in range(CB):
                lo = (n * CB + c) * CH
                m = e.matmul(bank[MISC][0:CH, c * D:(c + 1) * D], ctx[b][:, lo:lo + CH], wv[:, :], start=True, stop=True)
            m.then_inc(S["v_ps"], 1)

        def scores_matmul(e, u, b, j, k, first_unit):
            if k == 0:
                e.wait_ge(S["shift_row"], u + 1)
            if not first_unit:
                e.wait_ge(S["probs"], (u - 1) * KBANKS + k + 1)
            for c in range(CB):
                lo = (k * CB + c) * CH
                m = e.matmul(bank[SCORES + k][0:CH, c * Q:(c + 1) * Q], ks[b][:, j, lo:lo + CH], qs[b][:, j, :],
                             start=True, stop=True)
            m.then_inc(S["score_ps"], 1)

        def pv_matmul(e, u, b, j, k, first_unit):
            e.wait_ge(S["probs"], u * KBANKS + k + 1)
            if k == 0 and not first_unit:
                e.wait_ge(S["pv_copied"], u)
            for c in range(CB):
                m = e.matmul(bank[PV][32 * c:32 * c + 2 * PR, 0:Q], vs[b][:, k * CB + c, j, :], pt[k][:, c, :],
                             start=(k == 0), stop=(k == KBANKS - 1))
            m.then_inc(S["pv_ps"], 1)

        def shift_matmul(e, u, j):
            e.wait_ge(S["unit_max"], u + 1)
            e.matmul(bank[SHIFT][SHIFT_ROW:SHIFT_ROW + 1, 0:Q], nmx[j % 2][:, :], identb[0:Q, 0:Q],
                     start=True, stop=True).then_inc(S["shift_ps"], 1)

        def sum_matmul(e, b):
            for hh in range(2):
                m = e.matmul(bank[MISC][0:48, 0:PAIRS * SEQ], sumq[:, hh, :], pv[b][:, :, hh, :],
                             start=(hh == 0), stop=(hh == 1))
            m.then_inc(S["sum_ps"], 1)

        def tensor_slot(e, i, w, first, last):
            b, j = w // PAIRS, w % PAIRS
            seq, u = i * 2 + b, i * UT + w
            lb, lj, lu = (w - LAG) % UT // PAIRS, (w - LAG) % PAIRS, u - LAG
            pb, pj, pu = (w - LAG - 1) % UT // PAIRS, (w - LAG - 1) % PAIRS, lu - 1
            more = not (last and b == 1)
            for k in range(KBANKS):
                if k == 0:
                    if j % (PAIRS // 2) == 0:
                        e.wait_ge(k_stacked[b][j // (PAIRS // 2)], (i + 1) * KDMA)
                    if j == 0:
                        e.wait_ge(S[f"q_loaded{b}"], (i + 1) * QDMA)
                if not (first and w == 0):
                    e.wait_ge(S["bank_max"], (u - 1) * KBANKS + k + 1)
                    if k == SHIFT:
                        e.wait_ge(S["shift_row"], u)
                e.matmul(bank[k][0:Q, 0:KB], qs[b][:, j, :], ks[b][:, j, k * KB:(k + 1) * KB],
                         start=True, stop=True).then_inc(S["max_ps"], 1)
                if not (first and w < LAG):
                    scores_matmul(e, lu, lb, lj, k, first and w == LAG)
                if k < 2 and not (first and w < LAG + 1):
                    pv_matmul(e, pu, pb, pj, k + 1, first and w == LAG + 1)
                if k == 0 and not (first and w == 0):
                    shift_matmul(e, u - 1, (j - 1) % 2)
            if not (first and w == 0):
                spare_read(e, seq, b, j, first, last)
            if j in K_AT and not last:
                if j == K_AT[0]:
                    e.wait_ge(S[f"ctx_loaded{b}"], (i + 2) * 16)
                keys_matmul(e, b, K_AT.index(j))
            if j in V_AT and more:
                values_matmul(e, 1 - b, V_AT.index(j))
            if j == SUM_AT and not first:
                e.wait_ge(S["pv_copied"], (seq - 1) * PAIRS)
                sum_matmul(e, b)
            if not (first and w < LAG):
                if lj == 0:
                    e.wait_ge(S["v_copied"], (seq + 1) * KBANKS)
                pv_matmul(e, lu, lb, lj, 0, first and w == LAG)

        def spare_read(e, seq, b, j, first, last):
            if j - 1 == SUM_AT and not first:
                e.wait_ge(S["summed"], seq - 1)
            if j - 1 in K_AT and not last:
                e.wait_ge(S["k_f32"], (seq + 2) * KBANKS + K_AT.index(j - 1) + 1)
            if j - 1 in V_AT and not (last and b == 1):
                e.wait_ge(S["v_copied"], (seq + 1) * KBANKS + V_AT.index(j - 1) + 1)
            if j == 0:
                e.wait_ge(S["v_copied"], (seq + 1) * KBANKS)

        def key_copy(e, seq, n):
            e.wait_ge(S["k_ps"], seq * KBANKS + n + 1)
            if not (isinstance(seq, int) and seq == 0):
                e.wait_ge(P.sem, P.at(seq - 1, f"hh{n}"))
            e.activation(kf[:, n * KB:(n + 1) * KB], bank[MISC][:, 0:KB], ACT.Identity, bias=bk[:, :]).then_inc(S["k_f32"], 1)


        def value_copy(e, seq, b, n):
            e.wait_ge(S["v_ps"], seq * KBANKS + n + 1)
            e.copy(vs[b][:, n * CB:(n + 1) * CB, :, 0:PR],
                   bank[MISC][0:CH, :].rearrange("p (c j r) -> p c j r", c=CB, r=PR)).then_inc(S["v_copied"], 1)

        def exp_bank(e, u, k, first_unit):
            e.wait_ge(S["score_ps"], u * KBANKS + k + 1)
            if not first_unit:
                e.wait_ge(S["pv_ps"], (u - 1) * KBANKS + k + 1)
            e.activation(pt[k][:, :, :], bank[SCORES + k][0:CH, 0:CB * Q].rearrange("p (c q) -> p c q", c=CB),
                         ACT.Exp).then_inc(S["probs"], 1)

        def pv_copy(e, u, b, j):
            e.wait_ge(S["pv_ps"], (u + 1) * KBANKS)
            e.copy(pv[b][:, j, :, :], bank[PV][:, 0:Q].rearrange("p (h q) -> p h q", h=2)).then_inc(S["pv_copied"], 1)

        def sum_copy(e, seq):
            e.wait_ge(S["sum_ps"], seq + 1)
            e.wait_ge(S["bias_loaded_sums_stored"], 16 + seq * 32)
            e.copy(att[:, :], bank[MISC][0:48, 0:PAIRS * SEQ]).then_inc(S["summed"], 1)

        def scalar_slot(e, i, w, first, last):
            b, j = w // PAIRS, w % PAIRS
            seq, u = i * 2 + b, i * UT + w
            pb, pj, pu = (w - LAG - 1) % UT // PAIRS, (w - LAG - 1) % PAIRS, u - LAG - 1
            more = not (last and b == 1)
            for k in range(KBANKS):
                if not (first and w < LAG):
                    exp_bank(e, u - LAG, k, first and w == LAG)
                if k == 0:
                    if j == 0 and not (first and b == 0):
                        value_copy(e, seq, b, KBANKS - 1)
                    if j - 1 == SUM_AT and not first:
                        sum_copy(e, seq - 2)
                    if j - 1 in K_AT and not last:
                        key_copy(e, seq + 2, K_AT.index(j - 1))
                    if j - 1 in V_AT and more:
                        value_copy(e, seq + 1, 1 - b, V_AT.index(j - 1))
                if k == 1 and not (first and w < LAG + 1):
                    if pj == 0 and not first:
                        e.wait_ge(S["sum_ps"], seq - 1)
                    pv_copy(e, pu, pb, pj)

        def key_round(e, seq, b, n, turn):
            e.wait_ge(S["k_f32"], seq * KBANKS + n + 1)
            if turn is not None and n == 0:
                for half in range(2):
                    e.wait_ge(k_stacked[b][half], (turn + 1) * KDMA)
            e.tensor_copy(kp[b][:, 0, n * KB:(n + 1) * KB], kf[:, n * KB:(n + 1) * KB]).then_inc(S["k_rounded"], 1)

        def shift_copy(e, u, b, j):
            e.wait_ge(S["shift_ps"], u + 1)
            e.tensor_copy(qs[b][SHIFT_ROW:SHIFT_ROW + 1, j, :], bank[SHIFT][SHIFT_ROW:SHIFT_ROW + 1, 0:Q]).then_inc(S["shift_row"], 1)

        def vector_slot(e, i, w, first, last):
            b, j = w // PAIRS, w % PAIRS
            seq, u = i * 2 + b, i * UT + w
            for k in range(KBANKS):
                e.wait_ge(S["max_ps"], u * KBANKS + k + 1)
                e.tensor_reduce(mx3[w % 2][:, k:k + 1], bank[k][0:Q, 0:KB], AX, ALU.max).then_inc(S["bank_max"], 1)
                if k == 0 and not (first and w == 0):
                    shift_copy(e, u - 1, (w - 1) % UT // PAIRS, (w - 1) % PAIRS)
                if k == 1 and j - 1 in K_AT and not last:
                    key_round(e, seq + 2, b, K_AT.index(j - 1), i)
            e.wait_ge(S["bank_max"], (u + 1) * KBANKS)
            e.tensor_reduce(nmx[w % 2][:, :], mx3[w % 2][:, :], AX, ALU.max, negate=True).then_inc(S["unit_max"], 1)

        def split_keys(e, seq, b):
            for n in range(KBANKS):
                cols = slice(n * KB, (n + 1) * KB)
                hold(e, S["k_rounded"], seq * KBANKS + n + 1)
                e.tensor_tensor(krest[:, :], kf[:, cols], kp[b][:, 0, cols], ALU.subtract).then_inc(P.sem, P.one(f"rest{n}"))
                hold(e, P.sem, P.at(seq, f"rest{n}"))
                e.tensor_copy(kp[b][:, 1, cols], krest[:, :]).then_inc(P.sem, P.one(f"m{n}"))
                hold(e, P.sem, P.at(seq, f"m{n}"))
                e.tensor_tensor(kp[b][:, 3, cols], krest[:, :], kp[b][:, 1, cols], ALU.subtract).then_inc(P.sem, P.one(f"l{n}"))
                e.tensor_copy(kp[b][:, 2, cols], kp[b][:, 0, cols]).then_inc(P.sem, P.one(f"hh{n}"))
                hold(e, P.sem, P.at(seq, f"hh{n}"))

        def gpsimd_slot(e, i, w, first, last):
            b, j = w // PAIRS, w % PAIRS
            if j == 0 and not last:
                split_keys(e, i * 2 + b + 2, b)

        def load_queries(e, seq, b):
            e.dma_start(qs[b][0:SROWS, :, :], qx_dram[seq].rearrange("j r n -> r j n")).then_inc(S[f"q_loaded{b}"], 16)
            e.dma_start(qs[b][SHIFT_ROW:STACK, :, :], I["query_rows"]).then_inc(S[f"q_loaded{b}"], 16)
            if mask_rows is not None:
                e.dma_start(ks[b][MASK_ROW:STACK, :, :],
                            mask_rows[seq].rearrange("(a n) -> a n", a=1).unsqueeze(1).broadcast_to([1, PAIRS, KEYS])
                            ).then_inc(S[f"q_loaded{b}"], 16)

        def stack_keys(e, seq, b):
            hold(e, P.sem, P.turns(seq + 1))
            for j in range(PAIRS):
                for a in range(2):
                    e.dma_start(ks[b][a * SROWS // 2:(a + 1) * SROWS // 2, j, :],
                                kp[b][PR * j:PR * (j + 1), a:a + 3, :]).then_inc(k_stacked[b][j // (PAIRS // 2)], 16)

        def store(e, seq):
            hold(e, S["summed"], seq + 1)
            for dst, row in ((at_dram, 0), (den_dram, 32)):
                e.dma_start(dst.rearrange("(j r) t -> r j t", r=PR)[:, :, bass.ds(seq * SEQ, SEQ)],
                            att[row:row + PR, :].rearrange("r (j q) -> r j q", j=PAIRS)).then_inc(S["bias_loaded_sums_stored"], 16)

        def sync_seq(e, i, w, first, last):
            b, j = w // PAIRS, w % PAIRS
            if j:
                return
            seq = i * 2 + b
            if not last:
                hold(e, S["v_ps"], (seq + 1) * KBANKS)
                e.dma_start(ctx[b][:, :], I["ctxT"][seq + 2]).then_inc(S[f"ctx_loaded{b}"], 16)
            if not (last and b == 1):
                if not (first and b == 0):
                    hold(e, S["score_ps"], seq * PAIRS * KBANKS)
                load_queries(e, seq + 1, 1 - b)
                stack_keys(e, seq + 1, 1 - b)
            if not first:
                store(e, seq - 2)

        with nc.Block() as block:
            @block.sync
            def _(e):
                load_all(e, S["weights_loaded"], [(wk[:, :], I[W + "WkT"]), (wv[:, :], I[W + "WvT"])])
                e.dma_start(bk[:, :], column(I[W + "bk"])).then_inc(S["bias_loaded_sums_stored"], 16)
                for b in range(2):
                    e.dma_start(ctx[b][:, :], I["ctxT"][b]).then_inc(S[f"ctx_loaded{b}"], 16)
                for b in range(2):
                    e.dma_start(ks[b][SHIFT_ROW:STACK, :, :], I["key_rows"]).then_inc(S["rows_loaded"], 16)
                hold(e, S["rows_loaded"], 32)
                load_queries(e, 0, 0)
                stack_keys(e, 0, 0)
                turns(e, sync_seq)
                store(e, SEQS - 2)
                store(e, SEQS - 1)
                hold(e, S["bias_loaded_sums_stored"], 16 + SEQS * 32)

            @block.tensor
            def _(e):
                e.wait_ge(S["rows_loaded"], 32)
                e.wait_ge(S["ones_set"], 2)
                e.wait_ge(S["weights_loaded"], 32)
                e.wait_ge(S["ctx_loaded0"], 16)
                for n in range(KBANKS):
                    if n:
                        e.wait_ge(S["k_f32"], n)
                    keys_matmul(e, 0, n)
                e.wait_ge(S["k_f32"], KBANKS)
                for n in range(KBANKS):
                    if n:
                        e.wait_ge(S["v_copied"], n)
                    values_matmul(e, 0, n)
                e.wait_ge(S["v_copied"], KBANKS)
                e.wait_ge(S["ctx_loaded1"], 16)
                for n in range(KBANKS):
                    if n:
                        e.wait_ge(S["k_f32"], KBANKS + n)
                    keys_matmul(e, 1, n)
                e.wait_ge(S["k_f32"], 2 * KBANKS)
                turns(e, tensor_slot)
                last = SEQS * PAIRS
                e.wait_ge(S["bank_max"], last * KBANKS)
                shift_matmul(e, last - 1, 1)
                for k in (1, 2):
                    pv_matmul(e, last - LAG - 1, 1, (last - LAG - 1) % PAIRS, k, False)
                for u in range(last - LAG, last):
                    for k in range(KBANKS):
                        scores_matmul(e, u, 1, u % PAIRS, k, False)
                        pv_matmul(e, u, 1, u % PAIRS, k, False)
                e.wait_ge(S["pv_copied"], last - PAIRS)
                sum_matmul(e, 0)
                e.wait_ge(S["pv_copied"], last)
                e.wait_ge(S["summed"], SEQS - 1)
                sum_matmul(e, 1)

            @block.scalar
            def _(e):
                e.wait_ge(S["bias_loaded_sums_stored"], 16)
                for n in range(KBANKS):
                    key_copy(e, 0, n)
                e.wait_ge(S["ones_set"], 2)
                for n in range(KBANKS):
                    value_copy(e, 0, 0, n)
                for n in range(KBANKS):
                    key_copy(e, 1, n)
                turns(e, scalar_slot)
                last = SEQS * PAIRS
                pv_copy(e, last - LAG - 1, 1, (last - LAG - 1) % PAIRS)
                for u in range(last - LAG, last):
                    for k in range(KBANKS):
                        exp_bank(e, u, k, False)
                    pv_copy(e, u, 1, u % PAIRS)
                sum_copy(e, SEQS - 2)
                sum_copy(e, SEQS - 1)

            @block.vector
            def _(e):
                for b in range(2):
                    e.memset(vs[b][:, :, :, PR:2 * PR], 1.0).then_inc(S["ones_set"], 1)
                for seq in range(2):
                    for n in range(KBANKS):
                        key_round(e, seq, seq, n, None)
                    if seq == 0:
                        split_keys(e, 0, 0)
                turns(e, vector_slot)
                shift_copy(e, SEQS * PAIRS - 1, 1, PAIRS - 1)

            @block.gpsimd
            def _(e):
                hold(e, P.sem, P.turns(1))
                split_keys(e, 1, 1)
                turns(e, gpsimd_slot)


def project_and_route(nc, bank, name, layer, at_dram, den_dram, x_in, x_out, xT_dram, cT_dram, consts, I):
    W = f"L{layer}_xattn_"
    E = E0 if layer == 0 else E1
    with Stage(nc, name) as g:
        wo, wr = g.sb("wo", [D, D]), g.sb("wr", [D, E])
        bo, bv = g.sb("bo", [TILE, D]), g.sb("bv", [D, 1])
        ident, half = consts["ident"], consts["minus_half"]
        if layer == 0:
            cb = g.sb("cb", [TILE, E])
            lane_shapes = {"sfc": ([TILE, TILES, E],), "t8": ([TILE, TILES, G0, 8],), "gs": ([TILE, TILES, 12],), "gtop": ([TILE, TILES, 8],), "gm": ([TILE, TILES, 12],),
                           "masked": ([TILE, TILES, E],), "etop": ([TILE, TILES, 8],), "em": ([TILE, TILES, E],)}
            route = ("plus1 scores biased top2 gsum " + " ".join(f"gtop{s}" for s in range(4)) + " rep "
                     + " ".join(f"gpick{s}" for s in range(4)) + " gmask masked " + " ".join(f"etop{s}" for s in range(4)) + " "
                     + " ".join(f"epick{s}" for s in range(4)) + " emask chosen csum csum_eps cinv weights")
        else:
            lane_shapes = {"top": ([TILE, TILES, 8],)}
            route = " ".join(f"gtop{s}" for s in range(4)) + " keep less | kept csum cinv weights"
        weights, loaded = g.sem("weights_loaded"), g.sem("group_loaded")
        x_stored, xT_stored, cT_stored = g.sem("weight_loaded_x_stored"), g.sem("weight_loaded_xT_stored"), g.sem("weight_loaded_cT_stored")
        set_ = g.sem("sentinels_set") if layer == 0 else None
        T = LaneSteps(g.sem("tensor_steps"), "y_ps | xT_ps | logits_ps | cT_ps")
        A = LaneSteps(g.sem("scalar_steps"), "AT | xT | exp | cT")
        V = LaneSteps(g.sem("vector_steps"), "inv_den divided | y_bias y_res " + NORM_STATS + " | " + NORMED + " | " + route)
        P = LaneSteps(g.sem("gpsimd_steps"), "rstd")
        nw = [0]
        lanes = [dict(T=T.lane(b), A=A.lane(b), V=V.lane(b), P=P.lane(b), bank=bank[4 * b:4 * b + 4],
                      **{n: g.sb(f"{n}{b}", *shape) for n, shape in {
                          "AT": ([D, GROUP],), "DEN": ([D, GROUP],), "X": ([TILE, TILES, D],), "r": ([TILE, TILES, D],), "xn": ([TILE, TILES, D],),
                          "xT": ([D, GROUP],), "sc": ([TILE, TILES, E],), "combine": ([TILE, TILES, E],), "cT": ([E, GROUP],), "den": ([TILE, TILES],), "stats": ([TILE, 4, 6],), "mv": ([TILE, 4, 2],), "ve": ([TILE, 4],), "rstd": ([TILE, 4],),
                          **lane_shapes,
                      }.items()}) for b in range(LANES)]
        with nc.Block() as block:
            @block.sync
            def _(e):
                ws = [(cb[:, :], rows_of(I["L0_ffn_correction_bias"]))] if layer == 0 else []
                nw[0] = load_all(e, weights, [(wo[:, :], I[W + "WoT"])] + ws)
                load_all(e, x_stored, [(bo[:, :], rows_of(I[W + "bo"]))])
                load_all(e, xT_stored, [(bv[:, :], column(I[W + "bv"]))])
                load_all(e, cT_stored, [(wr[:, :], I["router" + str(layer)])])

                def load(t, b, c):
                    at = t * LANES + b
                    e.dma_start(c["DEN"][:, :], den_dram[:, bass.ds(at * GROUP, GROUP)]).then_inc(loaded, 16)
                    e.dma_start(c["AT"][:, :], at_dram[:, bass.ds(at * GROUP, GROUP)]).then_inc(loaded, 16)
                    e.dma_start(c["X"][:, :, :], tok_major(x_in, at)).then_inc(loaded, 16)

                def store_x(t, b, c):
                    hold(e, c["V"].sem, c["V"].at(t, "normed3"))
                    e.dma_start(tok_major(x_out, t * LANES + b), c["xn"][:, :, :]).then_inc(x_stored, 16)

                def store_rest(t, b, c):
                    at = t * LANES + b
                    hold(e, c["A"].sem, c["A"].at(t, "xT"))
                    e.dma_start(xT_dram[:, bass.ds(at * GROUP, GROUP)], c["xT"][:, :]).then_inc(xT_stored, 16)
                    hold(e, c["A"].sem, c["A"].at(t, "cT"))
                    e.dma_start(cT_dram[0:E, bass.ds(at * GROUP, GROUP)], c["cT"][:, :]).then_inc(cT_stored, 16)

                for b, c in enumerate(lanes):
                    load(0, b, c)
                with e.Fori(0, TURNS - 1) as t:
                    for b, c in enumerate(lanes):
                        hold(e, c["V"].sem, c["V"].at(t, "y_res"))
                        load(t + 1, b, c)
                    for b, c in enumerate(lanes):
                        store_x(t, b, c)
                    for b, c in enumerate(lanes):
                        store_rest(t, b, c)
                for b, c in enumerate(lanes):
                    store_x(TURNS - 1, b, c)
                for b, c in enumerate(lanes):
                    store_rest(TURNS - 1, b, c)
                for sem in (x_stored, xT_stored, cT_stored):
                    hold(e, sem, 16 * (1 + GROUPS))

            @block.tensor
            def _(e):
                e.wait_ge(weights, nw[0])
                e.wait_ge(cT_stored, 16)
                with e.Fori(0, TURNS) as t:
                    for c in lanes:
                        e.wait_ge(loaded, (t + 1) * 48 * LANES)
                        e.wait_ge(c["A"].sem, c["A"].at(t, "AT"))
                        for s in range(TILES):
                            m = e.matmul(c["bank"][0][0:TILE, s * D:(s + 1) * D], c["AT"][:, s * TILE:(s + 1) * TILE], wo[:, :], start=True, stop=True)
                        m.then_inc(c["T"].sem, c["T"].one("y_ps"))
                    for c in lanes:
                        e.wait_ge(c["V"].sem, c["V"].at(t, "normed3"))
                        for s in range(TILES):
                            m = e.transpose(c["bank"][1][:, s * TILE:(s + 1) * TILE], c["xn"][:, s, :], ident[0:TILE, 0:TILE])
                        m.then_inc(c["T"].sem, c["T"].one("xT_ps"))
                    for c in lanes:
                        e.wait_ge(c["A"].sem, c["A"].at(t, "xT"))
                        for s in range(TILES):
                            m = e.matmul(c["bank"][2][0:TILE, s * E:(s + 1) * E], c["xT"][:, s * TILE:(s + 1) * TILE], wr[:, :], start=True, stop=True)
                        m.then_inc(c["T"].sem, c["T"].one("logits_ps"))
                    for c in lanes:
                        hold(e, c["V"].sem, c["V"].at(t, "weights"))
                        for s in range(TILES):
                            m = e.transpose(c["bank"][3][0:E, s * TILE:(s + 1) * TILE], c["combine"][:, s, :], ident[0:TILE, 0:TILE])
                        m.then_inc(c["T"].sem, c["T"].one("cT_ps"))

            @block.scalar
            def _(e):
                e.wait_ge(xT_stored, 16)
                with e.Fori(0, TURNS) as t:
                    for c in lanes:
                        e.wait_ge(loaded, (t + 1) * 48 * LANES)
                        e.wait_ge(c["V"].sem, c["V"].at(t, "divided"))
                        e.activation(c["AT"][:, :], c["AT"][:, :], ACT.Identity, bias=bv[:, :]).then_inc(c["A"].sem, c["A"].one("AT"))
                    for c in lanes:
                        e.wait_ge(c["T"].sem, c["T"].at(t, "xT_ps"))
                        e.wait_ge(xT_stored, 16 + t * 16 * LANES)
                        e.copy(c["xT"][:, :], c["bank"][1][:, 0:GROUP]).then_inc(c["A"].sem, c["A"].one("xT"))
                    for c in lanes:
                        if layer == 0:
                            e.wait_ge(c["T"].sem, c["T"].at(t, "logits_ps"))
                            e.activation(c["sc"][:, :, :], c["bank"][2][0:TILE, 0:TILES * E].rearrange("p (s n) -> p s n", s=TILES), ACT.Exp, scale=-1.0).then_inc(c["A"].sem, c["A"].one("exp"))
                        else:
                            e.wait_ge(c["V"].sem, c["V"].at(t, "less"))
                            e.activation(c["sc"][:, :, :], c["combine"][:, :, :], ACT.Exp).then_inc(c["A"].sem, c["A"].one("exp"))
                    for c in lanes:
                        e.wait_ge(c["T"].sem, c["T"].at(t, "cT_ps"))
                        e.wait_ge(cT_stored, 16 + t * 16 * LANES)
                        e.copy(c["cT"][:, :], c["bank"][3][0:E, 0:GROUP]).then_inc(c["A"].sem, c["A"].one("cT"))

            @block.vector
            def _(e):
                e.wait_ge(weights, nw[0])
                e.wait_ge(x_stored, 16)
                if layer == 0:
                    for c in lanes:
                        e.memset(c["gs"][:, :, 8:12], ABSENT).then_inc(set_, 1)
                        e.memset(c["gtop"][:, :, :], ABSENT).then_inc(set_, 1)
                    e.wait_ge(set_, 2 * LANES)

                def step(before, name, f):
                    e.wait_ge(c["V"].sem, c["V"].at(t, before))
                    return f().then_inc(c["V"].sem, c["V"].one(name))

                with e.Fori(0, TURNS) as t:
                    for c in lanes:
                        e.wait_ge(loaded, (t + 1) * 48 * LANES)
                        e.reciprocal(c["DEN"][:, :], c["DEN"][:, :]).then_inc(c["V"].sem, c["V"].one("inv_den"))
                        step("inv_den", "divided", lambda: e.tensor_tensor(c["AT"][:, :], c["AT"][:, :], c["DEN"][:, :], ALU.mult))
                    for c in lanes:
                        e.wait_ge(c["T"].sem, c["T"].at(t, "y_ps"))
                        e.tensor_tensor(c["r"][:, :, :], c["bank"][0][0:TILE, :].rearrange("p (s d) -> p s d", s=TILES), bc(bo[:, :], TILES, 1), ALU.add).then_inc(c["V"].sem, c["V"].one("y_bias"))
                        e.wait_ge(c["V"].sem, c["V"].at(t, "y_bias"))
                        e.tensor_tensor(c["r"][:, :, :], c["r"][:, :, :], c["X"][:, :, :], ALU.add).then_inc(c["V"].sem, c["V"].one("y_res"))
                        norm_stats(e, c["V"], t, c["r"], c["stats"], c["mv"], c["ve"])
                    for c in lanes:
                        norm_apply(e, c["V"], c["P"], t, c["r"], c["mv"], c["rstd"], c["xn"], x_stored)
                    for c in lanes:
                        if layer == 0:
                            e.wait_ge(c["A"].sem, c["A"].at(t, "exp"))
                            e.tensor_scalar(c["sc"][:, :, :], c["sc"][:, :, :], 1.0, None, ALU.add).then_inc(c["V"].sem, c["V"].one("plus1"))
                            step("plus1", "scores", lambda: e.reciprocal(c["sc"][:, :, :], c["sc"][:, :, :]))
                            step("scores", "biased", lambda: e.tensor_tensor(c["sfc"][:, :, :], c["sc"][:, :, :], bc(cb[:, :], TILES, 1), ALU.add))
                            hold(e, c["V"].sem, c["V"].at(t, "biased"))
                            for s in range(TILES):
                                for k in range(G0):
                                    m = e.max(c["t8"][:, s, k, :], c["sfc"][:, s, k * 8:(k + 1) * 8])
                            m.then_inc(c["V"].sem, c["V"].one("top2"))
                            step("top2", "gsum", lambda: e.tensor_tensor(c["gs"][:, :, 0:8], c["t8"][:, :, :, 0], c["t8"][:, :, :, 1], ALU.add))
                            hold(e, c["V"].sem, c["V"].at(t, "gsum"))
                            for s in range(TILES):
                                e.max(c["em"][:, s, 0:8], c["gs"][:, s, 0:8]).then_inc(c["V"].sem, c["V"].one(f"gtop{s}"))
                            step("gtop3", "rep", lambda: e.tensor_copy(c["gtop"][:, :, 0:4], c["em"][:, :, 0:4]))
                            hold(e, c["V"].sem, c["V"].at(t, "rep"))
                            for s in range(TILES):
                                e.match_replace(out=c["gm"][:, s, :], in_to_replace=c["gtop"][:, s, :], in_values=c["gs"][:, s, :], imm_value=PICKED).then_inc(c["V"].sem, c["V"].one(f"gpick{s}"))
                            step("gpick3", "gmask", lambda: e.tensor_scalar(c["gm"][:, :, 0:8], c["gm"][:, :, 0:8], PICKED, None, ALU.is_ge))
                            step("gmask", "masked", lambda: e.tensor_tensor(c["masked"][:, :, :].rearrange("p s (g n) -> p s g n", g=G0),
                                 c["sfc"][:, :, :].rearrange("p s (g n) -> p s g n", g=G0), bc(c["gm"][:, :, 0:8], 8, 3), ALU.mult))
                            hold(e, c["V"].sem, c["V"].at(t, "masked"))
                            for s in range(TILES):
                                e.max(c["etop"][:, s, :], c["masked"][:, s, :]).then_inc(c["V"].sem, c["V"].one(f"etop{s}"))
                            hold(e, c["V"].sem, c["V"].at(t, "etop3"))
                            for s in range(TILES):
                                e.match_replace(out=c["em"][:, s, :], in_to_replace=c["etop"][:, s, :], in_values=c["masked"][:, s, :], imm_value=PICKED).then_inc(c["V"].sem, c["V"].one(f"epick{s}"))
                            step("epick3", "emask", lambda: e.tensor_scalar(c["em"][:, :, :], c["em"][:, :, :], PICKED, None, ALU.is_ge))
                            step("emask", "chosen", lambda: e.tensor_tensor(c["combine"][:, :, :], c["em"][:, :, :], c["sc"][:, :, :], ALU.mult))
                            step("chosen", "csum", lambda: e.tensor_reduce(c["den"][:, :], c["combine"][:, :, :], AX, ALU.add))
                            step("csum", "csum_eps", lambda: e.tensor_scalar(c["den"][:, :], c["den"][:, :], 1e-20, None, ALU.add))
                            step("csum_eps", "cinv", lambda: e.reciprocal(c["den"][:, :], c["den"][:, :]))
                            e.wait_ge(c["V"].sem, c["V"].at(t, "cinv"))
                            for s in range(TILES):
                                m = e.tensor_scalar(c["combine"][:, s, :], c["combine"][:, s, :], c["den"][:, s:s + 1], 2.5, ALU.mult, ALU.mult)
                            m.then_inc(c["V"].sem, c["V"].one("weights"))
                        else:
                            gate = c["bank"][2][0:TILE, 0:TILES * E].rearrange("p (s n) -> p s n", s=TILES)
                            hold(e, c["T"].sem, c["T"].at(t, "logits_ps"))
                            for s in range(TILES):
                                e.max(c["top"][:, s, :], gate[:, s, :]).then_inc(c["V"].sem, c["V"].one(f"gtop{s}"))
                            step("gtop3", "keep", lambda: e.tensor_tensor(c["r"][:, :, 0:E], gate, bc(c["top"][:, :, 1], E, 2), ALU.is_ge))
                            e.tensor_tensor(c["combine"][:, :, :], gate, bc(c["top"][:, :, 0], E, 2), ALU.subtract).then_inc(c["V"].sem, c["V"].one("less"))
                    for c in (lanes if layer else ()):
                        e.wait_ge(c["A"].sem, c["A"].at(t, "exp"))
                        e.tensor_tensor(c["combine"][:, :, :], c["sc"][:, :, :], c["r"][:, :, 0:E], ALU.mult).then_inc(c["V"].sem, c["V"].one("kept"))
                        step("kept", "csum", lambda: e.tensor_reduce(c["den"][:, :], c["combine"][:, :, :], AX, ALU.add))
                        step("csum", "cinv", lambda: e.reciprocal(c["den"][:, :], c["den"][:, :]))
                        e.wait_ge(c["V"].sem, c["V"].at(t, "cinv"))
                        for s in range(TILES):
                            m = e.tensor_scalar(c["combine"][:, s, :], c["combine"][:, s, :], c["den"][:, s:s + 1], 1.0 / E1, ALU.mult, ALU.mult)
                        m.then_inc(c["V"].sem, c["V"].one("weights"))

            @block.gpsimd
            def _(e):
                with e.Fori(0, TURNS) as t:
                    for c in lanes:
                        e.wait_ge(c["V"].sem, c["V"].at(t, "vareps"))
                        e.tensor_tensor(c["rstd"][:, :], c["ve"][:, :], half[0:TILE, :], ALU.pow).then_inc(c["P"].sem, c["P"].one("rstd"))


def experts(nc, bank, name, layer, xT_dram, cT_dram, yT_dram, consts, I):
    NCH, CPT = (NCH0, 4) if layer == 0 else (NCH1, 2 * I1 // 128)
    OFF = -NCH % CPT
    TURNS, UT, LAG, RING, BUFS = (NCH + OFF) // CPT, CPT * GROUPS, 3, 4, 4
    ACC, UP = 0, 4
    START = OFF * GROUPS
    with Stage(nc, name) as g:
        xT = g.sb("xT", [D, GROUPS, GROUP])
        wu = [g.sb(f"wu{i}", [D, D]) for i in range(BUFS)]
        wd = [g.sb(f"wd{i}", [D, D]) for i in range(BUFS)]
        cB = [g.sb(f"cB{i}", [D, GROUPS, GROUP]) for i in range(BUFS if layer == 0 else 2)]
        b1 = [g.sb(f"b1_{i}", [D, 1]) for i in range(BUFS)]
        hr = [g.sb(f"relu{i}", [D, GROUP]) for i in range(RING)]
        hc = [g.sb(f"weighted{i}", [D, GROUP]) for i in range(RING)]
        h2 = [g.sb(f"squared{i}", [D, GROUP]) for i in range(RING)] if layer == 0 else hc
        b2, cT = g.sb("b2", [E1, D]), g.sb("cT", [E1, GROUPS, GROUP])
        out = g.sb("out", [D, GROUPS, GROUP])
        S = {n: g.sem(n) for n in ["x_loaded", "up_ps", "relu", "weighted", "down_ps", "copied", "stored"]
             + (["squared", "bias_set"] if layer == 0 else [])}
        chunk_sem = [g.sem(f"chunk_loaded{i}") for i in range(BUFS)]
        expert_sem = [g.sem(f"expert_loaded{i}") for i in range(2)] if layer else None
        done = S["squared"] if layer == 0 else S["weighted"]
        NL = 16 * (4 if layer == 0 else 3)

        def spread(dst, row, n):
            return (dst, cT_dram[row].rearrange("(a g n) -> a g n", a=1, g=GROUPS).broadcast_to([n, GROUPS, GROUP]))

        def load_chunk(e, i, cc):
            f, b = i * CPT + cc - OFF, cc % BUFS
            known = isinstance(i, int)
            if layer and cc % BUFS == 0:
                h = cc // BUFS
                if not (known and f < 2 * BUFS):
                    hold(e, S["down_ps"], (f - BUFS) * GROUPS)
                e.dma_start(*spread(cB[h][:, :, :], i * 2 + h, D)).then_inc(expert_sem[h], 16)
            if not (known and f < BUFS):
                hold(e, S["down_ps"], (f - BUFS + 1) * GROUPS)
            loads = [(wu[b][:, :], I[f"up{layer}"][f]), (wd[b][:, :], I[f"down{layer}"][f])]
            if layer == 0:
                loads += [spread(cB[b][64 * h:64 * h + 64, :, :], 2 * f + h, 64) for h in range(2)]
            else:
                loads += [(b1[b][:, :], I["b1"][f])]
            for dst, src in loads:
                e.dma_start(dst, src).then_inc(chunk_sem[b], 16)

        def chunk_loaded(e, i, cc):
            b = cc % BUFS
            before = cc // BUFS - (1 if b < OFF else 0)
            e.wait_ge(chunk_sem[b], (i * (CPT // BUFS) + before + 1) * NL)

        def expert_loaded(e, i, cc):
            e.wait_ge(expert_sem[cc // BUFS], (i + 1) * 16)

        def weight_of(w):
            cc = w // GROUPS
            return cB[cc % BUFS if layer == 0 else cc // BUFS][:, w % GROUPS, :]

        def tensor_unit(e, i, w, first):
            k = w % GROUPS
            u = i * UT + w - START
            if k == 0:
                chunk_loaded(e, i, w // GROUPS)
            if not (first and w < START + 4):
                e.wait_ge(S["relu"], u - 3)
            e.matmul(bank[UP + w % 4][:, 0:GROUP], wu[w // GROUPS % BUFS][:, :], xT[:, k, :], start=True, stop=True).then_inc(S["up_ps"], 1)
            if not (first and w < START + LAG):
                down(e, u - LAG, (w - LAG) % UT)

        def down(e, u, w):
            e.wait_ge(done, u + 1)
            e.matmul(bank[ACC + w % GROUPS][:, 0:GROUP], wd[w // GROUPS % BUFS][:, :], h2[w % RING][:, :],
                     start=False, stop=False, skip_group_check=True).then_inc(S["down_ps"], 1)

        def scalar_unit(e, i, w, first):
            u = i * UT + w - START
            e.wait_ge(S["up_ps"], u + 1)
            if not (first and w < START + RING):
                e.wait_ge(done, u - RING + 1)
            e.activation(hr[w % RING][:, :], bank[UP + w % 4][:, 0:GROUP], ACT.Relu,
                         bias=b1[w // GROUPS % BUFS if layer else 0][:, :]).then_inc(S["relu"], 1)

        def vector_unit(e, i, w, first):
            u = i * UT + w - START
            e.wait_ge(S["relu"], u + 1)
            if not (first and w < START + RING):
                e.wait_ge(S["squared"] if layer == 0 else S["down_ps"], u - RING + 1)
            e.tensor_tensor(hc[w % RING][:, :], hr[w % RING][:, :], weight_of(w), ALU.mult).then_inc(S["weighted"], 1)

        def gpsimd_unit(e, i, w, first):
            u = i * UT + w - START
            e.wait_ge(S["weighted"], u + 1)
            if not (first and w < START + RING):
                e.wait_ge(S["down_ps"], u - RING + 1)
            e.tensor_tensor(h2[w % RING][:, :], hc[w % RING][:, :], hr[w % RING][:, :], ALU.mult).then_inc(S["squared"], 1)

        def turns(e, unit):
            for w in range(START, UT):
                unit(e, 0, w, True)
            with e.Fori(1, TURNS) as i:
                for w in range(UT):
                    unit(e, i, w, False)

        with nc.Block() as block:
            @block.sync
            def _(e):
                e.dma_start(xT[:, :, :], xT_dram.rearrange("d (g n) -> d g n", g=GROUPS)).then_inc(S["x_loaded"], 16)
                e.dma_start(b2[:, :], I["b2_or_zero" + str(layer)]).then_inc(S["x_loaded"], 16)
                e.dma_start(cT[:, :, :], cT_dram[0:E1].rearrange("c (g n) -> c g n", g=GROUPS)).then_inc(S["x_loaded"], 16)
                for i in range(2):
                    for cc in range(OFF if i == 0 else 0, CPT):
                        load_chunk(e, i, cc)
                with e.Fori(2, TURNS) as i:
                    for cc in range(CPT):
                        load_chunk(e, i, cc)
                hold(e, S["copied"], GROUPS)
                e.dma_start(yT_dram.rearrange("d (g n) -> d g n", g=GROUPS), out[:, :, :]).then_inc(S["stored"], 16)
                hold(e, S["stored"], 16)

            @block.tensor
            def _(e):
                e.wait_ge(S["x_loaded"], 48)
                for k in range(GROUPS):
                    e.matmul(bank[ACC + k][:, 0:GROUP], b2[:, :], cT[:, k, :], start=True, stop=False, skip_group_check=True)
                turns(e, tensor_unit)
                for w in range(UT - LAG, UT):
                    down(e, (TURNS - 1) * UT + w - START, w)

            @block.scalar
            def _(e):
                if layer == 0:
                    e.wait_ge(S["bias_set"], 1)

                def unit(e, i, w, first):
                    if layer and w % GROUPS == 0:
                        chunk_loaded(e, i, w // GROUPS)
                    scalar_unit(e, i, w, first)
                turns(e, unit)

            @block.vector
            def _(e):
                if layer == 0:
                    e.memset(b1[0][:, :], 0.0).then_inc(S["bias_set"], 1)

                def unit(e, i, w, first):
                    if layer == 0 and w % GROUPS == 0:
                        chunk_loaded(e, i, w // GROUPS)
                    if layer and w % (GROUPS * BUFS) == 0:
                        expert_loaded(e, i, w // GROUPS)
                    vector_unit(e, i, w, first)
                turns(e, unit)
                e.wait_ge(S["down_ps"], NCH * GROUPS)
                for k in range(GROUPS):
                    e.tensor_copy(out[:, k, :], bank[ACC + k][:, 0:GROUP]).then_inc(S["copied"], 1)

            if layer == 0:
                @block.gpsimd
                def _(e):
                    turns(e, gpsimd_unit)


def norm_and_project_1(nc, bank, yT_dram, x_in, x3, qkT_dram, v_dram, consts, I):
    with Stage(nc, "np1") as g:
        w = g.sb("w", [D, 3, D])
        qks = g.sb("qks", [D, 2])
        ident, half, ones8 = consts["ident"], consts["minus_half"], g.sb("ones8", [D, D])
        weights, loaded = g.sem("weights_loaded"), g.sem("group_loaded")
        x_stored, v_stored, qk_stored = g.sem("weight_loaded_x_stored"), g.sem("weight_loaded_v_stored"), g.sem("weight_loaded_qk_stored")
        T = LaneSteps(g.sem("tensor_steps"), "y_ps | xT_ps | q_ps k_ps v_ps | norms_ps")
        A = LaneSteps(g.sem("scalar_steps"), "xT | expq expk expv | norms")
        V = LaneSteps(g.sem("vector_steps"), "y_res " + NORM_STATS + " | " + NORMED + " | plus1 inv silu_q silu_k squares vplus1 vinv silu_v | r_eps r_inv ratio scaled_q scaled_k")
        P = LaneSteps(g.sem("gpsimd_steps"), "rstd")
        lanes = [dict(T=T.lane(b), A=A.lane(b), V=V.lane(b), P=P.lane(b), bank=bank[4 * b:4 * b + 4],
                      **{n: g.sb(f"{n}{b}", *shape) for n, shape in {
                          "YT": ([D, GROUP],), "X": ([TILE, TILES, D],), "r": ([TILE, TILES, D],), "xn": ([TILE, TILES, D],), "xT": ([D, GROUP],),
                          "qk": ([D, 2, GROUP],), "sig": ([D, 2, GROUP],), "sq": ([D, 2, GROUP],), "nrm": ([D, 2, GROUP],),
                          "v": ([TILE, TILES, D],), "sv": ([TILE, TILES, D],), "stats": ([TILE, 4, 6],), "mv": ([TILE, 4, 2],), "ve": ([TILE, 4],), "rstd": ([TILE, 4],),
                      }.items()}) for b in range(LANES)]
        with nc.Block() as block:
            @block.sync
            def _(e):
                load_all(e, weights, [(w[:, n, :], I[f"L1_attn_W{c}T"]) for n, c in enumerate("qkv")])
                load_all(e, x_stored, [(ones8[:, :], I["ones8"])])
                load_all(e, v_stored, [(qks[:, 0:1], column(I["q_scale_rows"]))])
                load_all(e, qk_stored, [(qks[:, 1:2], column(I["k_scale_rows"]))])

                def load(t, b, c):
                    at = t * LANES + b
                    e.dma_start(c["YT"][:, :], yT_dram[:, bass.ds(at * GROUP, GROUP)]).then_inc(loaded, 16)
                    e.dma_start(c["X"][:, :, :], tok_major(x_in, at)).then_inc(loaded, 16)

                def store_x(t, b, c):
                    hold(e, c["V"].sem, c["V"].at(t, "normed3"))
                    e.dma_start(tok_major(x3, t * LANES + b), c["xn"][:, :, :]).then_inc(x_stored, 16)

                def store_rest(t, b, c):
                    at = t * LANES + b
                    hold(e, c["V"].sem, c["V"].at(t, "silu_v"))
                    e.dma_start(tok_major(v_dram, at), c["v"][:, :, :]).then_inc(v_stored, 16)
                    hold(e, c["V"].sem, c["V"].at(t, "scaled_k"))
                    e.dma_start(qkT_dram[:, :, bass.ds(at * GROUP, GROUP)], c["qk"][:, :, :]).then_inc(qk_stored, 16)

                for b, c in enumerate(lanes):
                    load(0, b, c)
                with e.Fori(0, TURNS - 1) as t:
                    for b, c in enumerate(lanes):
                        hold(e, c["V"].sem, c["V"].at(t, "silu_v"))
                        load(t + 1, b, c)
                    for b, c in enumerate(lanes):
                        store_x(t, b, c)
                    for b, c in enumerate(lanes):
                        store_rest(t, b, c)
                for b, c in enumerate(lanes):
                    store_x(TURNS - 1, b, c)
                for b, c in enumerate(lanes):
                    store_rest(TURNS - 1, b, c)
                for sem in (x_stored, v_stored, qk_stored):
                    hold(e, sem, 16 * (1 + GROUPS))

            @block.tensor
            def _(e):
                e.wait_ge(weights, 48)
                e.wait_ge(x_stored, 16)
                with e.Fori(0, TURNS) as t:
                    for c in lanes:
                        e.wait_ge(loaded, (t + 1) * 32 * LANES)
                        for s in range(TILES):
                            m = e.transpose(c["bank"][0][0:TILE, s * D:(s + 1) * D], c["YT"][:, s * TILE:(s + 1) * TILE], ident[:, :])
                        m.then_inc(c["T"].sem, c["T"].one("y_ps"))
                    for c in lanes:
                        e.wait_ge(c["V"].sem, c["V"].at(t, "normed3"))
                        for s in range(TILES):
                            m = e.transpose(c["bank"][1][:, s * TILE:(s + 1) * TILE], c["xn"][:, s, :], ident[0:TILE, 0:TILE])
                        m.then_inc(c["T"].sem, c["T"].one("xT_ps"))
                    for c in lanes:
                        e.wait_ge(c["A"].sem, c["A"].at(t, "xT"))
                        for n, which in enumerate("qk"):
                            e.matmul(c["bank"][2 + n][:, 0:GROUP], w[:, n, :], c["xT"][:, :], start=True, stop=True).then_inc(c["T"].sem, c["T"].one(f"{which}_ps"))
                        for s in range(TILES):
                            m = e.matmul(c["bank"][0][0:TILE, s * D:(s + 1) * D], c["xT"][:, s * TILE:(s + 1) * TILE], w[:, 2, :], start=True, stop=True)
                        m.then_inc(c["T"].sem, c["T"].one("v_ps"))
                    for c in lanes:
                        e.wait_ge(c["V"].sem, c["V"].at(t, "squares"))
                        for n in range(2):
                            m = e.matmul(c["bank"][2 + n][:, 0:GROUP], ones8[:, :], c["sq"][:, n, :], start=True, stop=True)
                        m.then_inc(c["T"].sem, c["T"].one("norms_ps"))

            @block.scalar
            def _(e):
                with e.Fori(0, TURNS) as t:
                    for c in lanes:
                        e.wait_ge(loaded, (t + 1) * 32 * LANES)
                        e.wait_ge(c["T"].sem, c["T"].at(t, "xT_ps"))
                        e.copy(c["xT"][:, :], c["bank"][1][:, 0:GROUP]).then_inc(c["A"].sem, c["A"].one("xT"))
                    for c in lanes:
                        for n, which in enumerate("qk"):
                            e.wait_ge(c["T"].sem, c["T"].at(t, f"{which}_ps"))
                            e.activation(c["sig"][:, n, :], c["bank"][2 + n][:, 0:GROUP], ACT.Exp, scale=-1.0).then_inc(c["A"].sem, c["A"].one(f"exp{which}"))
                        e.wait_ge(c["T"].sem, c["T"].at(t, "v_ps"))
                        e.activation(c["sv"][:, :, :], c["bank"][0][0:TILE, :].rearrange("p (s d) -> p s d", s=TILES), ACT.Exp, scale=-1.0).then_inc(c["A"].sem, c["A"].one("expv"))
                    for c in lanes:
                        e.wait_ge(c["T"].sem, c["T"].at(t, "norms_ps"))
                        for n in range(2):
                            m = e.activation(c["nrm"][:, n, :], c["bank"][2 + n][:, 0:GROUP], ACT.Sqrt)
                        m.then_inc(c["A"].sem, c["A"].one("norms"))

            @block.vector
            def _(e):
                for sem in (v_stored, qk_stored):
                    e.wait_ge(sem, 16)

                def step(before, name, f):
                    e.wait_ge(c["V"].sem, c["V"].at(t, before))
                    return f().then_inc(c["V"].sem, c["V"].one(name))

                with e.Fori(0, TURNS) as t:
                    for c in lanes:
                        e.wait_ge(loaded, (t + 1) * 32 * LANES)
                        e.wait_ge(c["T"].sem, c["T"].at(t, "y_ps"))
                        e.tensor_tensor(c["r"][:, :, :], c["bank"][0][0:TILE, :].rearrange("p (s d) -> p s d", s=TILES), c["X"][:, :, :], ALU.add).then_inc(c["V"].sem, c["V"].one("y_res"))
                        norm_stats(e, c["V"], t, c["r"], c["stats"], c["mv"], c["ve"])
                    for c in lanes:
                        norm_apply(e, c["V"], c["P"], t, c["r"], c["mv"], c["rstd"], c["xn"], x_stored)
                    for c in lanes:
                        e.wait_ge(c["A"].sem, c["A"].at(t, "expk"))
                        e.tensor_scalar(c["sig"][:, :, :], c["sig"][:, :, :], 1.0, None, ALU.add).then_inc(c["V"].sem, c["V"].one("plus1"))
                        step("plus1", "inv", lambda: e.reciprocal(c["sig"][:, :, :], c["sig"][:, :, :]))
                        e.wait_ge(c["V"].sem, c["V"].at(t, "inv"))
                        e.wait_ge(qk_stored, 16 + t * 16 * LANES)
                        for n, which in enumerate("qk"):
                            e.tensor_tensor(c["qk"][:, n, :], c["sig"][:, n, :], c["bank"][2 + n][:, 0:GROUP], ALU.mult).then_inc(c["V"].sem, c["V"].one(f"silu_{which}"))
                        step("silu_k", "squares", lambda: e.tensor_tensor(c["sq"][:, :, :], c["qk"][:, :, :], c["qk"][:, :, :], ALU.mult))
                        e.wait_ge(c["A"].sem, c["A"].at(t, "expv"))
                        e.tensor_scalar(c["sv"][:, :, :], c["sv"][:, :, :], 1.0, None, ALU.add).then_inc(c["V"].sem, c["V"].one("vplus1"))
                        step("vplus1", "vinv", lambda: e.reciprocal(c["sv"][:, :, :], c["sv"][:, :, :]))
                        e.wait_ge(v_stored, 16 + t * 16 * LANES)
                        step("vinv", "silu_v", lambda: e.tensor_tensor(c["v"][:, :, :], c["sv"][:, :, :], c["bank"][0][0:TILE, :].rearrange("p (s d) -> p s d", s=TILES), ALU.mult))
                    for c in lanes:
                        e.wait_ge(c["A"].sem, c["A"].at(t, "norms"))
                        e.tensor_scalar(c["sig"][:, :, :], c["nrm"][:, :, :], 1e-6, None, ALU.add).then_inc(c["V"].sem, c["V"].one("r_eps"))
                        step("r_eps", "r_inv", lambda: e.reciprocal(c["sig"][:, :, :], c["sig"][:, :, :]))
                        step("r_inv", "ratio", lambda: e.tensor_tensor(c["sig"][:, :, :], c["sig"][:, :, :], c["nrm"][:, :, :], ALU.mult))
                        e.wait_ge(c["V"].sem, c["V"].at(t, "ratio"))
                        for n, which in enumerate("qk"):
                            e.scalar_tensor_tensor(out=c["qk"][:, n, :], in0=c["qk"][:, n, :], scalar=qks[:, n:n + 1], in1=c["sig"][:, n, :], op0=ALU.mult, op1=ALU.mult).then_inc(c["V"].sem, c["V"].one(f"scaled_{which}"))

            @block.gpsimd
            def _(e):
                with e.Fori(0, TURNS) as t:
                    for c in lanes:
                        e.wait_ge(c["V"].sem, c["V"].at(t, "vareps"))
                        e.tensor_tensor(c["rstd"][:, :], c["ve"][:, :], half[0:TILE, :], ALU.pow).then_inc(c["P"].sem, c["P"].one("rstd"))


def causal_attention(nc, bank, qkT_dram, v_dram, oT_dram, consts, I):
    N = HEADS * SEQ
    HH, HQ = HEADS // 2, HEADS // 4
    ROWS = 64 + SEQ
    TURNS = SEQS // 4
    with Stage(nc, "ca") as g:
        qk = [g.sb(f"qk{i}", [D, 2, 2, SEQ]) for i in range(2)]
        v = [g.sb(f"v{i}", [SEQ, 2, D]) for i in range(2)]
        kx = [g.sb(f"kx{i}", [D, 2, HEADS, SEQ]) for i in range(2)]
        p = [g.sb(f"p{i}", [ROWS, HEADS, SEQ]) for i in range(2)]
        pT = [g.sb(f"pT{i}", [SEQ, HEADS, ROWS]) for i in range(2)]
        mx, den = [g.sb(f"mx{i}", [ROWS, HEADS]) for i in range(2)], [g.sb(f"den{i}", [ROWS, HEADS]) for i in range(2)]
        o, oT = [g.sb(f"o{i}", [ROWS, D]) for i in range(2)], [g.sb(f"oT{i}", [D, 2, SEQ]) for i in range(2)]
        causal, headmask, ident = g.sb("causal", [ROWS, SEQ]), g.sb("headmask", [D, HEADS]), consts["ident"]
        banks_set = g.sem("banks_set")
        loaded = [g.sem(f"couple_loaded{i}") for i in range(2)]
        stored = [g.sem(f"constant_loaded_couple_stored{i}") for i in range(2)]
        T = [Steps(g.sem(f"tensor_steps{i}"), "s_ps pT_ps o_ps oT_ps") for i in range(2)]
        A = [Steps(g.sem(f"scalar_steps{i}"), "exp pT_0 pT_1 pT_2 pT_3 o oT") for i in range(2)]
        V = [Steps(g.sem(f"vector_steps{i}"), "masked_a masked_b max sum inv") for i in range(2)]
        P = [Steps(g.sem(f"gpsimd_steps{i}"), "kx0 kx1 shifted probs") for i in range(2)]
        with nc.Block() as block:
            @block.sync
            def _(e):
                load_all(e, stored[0], [(causal[:, :], I["causal"])])
                load_all(e, stored[1], [(headmask[:, :], I["headmask"])])

                def load(t, b):
                    at = (t * 2 + b) * 2 * SEQ
                    e.dma_start(qk[b][:, :, :, :], qkT_dram[:, :, bass.ds(at, 2 * SEQ)].rearrange("d a (s n) -> d a s n", s=2)).then_inc(loaded[b], 16)
                    e.dma_start(v[b][:, :, :], v_dram[bass.ds(at, 2 * SEQ), :].rearrange("(s p) d -> p s d", s=2)).then_inc(loaded[b], 16)

                def store(t, b):
                    hold(e, A[b].sem, A[b].at(t, "oT"))
                    e.dma_start(oT_dram[:, bass.ds((t * 2 + b) * 2 * SEQ, 2 * SEQ)], oT[b][:, :, :].rearrange("d s n -> d (s n)")).then_inc(stored[b], 16)

                for b in range(2):
                    load(0, b)
                with e.Fori(0, TURNS - 1) as t:
                    for b in range(2):
                        hold(e, T[b].sem, T[b].at(t, "o_ps"))
                        load(t + 1, b)
                    for b in range(2):
                        store(t, b)
                for b in range(2):
                    store(TURNS - 1, b)
                for b in range(2):
                    hold(e, stored[b], 16 * (1 + TURNS))

            @block.tensor
            def _(e):
                e.wait_ge(banks_set, 4)
                with e.Fori(0, TURNS) as t:
                    for b in range(2):
                        hold(e, loaded[b], (t + 1) * 32)
                        hold(e, P[b].sem, P[b].at(t, "kx1"))
                        for s in range(2):
                            for h in range(2):
                                m = e.matmul(bank[4 * b + h][64 * s:64 * s + SEQ, 0:N // 2], qk[b][:, 0, s, :],
                                             kx[b][:, s, h * HH:(h + 1) * HH, :], start=True, stop=True)
                        m.then_inc(T[b].sem, T[b].one("s_ps"))
                    for b in range(2):
                        hold(e, P[b].sem, P[b].at(t, "probs"))
                        for h in range(HEADS):
                            m = e.transpose(bank[4 * b + h // HQ][0:SEQ, h % HQ * ROWS:(h % HQ + 1) * ROWS],
                                            p[b][:, h, :], ident[0:ROWS, 0:ROWS])
                        m.then_inc(T[b].sem, T[b].one("pT_ps"))
                    for b in range(2):
                        hold(e, A[b].sem, A[b].at(t, "pT_3"))
                        for s in range(2):
                            for h in range(HEADS):
                                m = e.matmul(bank[4 * b][64 * s:64 * s + SEQ, h * HD:(h + 1) * HD], pT[b][:, h, 64 * s:64 * s + SEQ],
                                             v[b][:, s, h * HD:(h + 1) * HD], start=True, stop=True)
                        m.then_inc(T[b].sem, T[b].one("o_ps"))
                    for b in range(2):
                        hold(e, A[b].sem, A[b].at(t, "o"))
                        e.transpose(bank[4 * b + 3][:, 0:ROWS], o[b][:, :], ident[0:ROWS, 0:ROWS]).then_inc(T[b].sem, T[b].one("oT_ps"))

            @block.scalar
            def _(e):
                for b in range(2):
                    e.wait_ge(stored[b], 16)
                with e.Fori(0, TURNS) as t:
                    for b in range(2):
                        e.wait_ge(P[b].sem, P[b].at(t, "shifted"))
                        e.activation(p[b][:, :, :], p[b][:, :, :], ACT.Exp).then_inc(A[b].sem, A[b].one("exp"))
                    for b in range(2):
                        e.wait_ge(T[b].sem, T[b].at(t, "pT_ps"))
                        for h in range(4):
                            e.copy(pT[b][:, h * HQ:(h + 1) * HQ, :], bank[4 * b + h][0:SEQ, 0:HQ * ROWS].rearrange("p (h q) -> p h q", h=HQ)
                                   ).then_inc(A[b].sem, A[b].one(f"pT_{h}"))
                    for b in range(2):
                        e.wait_ge(T[b].sem, T[b].at(t, "o_ps"))
                        e.copy(o[b][:, :], bank[4 * b][0:ROWS, 0:D]).then_inc(A[b].sem, A[b].one("o"))
                    for b in range(2):
                        e.wait_ge(stored[b], 16 + t * 16)
                        e.wait_ge(T[b].sem, T[b].at(t, "oT_ps"))
                        e.copy(oT[b][:, :, :], bank[4 * b + 3][:, 0:2 * 64].rearrange("p (s q) -> p s q", s=2)[:, :, 0:SEQ]).then_inc(A[b].sem, A[b].one("oT"))

            @block.vector
            def _(e):
                for k in (0, 1, 4, 5):
                    e.memset(bank[k][:, :], 0.0).then_inc(banks_set, 1)
                e.wait_ge(stored[0], 16)
                with e.Fori(0, TURNS) as t:
                    for b in range(2):
                        e.wait_ge(T[b].sem, T[b].at(t, "s_ps"))
                        for h in range(2):
                            e.tensor_tensor(p[b][:, h * HH:(h + 1) * HH, :], bank[4 * b + h][0:ROWS, 0:N // 2].rearrange("p (h k) -> p h k", h=HH),
                                            bc(causal[:, :], HH, 1), ALU.add).then_inc(V[b].sem, V[b].one(f"masked_{'ab'[h]}"))
                        e.wait_ge(V[b].sem, V[b].at(t, "masked_b"))
                        e.tensor_reduce(mx[b][:, :], p[b][:, :, :], AX, ALU.max).then_inc(V[b].sem, V[b].one("max"))
                    for b in range(2):
                        e.wait_ge(A[b].sem, A[b].at(t, "exp"))
                        e.tensor_reduce(den[b][:, :], p[b][:, :, :], AX, ALU.add).then_inc(V[b].sem, V[b].one("sum"))
                        e.wait_ge(V[b].sem, V[b].at(t, "sum"))
                        e.reciprocal(den[b][:, :], den[b][:, :]).then_inc(V[b].sem, V[b].one("inv"))

            @block.gpsimd
            def _(e):
                e.wait_ge(stored[1], 16)
                with e.Fori(0, TURNS) as t:
                    for b in range(2):
                        e.wait_ge(loaded[b], (t + 1) * 32)
                        for s in range(2):
                            e.tensor_tensor(kx[b][:, s, :, :], bc(qk[b][:, 1, s, :], HEADS, 1), bc(headmask[:, :], SEQ, 2), ALU.mult).then_inc(P[b].sem, P[b].one(f"kx{s}"))
                    for b in range(2):
                        e.wait_ge(V[b].sem, V[b].at(t, "max"))
                        e.tensor_tensor(p[b][:, :, :], p[b][:, :, :], bc(mx[b][:, :], SEQ, 2), ALU.subtract).then_inc(P[b].sem, P[b].one("shifted"))
                    for b in range(2):
                        e.wait_ge(V[b].sem, V[b].at(t, "inv"))
                        e.tensor_tensor(p[b][:, :, :], p[b][:, :, :], bc(den[b][:, :], SEQ, 2), ALU.mult).then_inc(P[b].sem, P[b].one("probs"))


def project_1(nc, bank, oT_dram, x_in, x_out, qx_dram, consts, I):
    with Stage(nc, "pr1") as g:
        wo, wq, bq, bqs = g.sb("wo", [D, D]), g.sb("wq", [D, D]), g.sb("bq", [D, 1]), g.sb("bqs", [D, 1])
        ident, half, parity = consts["ident"], consts["minus_half"], consts["parity"]
        loaded, bias_loaded, scaled = g.sem("group_loaded"), g.sem("bias_loaded"), g.sem("bias_scaled")
        x_stored, q_stored = g.sem("weight_loaded_x_stored"), g.sem("weight_loaded_queries_stored")
        T = LaneSteps(g.sem("tensor_steps"), "y_ps | xT_ps | qT_ps")
        A = LaneSteps(g.sem("scalar_steps"), "xT | qT q_h q_m " + FACTORS)
        V = LaneSteps(g.sem("vector_steps"), "y_res " + NORM_STATS + " | " + NORMED)
        P = LaneSteps(g.sem("gpsimd_steps"), "rstd | q_rest q_l")
        lanes = [dict(T=T.lane(b), A=A.lane(b), V=V.lane(b), P=P.lane(b), bank=bank[4 * b:4 * b + 4],
                      **{n: g.sb(f"{n}{b}", *shape) for n, shape in {
                          "OT": ([D, GROUP],), "X": ([TILE, TILES, D],), "r": ([TILE, TILES, D],), "xn": ([TILE, TILES, D],),
                          "xT": ([D, GROUP],), "qT": ([D, GROUP],), "qh": ([D, GROUP], BF16), "qm": ([D, GROUP], BF16), "ql": ([D, GROUP], BF16), "qrest": ([D, GROUP],),
                          "qx": ([D, GSEQS, PROD, 2, SEQ], BF16), "stats": ([TILE, 4, 6],), "mv": ([TILE, 4, 2],), "ve": ([TILE, 4],), "rstd": ([TILE, 4],),
                      }.items()}) for b in range(LANES)]
        with nc.Block() as block:
            @block.sync
            def _(e):
                load_all(e, x_stored, [(wo[:, :], I["L1_attn_WoT"])])
                load_all(e, q_stored, [(wq[:, :], I["L1_xattn_Wq"])])
                load_all(e, bias_loaded, [(bq[:, :], column(I["L1_xattn_bq"]))])

                def load(t, b, c):
                    at = t * LANES + b
                    e.dma_start(c["OT"][:, :], oT_dram[:, bass.ds(at * GROUP, GROUP)]).then_inc(loaded, 16)
                    e.dma_start(c["X"][:, :, :], tok_major(x_in, at)).then_inc(loaded, 16)

                def store_x(t, b, c):
                    hold(e, c["V"].sem, c["V"].at(t, "normed3"))
                    e.dma_start(tok_major(x_out, t * LANES + b), c["xn"][:, :, :]).then_inc(x_stored, 16)

                def store_rest(t, b, c):
                    at = t * LANES + b
                    hold(e, c["A"].sem, c["A"].at(t, "x_h2"))
                    store_queries(e, q_stored, at, qx_dram, c["qx"])

                for b, c in enumerate(lanes):
                    load(0, b, c)
                with e.Fori(0, TURNS - 1) as t:
                    for b, c in enumerate(lanes):
                        hold(e, c["V"].sem, c["V"].at(t, "y_res"))
                        load(t + 1, b, c)
                    for b, c in enumerate(lanes):
                        store_x(t, b, c)
                    for b, c in enumerate(lanes):
                        store_rest(t, b, c)
                for b, c in enumerate(lanes):
                    store_x(TURNS - 1, b, c)
                for b, c in enumerate(lanes):
                    store_rest(TURNS - 1, b, c)
                hold(e, x_stored, 16 * (1 + GROUPS))
                hold(e, q_stored, 16 + TURNS * QUERY_STORES)

            @block.tensor
            def _(e):
                for sem in (x_stored, q_stored):
                    e.wait_ge(sem, 16)
                with e.Fori(0, TURNS) as t:
                    for c in lanes:
                        e.wait_ge(loaded, (t + 1) * 32 * LANES)
                        for s in range(TILES):
                            m = e.matmul(c["bank"][0][0:TILE, s * D:(s + 1) * D], c["OT"][:, s * TILE:(s + 1) * TILE], wo[:, :], start=True, stop=True)
                        m.then_inc(c["T"].sem, c["T"].one("y_ps"))
                    for c in lanes:
                        e.wait_ge(c["V"].sem, c["V"].at(t, "normed3"))
                        for s in range(TILES):
                            m = e.transpose(c["bank"][1][:, s * TILE:(s + 1) * TILE], c["xn"][:, s, :], ident[0:TILE, 0:TILE])
                        m.then_inc(c["T"].sem, c["T"].one("xT_ps"))
                    for c in lanes:
                        e.wait_ge(c["A"].sem, c["A"].at(t, "xT"))
                        e.matmul(c["bank"][2][:, 0:GROUP], wq[:, :], c["xT"][:, :], start=True, stop=True).then_inc(c["T"].sem, c["T"].one("qT_ps"))

            @block.scalar
            def _(e):
                e.wait_ge(scaled, 1)
                with e.Fori(0, TURNS) as t:
                    for c in lanes:
                        e.wait_ge(loaded, (t + 1) * 32 * LANES)
                        e.wait_ge(c["T"].sem, c["T"].at(t, "xT_ps"))
                        e.copy(c["xT"][:, :], c["bank"][1][:, 0:GROUP]).then_inc(c["A"].sem, c["A"].one("xT"))
                    for c in lanes:
                        e.wait_ge(c["T"].sem, c["T"].at(t, "qT_ps"))
                        e.activation(c["qT"][:, :], c["bank"][2][:, 0:GROUP], ACT.Identity, bias=bqs[:, :], scale=HD ** -0.5).then_inc(c["A"].sem, c["A"].one("qT"))
                        round_queries(e, c["A"], c["P"], t, c["qT"], c["qh"], c["qrest"], c["qm"])
                        expand_queries(e, c["A"], c["A"], c["P"], t, c["qh"], c["qm"], c["ql"], c["qx"], parity, q_stored)

            @block.vector
            def _(e):
                e.wait_ge(bias_loaded, 16)
                e.tensor_scalar(bqs[:, :], bq[:, :], HD ** -0.5, None, ALU.mult).then_inc(scaled, 1)
                with e.Fori(0, TURNS) as t:
                    for c in lanes:
                        e.wait_ge(loaded, (t + 1) * 32 * LANES)
                        e.wait_ge(c["T"].sem, c["T"].at(t, "y_ps"))
                        e.tensor_tensor(c["r"][:, :, :], c["bank"][0][0:TILE, :].rearrange("p (s d) -> p s d", s=TILES), c["X"][:, :, :], ALU.add).then_inc(c["V"].sem, c["V"].one("y_res"))
                        norm_stats(e, c["V"], t, c["r"], c["stats"], c["mv"], c["ve"])
                    for c in lanes:
                        norm_apply(e, c["V"], c["P"], t, c["r"], c["mv"], c["rstd"], c["xn"], x_stored)

            @block.gpsimd
            def _(e):
                with e.Fori(0, TURNS) as t:
                    for c in lanes:
                        e.wait_ge(c["V"].sem, c["V"].at(t, "vareps"))
                        e.tensor_tensor(c["rstd"][:, :], c["ve"][:, :], half[0:TILE, :], ALU.pow).then_inc(c["P"].sem, c["P"].one("rstd"))
                    for c in lanes:
                        rest_of_queries(e, c["P"], c["A"], t, c["qT"], c["qh"], c["qrest"], c["qm"], c["ql"])


def final_norm(nc, bank, yT_dram, x_in, out, consts):
    with Stage(nc, "fin") as g:
        ident, half = consts["ident"], consts["minus_half"]
        loaded, x_stored = g.sem("group_loaded"), g.sem("first_x_loaded_x_stored")
        T = LaneSteps(g.sem("tensor_steps"), "y_ps")
        V = LaneSteps(g.sem("vector_steps"), "y_res " + NORM_STATS + " | " + NORMED)
        P = LaneSteps(g.sem("gpsimd_steps"), "rstd")
        lanes = [dict(T=T.lane(b), V=V.lane(b), P=P.lane(b), bank=bank[4 * b:4 * b + 4],
                      **{n: g.sb(f"{n}{b}", *shape) for n, shape in {
                          "YT": ([D, GROUP],), "X": ([TILE, TILES, D],), "r": ([TILE, TILES, D],), "xn": ([TILE, TILES, D],),
                          "stats": ([TILE, 4, 6],), "mv": ([TILE, 4, 2],), "ve": ([TILE, 4],), "rstd": ([TILE, 4],),
                      }.items()}) for b in range(LANES)]
        with nc.Block() as block:
            @block.sync
            def _(e):

                def load(t, b, c):
                    at = t * LANES + b
                    e.dma_start(c["YT"][:, :], yT_dram[:, bass.ds(at * GROUP, GROUP)]).then_inc(loaded, 16)
                    e.dma_start(c["X"][:, :, :], tok_major(x_in, at)).then_inc(x_stored if isinstance(t, int) and t == 0 and b == 0 else loaded, 16)

                def store_x(t, b, c):
                    hold(e, c["V"].sem, c["V"].at(t, "normed3"))
                    e.dma_start(tok_major(out, t * LANES + b), c["xn"][:, :, :]).then_inc(x_stored, 16)

                for b, c in enumerate(lanes):
                    load(0, b, c)
                with e.Fori(0, TURNS - 1) as t:
                    for b, c in enumerate(lanes):
                        hold(e, c["V"].sem, c["V"].at(t, "normed3"))
                        load(t + 1, b, c)
                    for b, c in enumerate(lanes):
                        store_x(t, b, c)
                for b, c in enumerate(lanes):
                    store_x(TURNS - 1, b, c)
                hold(e, x_stored, 16 * (1 + GROUPS))

            @block.tensor
            def _(e):
                with e.Fori(0, TURNS) as t:
                    for c in lanes:
                        e.wait_ge(loaded, t * 32 * LANES + 48)
                        for s in range(TILES):
                            m = e.transpose(c["bank"][0][0:TILE, s * D:(s + 1) * D], c["YT"][:, s * TILE:(s + 1) * TILE], ident[:, :])
                        m.then_inc(c["T"].sem, c["T"].one("y_ps"))

            @block.vector
            def _(e):
                e.wait_ge(x_stored, 16)
                with e.Fori(0, TURNS) as t:
                    for c in lanes:
                        e.wait_ge(loaded, t * 32 * LANES + 48)
                        e.wait_ge(c["T"].sem, c["T"].at(t, "y_ps"))
                        e.tensor_tensor(c["r"][:, :, :], c["bank"][0][0:TILE, :].rearrange("p (s d) -> p s d", s=TILES), c["X"][:, :, :], ALU.add).then_inc(c["V"].sem, c["V"].one("y_res"))
                        norm_stats(e, c["V"], t, c["r"], c["stats"], c["mv"], c["ve"])
                    for c in lanes:
                        norm_apply(e, c["V"], c["P"], t, c["r"], c["mv"], c["rstd"], c["xn"], x_stored)

            @block.gpsimd
            def _(e):
                with e.Fori(0, TURNS) as t:
                    for c in lanes:
                        e.wait_ge(c["V"].sem, c["V"].at(t, "vareps"))
                        e.tensor_tensor(c["rstd"][:, :], c["ve"][:, :], half[0:TILE, :], ALU.pow).then_inc(c["P"].sem, c["P"].one("rstd"))


def set_up(nc, consts, mask_dram, cT_dram, I):
    with Stage(nc, "set") as g:
        m8, mf, mb = g.sb("m8", [SEQS, KEYS // 4], mybir.dt.int32), g.sb("mf", [SEQS, KEYS]), g.sb("mb", [SEQS, KEYS], BF16)
        loaded, turned, stored = g.sem("loaded"), g.sem("mask_turned"), g.sem("mask_stored")
        with nc.Block() as block:
            @block.sync
            def _(e):
                load_all(e, loaded, [(m8[:, :], I["mask"]), (consts["ident"][:, :], I["ident"]),
                                     (consts["parity"][:, :], I["parity"]), (consts["sumq"][:, :, :], I["sumq"])])
                e.dma_start(cT_dram[E0:E0 + SHARED // I0], I["ones_rows"]).then_inc(stored, 16)
                hold(e, turned, 3)
                e.dma_start(mask_dram, mb[:, :]).then_inc(stored, 16)
                hold(e, stored, 32)

            @block.vector
            def _(e):
                e.memset(consts["minus_half"][:, :], -0.5)
                e.wait_ge(loaded, 64)
                e.tensor_copy(consts["identb"][:, :], consts["ident"][:, :]).then_inc(turned, 1)
                e.tensor_copy(mf[:, :], m8[:, :].bitcast(U8)).then_inc(turned, 1)
                e.wait_ge(turned, 2)
                e.tensor_scalar(mb[:, :], mf[:, :], -1.0, PICKED, ALU.add, ALU.mult).then_inc(turned, 1)


def decoder(nc, I, out):
    with ExitStack() as ctx:
        bank = [ctx.enter_context(nc.psum_tensor(f"bank{i}", [128, 512], F32)) for i in range(8)]
        sb = lambda n, shape, dt=F32: ctx.enter_context(nc.sbuf_tensor(n, shape, dt))
        consts = {"ident": sb("ident_sb", [128, 128]), "identb": sb("identb_sb", [128, 128], BF16),
                  "parity": sb("parity_sb", [128, 2]), "sumq": sb("sumq_sb", [128, 2, 48]), "minus_half": sb("minus_half_sb", [128, 4])}
        dram = lambda n, shape, dt=F32: nc.dram_tensor(n, shape, dt, kind="Internal").ap()
        x = [dram(f"x_after{i}", (TOKENS, D)) for i in range(5)]
        qx = [dram(f"query_operands{i}", (SEQS, PAIRS, SROWS, 2 * SEQ), BF16) for i in range(2)]
        at = [dram(f"attended{i}", (D, TOKENS)) for i in range(2)]
        denominators = dram("attention_denominators", (D, TOKENS))
        xT = [dram(f"xT{i}", (D, TOKENS)) for i in range(2)]
        yT = [dram(f"yT{i}", (D, TOKENS)) for i in range(2)]
        cT = [dram("expert_weights0", (E0 + SHARED // I0, TOKENS)), dram("expert_weights1", (E1, TOKENS))]
        mask, qkT, v, oT = dram("mask_rows", (SEQS, KEYS), BF16), dram("qkT", (D, 2, TOKENS)), dram("v1", (TOKENS, D)), dram("oT1", (D, TOKENS))
        set_up(nc, consts, mask, cT[0], I)
        self_attention_0(nc, bank, I, x[0], qx[0], consts)
        cross_attention(nc, bank, "xa0", "L0_xattn_", qx[0], None, at[0], denominators, consts, I)
        project_and_route(nc, bank, "rt0", 0, at[0], denominators, x[0], x[1], xT[0], cT[0], consts, I)
        experts(nc, bank, "ex0", 0, xT[0], cT[0], yT[0], consts, I)
        norm_and_project_1(nc, bank, yT[0], x[1], x[2], qkT, v, consts, I)
        causal_attention(nc, bank, qkT, v, oT, consts, I)
        project_1(nc, bank, oT, x[2], x[3], qx[1], consts, I)
        cross_attention(nc, bank, "xa1", "L1_xattn_", qx[1], mask, at[1], denominators, consts, I)
        project_and_route(nc, bank, "rt1", 1, at[1], denominators, x[3], x[4], xT[1], cT[1], consts, I)
        experts(nc, bank, "ex1", 1, xT[1], cT[1], yT[1], consts, I)
        final_norm(nc, bank, yT[1], x[4], out, consts)


def shape_constants():
    f = np.float32
    pos = (np.arange(TILE) % SEQ).astype(f)
    inv = (f(1.0) / np.power(f(10000.0), np.arange(0, HD, 2, dtype=f) / f(HD))).astype(f)
    ang = pos[:, None] * inv[None, :]
    rows = np.arange(D)
    sumq = np.zeros((D, 2, 48), f)
    for p in range(D):
        r = p % 32
        if r < PR:
            sumq[p, r // HD, r] = 1
        else:
            sumq[p, (r - PR) // HD, 32 + r - PR] = 1
    causal = np.zeros((64 + SEQ, SEQ), f)
    causal[:SEQ] = causal[64:] = np.where(np.tril(np.ones((SEQ, SEQ), bool)), 0, -PICKED)
    bf = mybir.dt.np(BF16)
    return {
        "rope_cos": np.cos(ang).astype(f), "rope_sin": np.sin(ang).astype(f), "ident": np.eye(D, dtype=f),
        "parity": (rows[:, None] // HD % 2 == np.arange(2)[None]).astype(f), "sumq": sumq,
        "headmask": (rows[:, None] // HD == np.arange(HEADS)[None]).astype(f),
        "ones8": (rows[:, None] // HD == rows[None] // HD).astype(f),
        "causal": causal,
        "query_rows": np.stack([np.zeros((PAIRS, 2 * SEQ)), np.ones((PAIRS, 2 * SEQ))]).astype(bf),
        "key_rows": np.stack([np.ones((PAIRS, KEYS)), np.zeros((PAIRS, KEYS))]).astype(bf),
        "ones_rows": np.ones((SHARED // I0, TOKENS), f), "b2_or_zero0": np.zeros((E1, D), f),
    }


def kernel(**inputs):
    import concourse.bacc as bacc
    from concourse.bass_utils import run_bass_kernel_spmd

    a = {k: np.asarray(v) for k, v in inputs.items()}
    c = np.ascontiguousarray
    I = shape_constants()
    x = a["x"].reshape(TOKENS, D)
    I.update(x=c(x), xT=c(x.T), ctxT=c(a["ctx_1024"].transpose(0, 2, 1)), mask=c(a["mask_BxS2_bk0"]).view(np.int32))
    for n in ("L0_attn_Wq", "L0_attn_bq", "L0_attn_Wdown", "L0_attn_bdown", "L0_attn_Wup", "L0_attn_bup", "L0_attn_Wout",
              "L0_attn_bout", "L0_xattn_bq", "L0_xattn_bk", "L0_xattn_bv", "L0_xattn_bo", "L0_ffn_correction_bias",
              "L1_xattn_Wq", "L1_xattn_bq", "L1_xattn_bk", "L1_xattn_bv", "L1_xattn_bo"):
        I[n] = c(a[n])
    for n in ("L0_xattn_Wq", "L0_xattn_Wk", "L0_xattn_Wv", "L0_xattn_Wo", "L1_attn_Wq", "L1_attn_Wk", "L1_attn_Wv", "L1_attn_Wo"):
        I[n + "T"] = c(a[n].T)
    for n in ("Wk", "Wv", "Wo"):
        I[f"L1_xattn_{n}T"] = c(a[f"L1_xattn_{n}"])
    I["temperature_rows"] = np.repeat(a["L0_xattn_temperature"].reshape(HEADS), HD)
    I["q_scale_rows"], I["k_scale_rows"] = np.repeat(a["L1_attn_q_scale"], HD), np.repeat(a["L1_attn_k_scale"], HD)
    I["router0"], I["router1"] = c(a["L0_ffn_router_w"].T), c(a["L1_ffn_W_gate"])
    up = np.concatenate([a["L0_ffn_up_w"].transpose(1, 0, 2).reshape(D, E0 * I0), a["L0_ffn_shared_up_w"]], axis=1)
    I["up0"] = c(up.reshape(D, NCH0, 128).transpose(1, 0, 2))
    I["down0"] = np.concatenate([a["L0_ffn_down_w"].reshape(E0 * I0, D), a["L0_ffn_shared_down_w"]]).reshape(NCH0, 128, D)
    n = I1 // 128
    I["up1"] = c(a["L1_ffn_W1"].reshape(E1, D, n, 128).transpose(0, 2, 1, 3).reshape(NCH1, D, 128))
    I["down1"] = c(a["L1_ffn_W2"].reshape(NCH1, 128, D))
    I["b1"] = c(a["L1_ffn_b1"].reshape(NCH1, 128, 1))
    I["b2_or_zero1"] = c(a["L1_ffn_b2"])

    nc = bacc.Bacc("TRN2", target_bir_lowering=False, num_devices=1)
    arrays = {f"in_{k}": v for k, v in I.items()}
    aps = {k: nc.dram_tensor(f"in_{k}", v.shape, mybir.dt.from_np(v.dtype), kind="ExternalInput").ap() for k, v in I.items()}
    out = nc.dram_tensor("out_0", (TOKENS, D), F32, kind="ExternalOutput").ap()
    decoder(nc, aps, out)
    r = run_bass_kernel_spmd(nc, [arrays], core_ids=[0])
    return r.results[0]["out_0"].reshape(SEQS, SEQ, D)
```
